# Optimizing a Trainium2 kernel written in Bass

```python
import numpy as np
import jax
import jax.numpy as jnp

def _softmax(x, axis=-1):
    return jax.nn.softmax(x, axis=axis)

def _gelu(x):
    return jax.nn.gelu(x, approximate=True)

def _silu(x):
    return jax.nn.silu(x)

def _sigmoid(x):
    return jax.nn.sigmoid(x)

def _layernorm(x, axis=-1, eps=1e-05):
    m = jnp.mean(x, axis=axis, keepdims=True)
    v = jnp.var(x, axis=axis, keepdims=True)
    return (x - m) / jnp.sqrt(v + eps)

def _scatter_add(tgt, idx, src, axis=0):
    return tgt.at[idx].add(src)

def _segment_sum(src, seg, n):
    return jax.ops.segment_sum(src, seg, n)
kernel_name = 'mk_gnn_preln_d4_gnn_r8_8c3d23'

def setup_inputs(seed: int=0):
    np.random.seed(seed)
    _w = jnp.asarray

    def _rec_inputs():
        import jax
        import jax.numpy as jnp
        _gk = jax.random.key(seed)
        x = -0.000202 + 1 * jax.random.normal(jax.random.fold_in(_gk, 1), (6250, 128), jnp.float32)
        _s = jax.random.randint(jax.random.fold_in(_gk, 2), (50000,), 0, 6250, jnp.int32)
        _d = jax.random.randint(jax.random.fold_in(_gk, 3), (50000,), 0, 6250, jnp.int32)
        _loop = jnp.arange(6250, dtype=jnp.int32)
        src = jnp.concatenate([_s, _d, _loop])
        dst = jnp.concatenate([_d, _s, _loop])
        _o = jnp.argsort(dst, stable=True)
        src = src[_o]
        dst = dst[_o]
        edge_attr_64 = -5.16925e-05 + 1.00005 * jax.random.normal(jax.random.fold_in(_gk, 11), (106250, 64), jnp.float32)
        return (x, src, dst, edge_attr_64)
    x, src, dst, edge_attr_64 = _rec_inputs()

    def _L0_gnn_setup():
        import jax, jax.numpy as jnp
        import numpy as np
        N_NODES = 6250
        N_EDGES = 75000
        D_FEAT = 128
        D_OUT = 128
        key = jax.random.key(seed)
        k1, k2, k3, k4 = jax.random.split(key, 4)
        x = jax.random.normal(k1, (N_NODES, D_FEAT), dtype=jnp.float32)
        edge_index = jax.random.randint(k2, (2, N_EDGES), 0, N_NODES, dtype=jnp.int64)
        lim = 1.0 / np.sqrt(2 * D_FEAT)
        W = jax.random.uniform(k3, (D_OUT, 2 * D_FEAT), minval=-lim, maxval=lim, dtype=jnp.float32)
        b = jax.random.uniform(k4, (D_OUT,), minval=-lim, maxval=lim, dtype=jnp.float32)
        return {'x': x, 'edge_index': edge_index, 'W': W, 'b': b}
    _L0_gnn_all = _L0_gnn_setup()
    _L0_gnn_in = {k: v for k, v in _L0_gnn_all.items() if k in ('W', 'b')}
    del _L0_gnn_all

    def _L1_gnn_setup():
        import jax, jax.numpy as jnp
        import numpy as np
        N = 12500
        E = 200000
        IN_DIM = 128
        HID = 256

        def _sage_conv(x, src, dst, Wl, bl, Wr, num_nodes):
            agg = jax.ops.segment_sum(x[src], dst, num_segments=num_nodes)
            cnt = jax.ops.segment_sum(jnp.ones((src.shape[0],), x.dtype), dst, num_segments=num_nodes)
            mean = agg / jnp.maximum(cnt, 1.0)[:, None]
            return mean @ Wl.T + bl + x @ Wr.T
        key = jax.random.key(seed)
        ks = jax.random.split(key, 12)
        x = jax.random.normal(ks[0], (N, IN_DIM), dtype=jnp.float32)
        edge_index = jax.random.randint(ks[1], (2, E), 0, N, dtype=jnp.int32)

        def lin(k, out_d, in_d):
            s = 1.0 / np.sqrt(in_d)
            return jax.random.uniform(k, (out_d, in_d), jnp.float32, -s, s)
        return {'x': x, 'edge_index': edge_index, 'W1l': lin(ks[2], HID, IN_DIM), 'b1': jnp.zeros((HID,), jnp.float32), 'W1r': lin(ks[3], HID, IN_DIM), 'W2l': lin(ks[4], HID, HID), 'b2': jnp.zeros((HID,), jnp.float32), 'W2r': lin(ks[5], HID, HID), 'W3l': lin(ks[6], HID // 2, HID), 'b3': jnp.zeros((HID // 2,), jnp.float32), 'W3r': lin(ks[7], HID // 2, HID)}
    _L1_gnn_all = _L1_gnn_setup()
    _L1_gnn_in = {k: v for k, v in _L1_gnn_all.items() if k in ('W1l', 'b1', 'W1r', 'W2l', 'b2', 'W2r', 'W3l', 'b3', 'W3r')}
    del _L1_gnn_all

    def _L2_gnn_setup():
        import jax, jax.numpy as jnp
        import numpy as np
        N, E, H, ED, GD = (12500, 200000, 128, 64, 64)
        LN_EPS = 1e-05

        def _mlp(x, w1, b1, w2, b2):
            return jax.nn.relu(x @ w1 + b1) @ w2 + b2
        key = jax.random.key(seed)
        ks = jax.random.split(key, 16)
        s = lambda d: 1.0 / np.sqrt(d)
        return {'node_state': jax.random.normal(ks[0], (N, H), jnp.float32), 'edge_index': jax.random.randint(ks[1], (2, E), 0, N, jnp.int64), 'edge_state': jax.random.normal(ks[2], (E, ED), jnp.float32), 'global_state': jax.random.normal(ks[3], (GD,), jnp.float32), 'msg_w1': jax.random.normal(ks[4], (H + ED + GD, H), jnp.float32) * s(H + ED + GD), 'msg_b1': jnp.zeros((H,), jnp.float32), 'msg_w2': jax.random.normal(ks[5], (H, H), jnp.float32) * s(H), 'msg_b2': jnp.zeros((H,), jnp.float32), 'upd_w1': jax.random.normal(ks[6], (2 * H + GD, H), jnp.float32) * s(2 * H + GD), 'upd_b1': jnp.zeros((H,), jnp.float32), 'upd_w2': jax.random.normal(ks[7], (H, H), jnp.float32) * s(H), 'upd_b2': jnp.zeros((H,), jnp.float32), 'ln_gamma': jnp.ones((H,), jnp.float32), 'ln_beta': jnp.zeros((H,), jnp.float32)}
    _L2_gnn_all = _L2_gnn_setup()
    _L2_gnn_in = {k: v for k, v in _L2_gnn_all.items() if k in ('global_state', 'msg_w1', 'msg_b1', 'msg_w2', 'msg_b2', 'upd_w1', 'upd_b1', 'upd_w2', 'upd_b2', 'ln_gamma', 'ln_beta')}
    del _L2_gnn_all

    def _L3_gnn_setup():
        import jax, jax.numpy as jnp
        import numpy as np
        N_NODES = 12500
        N_EDGES = 200000
        IN_F = 128
        OUT_F = 32
        HEADS = 4
        NEG_SLOPE = 0.2
        EPS = 1e-08
        key = jax.random.key(seed)
        k1, k2, k3, k4 = jax.random.split(key, 4)
        x = jax.random.normal(k1, (N_NODES, IN_F), dtype=jnp.float32)
        limW = float(np.sqrt(6.0 / (IN_F + OUT_F * HEADS)))
        W = jax.random.uniform(k2, (OUT_F * HEADS, IN_F), dtype=jnp.float32, minval=-limW, maxval=limW)
        lima = float(np.sqrt(6.0 / (HEADS + 2 * OUT_F)))
        a = jax.random.uniform(k3, (HEADS, 2 * OUT_F), dtype=jnp.float32, minval=-lima, maxval=lima)
        edge_index = jax.random.randint(k4, (2, N_EDGES), 0, N_NODES, dtype=jnp.int64)
        return {'x': x, 'W': W, 'a': a, 'edge_index': edge_index}
    _L3_gnn_all = _L3_gnn_setup()
    _L3_gnn_in = {k: v for k, v in _L3_gnn_all.items() if k in ('W', 'a')}
    del _L3_gnn_all
    return {'x': x, 'src': src, 'dst': dst, 'edge_attr_64': edge_attr_64, 'L0_gnn_W': _L0_gnn_in['W'], 'L0_gnn_b': _L0_gnn_in['b'], 'L1_gnn_W1l': _L1_gnn_in['W1l'], 'L1_gnn_b1': _L1_gnn_in['b1'], 'L1_gnn_W1r': _L1_gnn_in['W1r'], 'L1_gnn_W2l': _L1_gnn_in['W2l'], 'L1_gnn_b2': _L1_gnn_in['b2'], 'L1_gnn_W2r': _L1_gnn_in['W2r'], 'L1_gnn_W3l': _L1_gnn_in['W3l'], 'L1_gnn_b3': _L1_gnn_in['b3'], 'L1_gnn_W3r': _L1_gnn_in['W3r'], 'L2_gnn_global_state': _L2_gnn_in['global_state'], 'L2_gnn_msg_w1': _L2_gnn_in['msg_w1'], 'L2_gnn_msg_b1': _L2_gnn_in['msg_b1'], 'L2_gnn_msg_w2': _L2_gnn_in['msg_w2'], 'L2_gnn_msg_b2': _L2_gnn_in['msg_b2'], 'L2_gnn_upd_w1': _L2_gnn_in['upd_w1'], 'L2_gnn_upd_b1': _L2_gnn_in['upd_b1'], 'L2_gnn_upd_w2': _L2_gnn_in['upd_w2'], 'L2_gnn_upd_b2': _L2_gnn_in['upd_b2'], 'L2_gnn_ln_gamma': _L2_gnn_in['ln_gamma'], 'L2_gnn_ln_beta': _L2_gnn_in['ln_beta'], 'L3_gnn_W': _L3_gnn_in['W'], 'L3_gnn_a': _L3_gnn_in['a']}

def reference(x, src, dst, edge_attr_64, L0_gnn_W, L0_gnn_b, L1_gnn_W1l, L1_gnn_b1, L1_gnn_W1r, L1_gnn_W2l, L1_gnn_b2, L1_gnn_W2r, L1_gnn_W3l, L1_gnn_b3, L1_gnn_W3r, L2_gnn_global_state, L2_gnn_msg_w1, L2_gnn_msg_b1, L2_gnn_msg_w2, L2_gnn_msg_b2, L2_gnn_upd_w1, L2_gnn_upd_b1, L2_gnn_upd_w2, L2_gnn_upd_b2, L2_gnn_ln_gamma, L2_gnn_ln_beta, L3_gnn_W, L3_gnn_a):
    import jax
    import jax.numpy as jnp

    def _L0_gnn_ref(x, edge_index, W, b):
        import jax, jax.numpy as jnp
        import numpy as np
        N_NODES = 6250
        N_EDGES = 75000
        D_FEAT = 128
        D_OUT = 128
        row, col = (edge_index[0], edge_index[1])
        agg = jax.ops.segment_sum(x[col], row, num_segments=x.shape[0])
        h = jnp.concatenate([x, agg], axis=1)
        out = h @ W.T + b
        return jax.nn.relu(out)

    def _L1_gnn_ref(x, edge_index, W1l, b1, W1r, W2l, b2, W2r, W3l, b3, W3r):
        import jax, jax.numpy as jnp
        import numpy as np
        N = 12500
        E = 200000
        IN_DIM = 128
        HID = 256

        def _sage_conv(x, src, dst, Wl, bl, Wr, num_nodes):
            agg = jax.ops.segment_sum(x[src], dst, num_segments=num_nodes)
            cnt = jax.ops.segment_sum(jnp.ones((src.shape[0],), x.dtype), dst, num_segments=num_nodes)
            mean = agg / jnp.maximum(cnt, 1.0)[:, None]
            return mean @ Wl.T + bl + x @ Wr.T
        src, dst = (edge_index[0], edge_index[1])
        n = x.shape[0]
        h = jax.nn.relu(_sage_conv(x, src, dst, W1l, b1, W1r, n))
        h = jax.nn.relu(_sage_conv(h, src, dst, W2l, b2, W2r, n))
        h = jax.nn.relu(_sage_conv(h, src, dst, W3l, b3, W3r, n))
        return h

    def _L2_gnn_ref(node_state, edge_index, edge_state, global_state, msg_w1, msg_b1, msg_w2, msg_b2, upd_w1, upd_b1, upd_w2, upd_b2, ln_gamma, ln_beta):
        import jax, jax.numpy as jnp
        import numpy as np
        N, E, H, ED, GD = (12500, 200000, 128, 64, 64)
        LN_EPS = 1e-05

        def _mlp(x, w1, b1, w2, b2):
            return jax.nn.relu(x @ w1 + b1) @ w2 + b2
        src, dst = (edge_index[0], edge_index[1])
        num_nodes = node_state.shape[0]
        num_edges = src.shape[0]
        global_edges = jnp.broadcast_to(global_state, (num_edges, global_state.shape[0]))
        message_input = jnp.concatenate([node_state[src], edge_state, global_edges], axis=-1)
        messages = _mlp(message_input, msg_w1, msg_b1, msg_w2, msg_b2)
        aggregated = jax.ops.segment_sum(messages, dst, num_segments=num_nodes)
        degree = jax.ops.segment_sum(jnp.ones((num_edges,), node_state.dtype), dst, num_segments=num_nodes)
        aggregated = aggregated / jnp.maximum(degree, 1.0)[:, None]
        global_nodes = jnp.broadcast_to(global_state, (num_nodes, global_state.shape[0]))
        update_input = jnp.concatenate([node_state, aggregated, global_nodes], axis=-1)
        delta = _mlp(update_input, upd_w1, upd_b1, upd_w2, upd_b2)
        x = node_state + delta
        mu = jnp.mean(x, axis=-1, keepdims=True)
        var = jnp.mean(jnp.square(x - mu), axis=-1, keepdims=True)
        return (x - mu) * jax.lax.rsqrt(var + LN_EPS) * ln_gamma + ln_beta

    def _L3_gnn_ref(x, W, a, edge_index):
        import jax, jax.numpy as jnp
        import numpy as np
        N_NODES = 12500
        N_EDGES = 200000
        IN_F = 128
        OUT_F = 32
        HEADS = 4
        NEG_SLOPE = 0.2
        EPS = 1e-08
        N = x.shape[0]
        H = HEADS
        F = OUT_F
        h = (x @ W.T).reshape(N, H, F)
        src, dst = (edge_index[0], edge_index[1])
        h_src = h[src]
        h_dst = h[dst]
        a_src, a_dst = (a[:, :F], a[:, F:])
        att = jnp.einsum('ehf,hf->eh', h_src, a_src) + jnp.einsum('ehf,hf->eh', h_dst, a_dst)
        att = jnp.where(att >= 0, att, NEG_SLOPE * att)
        att = jnp.exp(att - att.max())
        att_sum = jax.ops.segment_sum(att, dst, num_segments=N)
        att = att / (att_sum[dst] + EPS)
        out = jax.ops.segment_sum(att[..., None] * h_src, dst, num_segments=N)
        return out.reshape(N, H * F)
    edge_index = jnp.stack([src, dst])
    h = jnp.maximum(_layernorm(x, axis=-1), 0.0)
    x = x + _L0_gnn_ref(h, edge_index, L0_gnn_W, L0_gnn_b)
    h = jnp.maximum(_layernorm(x, axis=-1), 0.0)
    x = x + _L1_gnn_ref(h, edge_index, L1_gnn_W1l, L1_gnn_b1, L1_gnn_W1r, L1_gnn_W2l, L1_gnn_b2, L1_gnn_W2r, L1_gnn_W3l, L1_gnn_b3, L1_gnn_W3r)
    h = jnp.maximum(_layernorm(x, axis=-1), 0.0)
    x = x + _L2_gnn_ref(h, edge_index, edge_attr_64, L2_gnn_global_state, L2_gnn_msg_w1, L2_gnn_msg_b1, L2_gnn_msg_w2, L2_gnn_msg_b2, L2_gnn_upd_w1, L2_gnn_upd_b1, L2_gnn_upd_w2, L2_gnn_upd_b2, L2_gnn_ln_gamma, L2_gnn_ln_beta)
    h = jnp.maximum(_layernorm(x, axis=-1), 0.0)
    x = x + _L3_gnn_ref(h, L3_gnn_W, L3_gnn_a, edge_index)
    return x

_drawn_inputs = setup_inputs


def setup_inputs(seed=0):
    import zlib

    import numpy as np

    out = dict(_drawn_inputs(seed))
    spreads = {'L1_gnn_b1': (0.0, 0.8),
     'L1_gnn_b2': (0.0, 0.484),
     'L1_gnn_b3': (0.0, 0.333),
     'L2_gnn_msg_b1': (0.0, 0.757),
     'L2_gnn_msg_b2': (0.0, 0.581),
     'L2_gnn_upd_b1': (0.0, 0.363),
     'L2_gnn_upd_b2': (0.0, 0.295),
     'L2_gnn_ln_gamma': (1.0, 0.2),
     'L2_gnn_ln_beta': (0.0, 0.1)}
    factors = {'edge_attr_64': 4.495, 'L0_gnn_b': 5.148, 'L3_gnn_a': 3.812}
    for name, (base, spread) in spreads.items():
        noise = np.random.default_rng([zlib.crc32(name.encode()), seed]).standard_normal(out[name].shape)
        drawn = base * np.exp(spread * noise) if base else spread * noise
        out[name] = jnp.asarray(drawn.astype(out[name].dtype))
    for name, factor in factors.items():
        out[name] = (out[name] * factor).astype(out[name].dtype)
    return out
```

```python
import concourse.bass as bass
from concourse import mybir
from contextlib import ExitStack


class Steps:

    def __init__(self, eng, sem):
        self.eng, self.sem, self.base, self.k = eng, sem, 0, 0

    def at(self, base):
        self.base, self.k = base, 0

    def __call__(self, ins):
        self.k += 1
        ins.then_inc(self.sem, 1)
        self.eng.wait_ge(self.sem, self.base + self.k)


def iterations(eng, n):
    yield 0
    if n > 1:
        with eng.Fori(1, n) as i:
            yield i


def after(eng, sem, value):
    if not isinstance(value, int) or value > 0:
        eng.wait_ge(sem, value)


def bass_gnn_preln_d4(nc, x, src, dst, edge_attr_64, L0_gnn_W, L0_gnn_b, L1_gnn_W1l, L1_gnn_b1, L1_gnn_W1r,
                      L1_gnn_W2l, L1_gnn_b2, L1_gnn_W2r, L1_gnn_W3l, L1_gnn_b3, L1_gnn_W3r, L2_gnn_global_state,
                      L2_gnn_msg_w1, L2_gnn_msg_b1, L2_gnn_msg_w2, L2_gnn_msg_b2, L2_gnn_upd_w1, L2_gnn_upd_b1,
                      L2_gnn_upd_w2, L2_gnn_upd_b2, L2_gnn_ln_gamma, L2_gnn_ln_beta, L3_gnn_W, L3_gnn_a, out):
    f32, i32 = mybir.dt.float32, mybir.dt.int32
    ALU, ACT, AX = mybir.AluOpType, mybir.ActivationFunctionType, mybir.AxisListType

    P = 128
    N, F = x.shape
    E, ED = edge_attr_64.shape
    GD = L2_gnn_global_state.shape[0]
    HEADS, HF = L3_gnn_a.shape[0], F // L3_gnn_a.shape[0]
    U = 7
    NT = U * -(-N // (P * U))
    NI = NT // U
    NFULL, NTAIL = N // P, N % P
    G = 8
    PAIRS = -(-E // (2 * G * P))
    NG, ET = 2 * PAIRS, 2 * PAIRS * G
    EFULL, ETAIL = E // P, E % P
    NW = NT * P + P
    QB = -(-ET // P)
    TW = F + HEADS
    LN_EPS, ATT_EPS, SLOPE, FAR = 1e-5, 1e-8, 0.2, -1e30

    T_C1, T_C3, T_MSG = [nc.dram_tensor(f"table_{n}", [NT * P, F], f32, kind="Internal").ap() for n in ("c1", "c3", "msg")]
    T_L0 = nc.dram_tensor("table_l0", [NW, F], f32, kind="Internal").ap()
    T_C2 = nc.dram_tensor("table_c2", [NT * P, 2 * F], f32, kind="Internal").ap()
    T_ATT = nc.dram_tensor("table_att", [NT * P, TW], f32, kind="Internal").ap()
    NACC = 4
    T_PART = [nc.dram_tensor(f"sum_by_source_{q}", [NT * P + P, F], f32, kind="Internal").ap() for q in range(NACC)]
    T_DST = nc.dram_tensor("table_dst_logits", [NW, HEADS], f32, kind="Internal").ap()

    with ExitStack() as ctx:
        def sb(name, shape, dt=f32):
            return ctx.enter_context(nc.sbuf_tensor(name, shape, dt))

        X = sb("X", [P, NT, F])
        acc = sb("acc", [P, 2, NW])
        rcnt = sb("rcnt", [P, NW])
        Hflat = sb("Hbuf", [P, 2 * NT * P])
        Hbuf = Hflat[:, :].rearrange("p (k n) -> p k n", k=2)
        scol = Hflat[:, 0:NW]
        work = sb("work", [P, 8192])
        srcI = sb("srcI", [P, ET], i32)
        dstF = sb("dstF", [P, ET])
        dl = sb("dl", [P, ET])
        base0 = sb("base0", [P, NG])
        baseF = sb("baseF", [P, NG])
        baseI = sb("baseI", [1, NG], i32)
        step = sb("step", [P, 1])
        sweeps = sb("sweeps", [1, 4], i32)
        idx = sb("idx", [P, 2, G], i32)
        wt = sb("wt", [P, 25, F])
        wext = sb("wext", [P, F + 2 * HEADS])
        cols = sb("cols", [P, 8])
        rows = sb("rows", [1, 3, F])
        ones = sb("ones", [P, P])
        ident = sb("ident", [P, P])
        small = sb("small", [P, 8])
        dwin = sb("dwin", [P, 2, HEADS])
        PS = [ctx.enter_context(nc.psum_tensor(f"ps{i}", [P, 2, 512], f32)) for i in range(4)]

        W_NAMES = (["l0x", "l0a"] + [f"c1{s}0{o}" for s in "lr" for o in range(2)]
                   + [f"c2{s}{i}{o}" for s in "lr" for i in range(2) for o in range(2)]
                   + [f"c3{s}{i}0" for s in "lr" for i in range(2)]
                   + ["m1n", "m1a", "m1b", "w2u", "u1h", "u2", "iota"])
        assert len(W_NAMES) <= 25

        def W(name):
            return wt[:, W_NAMES.index(name), :]

        iota = W("iota")
        B0, B1, B2, CU, UB2, EPSC = 0, 1, 3, 5, 6, 7

        g256 = work[:, 0:2 * G * 256].rearrange("p (s j f) -> p s j f", s=2, j=G)
        g128 = work[:, 0:2 * G * 128].rearrange("p (s j f) -> p s j f", s=2, j=G)
        g132 = work[:, 0:2 * G * TW].rearrange("p (s j f) -> p s j f", s=2, j=G)
        bufA = work[:, 2112:3136].rearrange("p (j f) -> p j f", j=G)
        winF = work[:, 3136:3264]
        lg = work[:, 3264:3264 + 3 * G * HEADS].rearrange("p (k c) -> p k c", k=3)
        onehot = work[:, 4096:5120].rearrange("p (j f) -> p j f", j=G)
        bufB = work[:, 5120:6144].rearrange("p (j f) -> p j f", j=G)
        bufC = work[:, 6144:7168].rearrange("p (j f) -> p j f", j=G)
        ea = work[:, 7168:8192].rearrange("p (s c) -> p s c", s=2)
        st = work[:, 0:2 * U * F].rearrange("p (a o f) -> p a o f", a=U, o=2)
        hn = work[:, 1792:1792 + U * F].rearrange("p (a f) -> p a f", a=U)
        hs = work[:, 2688:2688 + U * F].rearrange("p (a f) -> p a f", a=U)
        nm = work[:, 3584:3584 + U * 256].rearrange("p (a f) -> p a f", a=U)
        tmp = work[:, 5376:5376 + U * F].rearrange("p (a f) -> p a f", a=U)
        gamma = work[:, 7168:7168 + F]
        beta = work[:, 7168 + F:7168 + 2 * F]
        stats = work[:, 7424:7424 + NT * 6].rearrange("p (t c) -> p t c", c=6)
        ln = work[:, 7424 + NT * 6:7424 + NT * 11].rearrange("p (k t) -> p k t", k=5)

        def phase():
            s, mine = ExitStack(), []
            uid = phase.n
            phase.n += 1

            def sem(name):
                mine.append(nc.alloc_semaphore(f"{name}_{uid}"))
                return mine[-1]

            s.callback(nc.all_engine_barrier)
            s.callback(lambda: nc.clear_and_free_semaphores(mine))
            return s, sem
        phase.n = 0

        def prepare():
            s, sem = phase()
            with s:
                loaded, indices, filled, pads = sem("loaded"), sem("indices"), sem("filled"), sem("pads")
                steps, asfloat, turned, kept, made = (sem("vector_steps"), sem("asfloat"), sem("turned"), sem("kept"),
                                                      sem("made"))
                zeroed = sem("dst_table_zeroed")
                rawI = work[:, 0:2 * QB * P].bitcast(i32).rearrange("p (k q c) -> p k q c", k=2, q=QB)
                rawF = work[:, 1792:1792 + 2 * QB * P].rearrange("p (k q c) -> p k q c", k=2, q=QB)
                nat = work[:, 3584:3584 + 20 * F].rearrange("p (b f) -> p b f", f=F)
                w1g = work[:, 6144:6144 + F]
                u1c = work[:, 6272:6272 + F]
                u1b = work[:, 6400:6400 + F]
                w2t = work[:, 6528:6528 + F]
                ablk = work[:, 6656:6656 + 2 * HEADS]
                gcol = work[:, 6672:6673]
                mb2 = work[:, 6673:6674]
                zero4 = work[:, 6676:6676 + HEADS]
                ub1 = work[:, 6680:6681]
                natural = [(L0_gnn_W, 0, 0), (L0_gnn_W, 0, 1)]
                natural += [(w, o, 0) for w in (L1_gnn_W1l, L1_gnn_W1r) for o in range(2)]
                natural += [(w, o, i) for w in (L1_gnn_W2l, L1_gnn_W2r) for i in range(2) for o in range(2)]
                natural += [(w, 0, i) for w in (L1_gnn_W3l, L1_gnn_W3r) for i in range(2)]
                natural += [(L3_gnn_W, 0, 0), (L2_gnn_msg_w2, 0, 0)]
                NB, IL3, IMW2 = len(natural), len(natural) - 2, len(natural) - 1
                with nc.Block() as block:
                    @block.sync
                    def _(sp):
                        sp.wait_ge(filled, 1)
                        n = 0
                        for k, v in ((0, src), (1, dst)):
                            for q in range(QB):
                                r = min(P, EFULL - q * P)
                                if r > 0:
                                    sp.dma_start(rawI[0:r, k, q, :], v[q * P * P:(q * P + r) * P].rearrange(
                                        "(t p) -> t p", p=P)).then_inc(indices, 16)
                                    n += 1
                            if ETAIL:
                                q, r = EFULL // P, EFULL % P
                                sp.dma_start(rawI[r:r + 1, k, q, 0:ETAIL],
                                             v[EFULL * P:E].rearrange("(o c) -> o c", o=1)).then_inc(indices, 16)
                                n += 1
                        prepare.n_idx = n
                        m = 0
                        def load(o, i):
                            sp.dma_start(o, i).then_inc(loaded, 16)
                        for q in range(NACC):
                            sp.dma_start(T_PART[q].rearrange("(t p) f -> p t f", p=P),
                                         acc[:, 0, :].rearrange("p (t f) -> p t f", f=P)).then_inc(zeroed, 16)
                        for b, (w, r, c) in enumerate(natural):
                            load(nat[:, b, :], w[r * P:(r + 1) * P, c * P:(c + 1) * P])
                        load(X[:, 0:NFULL, :], x[0:NFULL * P, :].rearrange("(t p) f -> p t f", p=P))
                        if NTAIL:
                            load(X[0:NTAIL, NFULL, :], x[NFULL * P:N, :])
                        load(W("m1n"), L2_gnn_msg_w1[0:F, :])
                        load(W("m1a")[0:ED, :], L2_gnn_msg_w1[F:F + ED, :])
                        load(W("m1b")[ED:2 * ED, :], L2_gnn_msg_w1[F:F + ED, :])
                        load(w1g[0:GD, :], L2_gnn_msg_w1[F + ED:F + ED + GD, :])
                        load(W("u1h"), L2_gnn_upd_w1[0:F, :])
                        load(u1b, L2_gnn_upd_w1[F:2 * F, :])
                        load(u1c[0:GD, :], L2_gnn_upd_w1[2 * F:2 * F + GD, :])
                        load(W("u2"), L2_gnn_upd_w2)
                        for h in range(HEADS):
                            for k in range(2):
                                load(ablk[HF * h:HF * (h + 1), HEADS * k + h:HEADS * k + h + 1],
                                     L3_gnn_a[h, HF * k:HF * (k + 1)].rearrange("(f o) -> f o", o=1))
                        load(gcol[0:GD, :], L2_gnn_global_state.rearrange("(f o) -> f o", o=1))
                        load(mb2, L2_gnn_msg_b2.rearrange("(f o) -> f o", o=1))
                        load(cols[:, B0:B0 + 1], L0_gnn_b.rearrange("(f o) -> f o", o=1))
                        for o in range(2):
                            load(cols[:, B1 + o:B1 + o + 1], L1_gnn_b1[o * P:(o + 1) * P].rearrange("(f o) -> f o", o=1))
                            load(cols[:, B2 + o:B2 + o + 1], L1_gnn_b2[o * P:(o + 1) * P].rearrange("(f o) -> f o", o=1))
                        load(ub1, L2_gnn_upd_b1.rearrange("(f o) -> f o", o=1))
                        load(cols[:, UB2:UB2 + 1], L2_gnn_upd_b2.rearrange("(f o) -> f o", o=1))
                        load(rows[0:1, 0, :], L1_gnn_b3.rearrange("(o f) -> o f", o=1))
                        load(rows[0:1, 1, :], L2_gnn_msg_b1.rearrange("(o f) -> o f", o=1))
                        sp.dma_start(T_L0[NT * P:NT * P + P, :], acc[:, 0, 0:F]).then_inc(zeroed, 16)
                        for t in range(NT + 1):
                            if t >= NFULL:
                                sp.dma_start(T_DST[t * P:(t + 1) * P, :], zero4).then_inc(zeroed, 16)
                        sp.wait_ge(zeroed, 16 * (NT + 1 - NFULL + NACC + 1))

                    n_idx = 2 * sum(min(P, EFULL - q * P) > 0 for q in range(QB)) + 2 * (ETAIL > 0)
                    n_load = (NB + 1 + (NTAIL > 0) + 8 + 2 * HEADS + 2 + 1 + 4 + 2 + 2)

                    @block.gpsimd
                    def _(pool):
                        pool.iota(iota, [[1, P]], base=0, channel_multiplier=0,
                                  allow_small_or_imprecise_dtypes=True).then_inc(pads, 1)
                        pool.iota(small[:, 0:1], [[0, 1]], base=0, channel_multiplier=1,
                                  allow_small_or_imprecise_dtypes=True).then_inc(pads, 1)

                    @block.vector
                    def _(dve):
                        link = Steps(dve, steps)
                        dve.memset(rawI[:, 0, :, :], 0)
                        dve.memset(rawI[:, 1, :, :], -4096)
                        dve.memset(acc[:, 0, :], 0.0)
                        dve.memset(X[:, NFULL:NT, :], 0.0)
                        dve.memset(W("m1a"), 0.0)
                        dve.memset(W("m1b"), 0.0)
                        dve.memset(ablk, 0.0)
                        dve.memset(zero4, 0.0)
                        dve.memset(ones[:, :], 1.0)
                        dve.memset(cols[:, EPSC:EPSC + 1], LN_EPS)
                        link(dve.memset(rows[:, :, :], 0.0))
                        dve.sem_inc(filled)
                        dve.wait_ge(pads, 2)
                        link(dve.tensor_scalar(ident[:, :], iota, small[:, 0:1], None, ALU.is_equal))
                        dve.wait_ge(indices, 16 * n_idx)
                        dve.tensor_copy(rawF[:, :, :, :], rawI[:, :, :, :]).then_inc(asfloat, 1)
                        blocks = [(k, q) for k in range(2) for q in range(QB)]
                        for b, (k, q) in enumerate(blocks):
                            dve.wait_ge(turned, b + 1)
                            c = min(P, ET - q * P)
                            to = (srcI if k == 0 else dstF)[:, q * P:q * P + c]
                            dve.tensor_copy(to, PS[b % 2][:, 0, 0:c]).then_inc(kept, 1)
                        for b in range(NB):
                            dve.wait_ge(turned, len(blocks) + b + 1)
                            to = wext[:, 0:F] if b == IL3 else w2t if b == IMW2 else wt[:, b, :]
                            dve.tensor_copy(to, PS[(len(blocks) + b) % 2][:, 0, 0:P]).then_inc(kept, 1)
                        dve.wait_ge(made, 5)
                        dve.tensor_copy(wext[:, F:F + 2 * HEADS], PS[2][:, 0, 0:2 * HEADS])
                        dve.tensor_tensor(rows[0:1, 1, :], rows[0:1, 1, :], PS[2][0:1, 1, 0:F], ALU.add)
                        dve.tensor_copy(rows[0:1, 2, :], PS[3][0:1, 0, 0:F])
                        dve.tensor_tensor(cols[:, CU:CU + 1], ub1, PS[3][:, 1, 0:1], ALU.add)
                        dve.wait_ge(made, 6)
                        dve.tensor_copy(W("w2u"), PS[0][:, 1, 0:F])
                        first = dstF[:, :].rearrange("p (g j) -> p g j", j=G)[0:1, :, 0]
                        link(dve.tensor_copy(base0[0:1, :], first))
                        dve.sem_inc(filled)
                        dve.wait_ge(made, 7)
                        link(dve.tensor_copy(base0[:, :], PS[1][:, 1, 0:NG]))
                        d3, b3 = (v[:, :].rearrange("p (g j) -> p g j", j=G) for v in (dl, dstF))
                        link(dve.tensor_tensor(d3, b3, base0[:, :].unsqueeze(2).to_broadcast([P, NG, G]), ALU.subtract))
                        inw = rawF[:, :, :, :].rearrange("p k q c -> p (k q c)")[:, 0:ET]
                        link(dve.tensor_scalar(inw, dl[:, :], 0.0, None, ALU.is_ge))
                        link(dve.scalar_tensor_tensor(out=inw, in0=dl[:, :], scalar=float(P - 1), in1=inw,
                                                      op0=ALU.is_le, op1=ALU.mult))
                        if ETAIL:
                            link(dve.tensor_scalar(small[:, 1:2], small[:, 0:1], float(ETAIL), None, ALU.is_ge))
                            link(dve.tensor_tensor(inw[:, EFULL:EFULL + 1], inw[:, EFULL:EFULL + 1], small[:, 1:2], ALU.max))
                        link(dve.tensor_reduce(small[:, 2:3], inw[:, 0:EFULL + (ETAIL > 0)], AX.X, ALU.min))
                        dve.sem_inc(filled)
                        dve.wait_ge(made, 8)
                        link(dve.tensor_reduce(small[0:1, 3:4], PS[2][0:1, 0, 0:P], AX.X, ALU.min))
                        dve.sem_inc(filled)
                        link(dve.tensor_scalar(small[0:1, 4:5], small[0:1, 3:4], float(1 - NT), float(NT), ALU.mult, ALU.add))
                        link(dve.tensor_copy(sweeps[0:1, 0:1], small[0:1, 4:5]))
                        dve.wait_ge(made, 9)
                        link(dve.tensor_copy(small[:, 5:6], PS[3][:, 0, 0:1]))
                        link(dve.tensor_scalar(step[:, :], small[:, 5:6], float(-P), float(P), ALU.mult, ALU.add))
                        link(dve.tensor_scalar(base0[:, :], base0[:, :], small[:, 5:6], None, ALU.mult))
                        for t in range(NT):
                            last = dve.bn_stats(stats[:, t, :], X[:, t, :])
                        link(last)

                    @block.tensor
                    def _(pe):
                        blocks = [(k, q) for k in range(2) for q in range(QB)]
                        pe.wait_ge(asfloat, 1)
                        pe.wait_ge(steps, 2)
                        for b, (k, q) in enumerate(blocks):
                            if b >= 2:
                                pe.wait_ge(kept, b - 1)
                            pe.transpose(PS[b % 2][:, 0, 0:P], rawF[:, k, q, :], ident[:, :]).then_inc(turned, 1)
                        pe.wait_ge(loaded, 16 * n_load)
                        for b in range(NB):
                            pe.wait_ge(kept, len(blocks) + b - 1)
                            pe.transpose(PS[(len(blocks) + b) % 2][:, 0, 0:P], nat[:, b, :], ident[:, :]).then_inc(turned, 1)
                        pe.matmul(PS[2][:, 0, 0:2 * HEADS], nat[:, IL3, :], ablk, start=True, stop=True).then_inc(made, 1)
                        pe.matmul(PS[2][0:1, 1, 0:F], gcol[0:GD, :], w1g[0:GD, :], start=True, stop=True).then_inc(made, 1)
                        pe.matmul(PS[3][0:1, 0, 0:F], mb2, u1b, start=True, stop=True).then_inc(made, 1)
                        pe.matmul(PS[3][:, 1, 0:1], u1c[0:GD, :], gcol[0:GD, :], start=True, stop=True).then_inc(made, 1)
                        pe.wait_ge(kept, len(blocks) + NB)
                        pe.sem_inc(made)
                        pe.matmul(PS[0][:, 1, 0:F], w2t, u1b, start=True, stop=True).then_inc(made, 1)
                        pe.wait_ge(filled, 2)
                        pe.matmul(PS[1][:, 1, 0:NG], ones[0:1, :], base0[0:1, :], start=True, stop=True).then_inc(made, 1)
                        pe.wait_ge(filled, 3)
                        pe.transpose(PS[2][0:1, 0, 0:P], small[:, 2:3], ident[:, :]).then_inc(made, 1)
                        pe.wait_ge(filled, 4)
                        pe.matmul(PS[3][:, 0, 0:1], ones[0:1, :], small[0:1, 3:4], start=True, stop=True).then_inc(made, 1)

        def reverse_edges():
            s, sem = phase()
            with s:
                base_ready, used, hot, gate, steps, added = (sem("base_ready"), sem("groups_used"), sem("onehot_ready"),
                                                             sem("gate"), sem("vector_steps"), sem("added"))
                window = [sem(f"window_rows{k}") for k in range(2)]
                scattered = [sem(f"scattered{q}") for q in range(NACC)]
                spread, same_ready, mixed, copied, summed, out_ready, idx_ready, taken, start = (
                    sem("sources_spread"), sem("same_ready"), sem("mixed"), sem("mixed_copied"), sem("summed"),
                    sem("rows_ready"), sem("idx_ready"), sem("rows_scattered"), sem("degrees"))
                hwin = work[:, 0:2 * F].rearrange("p (k f) -> p k f", k=2)
                rows_out = work[:, 256:256 + G * F].rearrange("p (j f) -> p j f", j=G)
                same = work[:, 2304:3328].rearrange("p (j f) -> p j f", j=G)
                lead = work[:, 3328:3328 + 2 * G].rearrange("p (k j) -> p k j", k=2)
                below = work[:, 3392:3392 + P]
                trash = work[:, 3584:3585]
                diag = bufC
                mixT = bufB

                def halves_of(v):
                    return v[:, :, :].rearrange("p (q j) f -> p q (j f)", q=2)

                with nc.Block() as block:
                    @block.gpsimd
                    def _(pool):
                        pool.iota(small[:, 0:1], [[0, 1]], base=0, channel_multiplier=1,
                                  allow_small_or_imprecise_dtypes=True).then_inc(start, 1)
                        count = pool.value_load(sweeps[0:1, 0:1], min_val=1, max_val=NT)
                        with pool.Fori(0, count) as sw:
                            with pool.Fori(0, NG) as g:
                                n = sw * NG + g
                                pool.wait_ge(out_ready, 2 * n + 2)
                                pool.wait_ge(idx_ready, n + 1)
                                pool.sem_inc(gate)
                                for j in range(G):
                                    q = j % NACC
                                    pool.indirect_dma_start(T_PART[q], bass.IndirectOffsetOnAxis(ap=idx[:, 0, j:j + 1], axis=0),
                                                            rows_out[:, j, :], None, compute_op=ALU.add
                                                            ).then_inc(scattered[q], 16)
                                    pool.wait_ge(scattered[(j + 1) % NACC], 32 * n + 16 * ((j + 1) // NACC)) if j + 1 >= NACC else None
                                    pool.sem_inc(gate)
                                for q in range(NACC):
                                    pool.wait_ge(scattered[q], 32 * n + 32)
                                pool.sem_inc(taken)

                    @block.sync
                    def _(sp):
                        count = sp.value_load(sweeps[0:1, 0:1], min_val=1, max_val=NT)
                        with sp.Fori(0, count) as sw:
                            sp.wait_ge(base_ready, sw + 1)
                            sp.sem_inc(gate)
                            with sp.Fori(0, PAIRS) as i:
                                for k in range(2):
                                    n = sw * NG + 2 * i + k
                                    at = sp.value_load(baseI[0:1, bass.ds(2 * i + k, 1)], min_val=0, max_val=NW - P)
                                    sp.wait_ge(used, n + 1)
                                    sp.dma_start(hwin[:, k, :], T_L0[bass.ds(at, P), :]).then_inc(window[k], 16)

                    @block.tensor
                    def _(pe):
                        count = pe.value_load(sweeps[0:1, 0:1], min_val=1, max_val=NT)
                        pe.sem_inc(used, 2)
                        with pe.Fori(0, count) as sw:
                            with pe.Fori(0, PAIRS) as i:
                                for k in range(2):
                                    n = sw * NG + 2 * i + k
                                    pe.wait_ge(hot, n + 1)
                                    for j in range(G):
                                        last = pe.matmul(PS[1][:, j // 4, (j % 4) * P:(j % 4 + 1) * P], ones[:, :],
                                                         diag[:, j, :], start=True, stop=True)
                                    last.then_inc(spread, 1)
                                    for j in range(G):
                                        pe.matmul(PS[0][:, 0, k * P:(k + 1) * P], ones[:, :], onehot[:, j, :],
                                                  start=j == 0, stop=j == G - 1)
                                    pe.wait_ge(same_ready, n + 1)
                                    for j in range(G):
                                        last = pe.matmul(PS[2][:, j // 4, (j % 4) * P:(j % 4 + 1) * P], onehot[:, j, :],
                                                         same[:, j, :], start=True, stop=True)
                                        if j % 4 == 3:
                                            last.then_inc(mixed, 1)
                                    pe.wait_ge(window[k], 16 * (sw * PAIRS + i + 1))
                                    for j in range(G):
                                        if j % 4 == 0:
                                            pe.wait_ge(copied, 2 * n + j // 4 + 1)
                                        last = pe.matmul(PS[3][:, j // 4, (j % 4) * P:(j % 4 + 1) * P], mixT[:, j, :],
                                                         hwin[:, k, :], start=True, stop=True)
                                        if j % 4 == 3:
                                            last.then_inc(summed, 1)
                                    pe.wait_ge(summed, 2 * n + 2)
                                    pe.sem_inc(used)

                    @block.scalar
                    def _(act):
                        count = act.value_load(sweeps[0:1, 0:1], min_val=1, max_val=NT)
                        act.wait_ge(base_ready, 1)
                        act.sem_inc(taken)
                        with act.Fori(0, count) as sw:
                            with act.Fori(0, NG) as g:
                                n = sw * NG + g
                                for q in range(2):
                                    act.wait_ge(mixed, 2 * n + q + 1)
                                    act.copy(halves_of(mixT)[:, q, :], PS[2][:, q, :]).then_inc(copied, 1)
                                act.wait_ge(taken, n + 1)
                                for q in range(2):
                                    act.wait_ge(summed, 2 * n + q + 1)
                                    act.copy(halves_of(rows_out)[:, q, :], PS[3][:, q, :]).then_inc(out_ready, 1)

                    @block.vector
                    def _(dve):
                        link = Steps(dve, steps)
                        dve.memset(acc[:, 1, :], 0.0)
                        dve.wait_ge(start, 1)
                        dve.tensor_scalar(below, iota, small[:, 0:1], None, ALU.is_lt)
                        dve.tensor_scalar(trash, small[:, 0:1], float(NT * P), None, ALU.add)
                        link(dve.tensor_copy(baseF[:, :], base0[:, :]))
                        dve.sem_inc(added)
                        count = dve.value_load(sweeps[0:1, 0:1], min_val=1, max_val=NT)
                        at = dve.alloc_register("degree_window")
                        SPS, SPG = 3, 8
                        with dve.Fori(0, count) as sw:
                            link.at(1 + sw * (SPS + NG * SPG))
                            d3, s3 = (v[:, :].rearrange("p (g j) -> p g j", j=G) for v in (dl, dstF))
                            link(dve.tensor_copy(baseI[0:1, :], baseF[0:1, :]))
                            link(dve.tensor_tensor(d3, s3, baseF[:, :].unsqueeze(2).to_broadcast([P, NG, G]), ALU.subtract))
                            link(dve.tensor_tensor(baseF[:, :], baseF[:, :], step[:, :].to_broadcast([P, NG]), ALU.add))
                            dve.sem_inc(base_ready)
                            with dve.Fori(0, PAIRS) as i:
                                for k in range(2):
                                    gi = 2 * i + k
                                    n = sw * NG + gi
                                    link.at(1 + SPS + sw * SPS + n * SPG)
                                    source = srcI[:, bass.ds(gi * G, G)]
                                    full = [P, G, P]
                                    link(dve.tensor_tensor(onehot[:, :, :], iota.unsqueeze(1).to_broadcast(full),
                                                           dl[:, bass.ds(gi * G, G)].unsqueeze(2).to_broadcast(full),
                                                           ALU.is_equal))
                                    link(dve.tensor_tensor(diag[:, :, :], ident[:, :].unsqueeze(1).to_broadcast(full),
                                                           source.unsqueeze(2).to_broadcast(full), ALU.mult))
                                    dve.sem_inc(hot)
                                    dve.load(at, baseI[0:1, bass.ds(gi, 1)])
                                    win = dve.snap(at, min_val=0, max_val=NW - P)
                                    dve.wait_ge(spread, n + 1)
                                    link(dve.tensor_tensor(same[:, :, :],
                                                           PS[1][:, :, :].rearrange("p q (j f) -> p (q j) f", f=P),
                                                           source.unsqueeze(2).to_broadcast(full), ALU.is_equal))
                                    dve.sem_inc(same_ready)
                                    link(dve.tensor_tensor(diag[:, :, :], same[:, :, :],
                                                           below.unsqueeze(1).to_broadcast(full), ALU.mult))
                                    link(dve.tensor_reduce(lead[:, 0, :], diag[:, :, :], AX.X, ALU.max))
                                    link(dve.tensor_tensor(lead[:, 1, :], trash.to_broadcast([P, G]), source, ALU.subtract))
                                    link(dve.tensor_tensor(lead[:, 1, :], lead[:, 1, :], lead[:, 0, :], ALU.mult))
                                    dve.wait_ge(taken, n + 1)
                                    dve.tensor_tensor(idx[:, 0, :], lead[:, 1, :], source, ALU.add).then_inc(idx_ready, 1)
                                    dve.wait_ge(used, n + 3)
                                    dve.wait_ge(added, n + 1)
                                    link(dve.tensor_tensor(acc[:, 1, bass.ds(win, P)], acc[:, 1, bass.ds(win, P)],
                                                           PS[0][:, 0, k * P:(k + 1) * P], ALU.add))
                                    dve.sem_inc(added)
                                    assert link.k == SPG
                        dve.tensor_scalar(rcnt[:, :], acc[:, 1, :], 1.0, None, ALU.max).then_inc(start, 1)
                        dve.wait_ge(start, 2)
                        dve.reciprocal(rcnt[:, :], rcnt[:, :]).then_inc(start, 1)
                        dve.wait_ge(start, 3)
                        dve.scalar_tensor_tensor(out=rcnt[:, :], in0=acc[:, 1, :], scalar=0.5, in1=rcnt[:, :],
                                                 op0=ALU.is_ge, op1=ALU.mult)

        def edges(kind, table):
            s, sem = phase()
            halves = 1 if kind in ("sum", "message") else 2
            gbuf = {"wide": g256, "attention": g132}.get(kind, g128)
            with s:
                base_ready, idx_ready, used, hot = sem("base_ready"), sem("idx_ready"), sem("groups_used"), sem("onehot_ready")
                gathered = [sem(f"gathered{k}") for k in range(2)]
                side = [sem(f"side_loaded{k}") for k in range(2)]
                gate, steps, added, summed = sem("gate"), sem("vector_steps"), sem("added"), sem("summed")
                turned, copied, hidden, relu_done, start = (sem("turned"), sem("copied"), sem("hidden"), sem("relu_done"),
                                                            sem("start"))
                logit, colmax, topped, spread, shift, weighted, scaled, wide_w, wsteps = (
                    sem("dst_logits"), sem("colmax"), sem("topped"), sem("spread"), sem("shift"), sem("weights_ready"),
                    sem("scaled"), sem("weights_spread"), sem("rescale_ready"))
                aggA = PS[0]
                pen = rcnt
                Gw = bufB

                with nc.Block() as block:
                    @block.gpsimd
                    def _(pool):
                        count = pool.value_load(sweeps[0:1, 0:1], min_val=1, max_val=NT)
                        with pool.Fori(0, count) as sw:
                            with pool.Fori(0, PAIRS) as i:
                                for k in range(2):
                                    n = sw * NG + 2 * i + k
                                    pool.wait_ge(idx_ready, n + 1)
                                    pool.wait_ge(used, n + 1)
                                    pool.sem_inc(gate)
                                    for j in range(G):
                                        pool.indirect_dma_start(
                                            gbuf[:, k, j, :], None, table,
                                            bass.IndirectOffsetOnAxis(ap=idx[:, k, j:j + 1], axis=0)
                                        ).then_inc(gathered[k], 16)

                    @block.sync
                    def _(sp):
                        if kind == "message":
                            eat = edge_attr_64[0:EFULL * P, :].rearrange("(t p) c -> p t c", p=P)
                            count = sp.value_load(sweeps[0:1, 0:1], min_val=1, max_val=NT)
                            def load(n, t, k, tiles, tail):
                                sp.wait_ge(used, n + 1)
                                to = ea[:, k, :].rearrange("p (j c) -> p j c", c=ED)
                                if tiles:
                                    sp.dma_start(to[:, 0:tiles, :], eat[:, bass.ds(t, tiles), :]).then_inc(side[k], 16)
                                else:
                                    sp.sem_inc(side[k], 16)
                                if tail:
                                    sp.dma_start(to[0:ETAIL, tiles, :], edge_attr_64[EFULL * P:E, :]).then_inc(side[k], 16)
                                else:
                                    sp.sem_inc(side[k], 16)
                            with sp.Fori(0, count) as sw:
                                with sp.Fori(0, PAIRS - 1) as i:
                                    for k in range(2):
                                        load(sw * NG + 2 * i + k, (2 * i + k) * G, k, G, False)
                                for k in range(2):
                                    t = (NG - 2 + k) * G
                                    tiles = min(G, max(0, EFULL - t))
                                    load(sw * NG + NG - 2 + k, t, k, tiles, bool(ETAIL) and tiles < G and t + tiles == EFULL)
                        if kind == "attention":
                            count = sp.value_load(sweeps[0:1, 0:1], min_val=1, max_val=NT)
                            with sp.Fori(0, count) as sw:
                                sp.wait_ge(base_ready, sw + 1)
                                sp.sem_inc(gate)
                                with sp.Fori(0, PAIRS) as i:
                                    for k in range(2):
                                        n = sw * NG + 2 * i + k
                                        at = sp.value_load(baseI[0:1, bass.ds(2 * i + k, 1)], min_val=0, max_val=NW - P)
                                        sp.wait_ge(used, n + 1)
                                        sp.dma_start(dwin[:, k, :], T_DST[bass.ds(at, P), :]).then_inc(side[k], 16)

                    @block.scalar
                    def _(act):
                        count = act.value_load(sweeps[0:1, 0:1], min_val=1, max_val=NT)
                        with act.Fori(0, count) as sw:
                            with act.Fori(0, PAIRS) as i:
                                for k in range(2):
                                    n = sw * NG + 2 * i + k
                                    act.wait_ge(used, n + 1)
                                    act.copy(idx[:, k, :], srcI[:, bass.ds((2 * i + k) * G, G)]).then_inc(idx_ready, 1)
                                for k in range(2):
                                    n = sw * NG + 2 * i + k
                                    if kind == "message":
                                        act.wait_ge(turned, n + 1)
                                        act.copy(bufB[:, 0:4, :], PS[1][:, 0, :].rearrange("p (j f) -> p j f", j=4)
                                                 ).then_inc(copied, 1)
                                        for q in range(2):
                                            act.wait_ge(hidden, 2 * n + q + 1)
                                            act.activation(bufA[:, 4 * q:4 * q + 4, :],
                                                           PS[2][:, q, :].rearrange("p (j f) -> p j f", j=4),
                                                           ACT.Relu).then_inc(relu_done, 1)
                                    if kind == "attention":
                                        act.wait_ge(turned, n + 1)
                                        act.copy(bufC[:, :, :].rearrange("p (q j) f -> p q (j f)", q=2),
                                                 PS[2][:, :, :]).then_inc(copied, 1)
                                        act.wait_ge(shift, n + 1)
                                        act.activation(lg[:, 1, :], lg[:, 0, :], ACT.Exp).then_inc(weighted, 1)
                                        act.activation(winF, winF, ACT.Exp).then_inc(scaled, 1)
                                        act.wait_ge(weighted, n + 1)
                                        act.copy(bufA[:, :, :].rearrange("p j (h f) -> p (j h) f", f=HF),
                                                 lg[:, 1, :].unsqueeze(2).to_broadcast([P, G * HEADS, HF])
                                                 ).then_inc(wide_w, 1)

                    @block.tensor
                    def _(pe):
                        count = pe.value_load(sweeps[0:1, 0:1], min_val=1, max_val=NT)
                        pe.sem_inc(used, 2)
                        with pe.Fori(0, count) as sw:
                            with pe.Fori(0, PAIRS) as i:
                                for k in range(2):
                                    n = sw * NG + 2 * i + k
                                    m = sw * PAIRS + i
                                    A = aggA[:, 0, k * P:(k + 1) * P]
                                    B = aggA[:, 1, k * P:(k + 1) * P]
                                    if kind == "message":
                                        pe.wait_ge(side[k], 32 * (m + 1))
                                        for q in range(4):
                                            last = pe.transpose(PS[1][:, 0, q * P:(q + 1) * P],
                                                                ea[:, k, q * P:(q + 1) * P], ident[:, :])
                                        last.then_inc(turned, 1)
                                    pe.wait_ge(hot, n + 1)
                                    if kind == "attention":
                                        for j in range(G):
                                            last = pe.transpose(PS[2][:, j // 4, (j % 4) * P:(j % 4 + 1) * P],
                                                                onehot[:, j, :], ident[:, :])
                                        last.then_inc(turned, 1)
                                        pe.wait_ge(side[k], 16 * (m + 1))
                                        pe.wait_ge(copied, n + 1)
                                        for j in range(G):
                                            last = pe.matmul(PS[1][:, 0, HEADS * j:HEADS * (j + 1)], bufC[:, j, :],
                                                             dwin[:, k, :], start=True, stop=True)
                                        last.then_inc(logit, 1)
                                        pe.wait_ge(colmax, n + 1)
                                        pe.transpose(PS[1][0:1, 1, 0:P], small[:, 0:1], ident[:, :]).then_inc(topped, 1)
                                        pe.wait_ge(spread, n + 1)
                                        pe.matmul(PS[1][:, 1, P:P + 1], ones[0:1, :], small[0:1, 1:2],
                                                  start=True, stop=True).then_inc(wsteps, 1)
                                        pe.wait_ge(summed, n + 1)
                                        lhs = [Gw, bufA]
                                    elif kind == "message":
                                        pe.wait_ge(gathered[k], (G * 16) * (m + 1))
                                        pe.wait_ge(copied, n + 1)
                                        for j in range(G):
                                            to = PS[2][:, j // 4, (j % 4) * P:(j % 4 + 1) * P]
                                            pe.matmul(to, bufB[:, j // 2, :], W("m1b" if j % 2 else "m1a"), start=True, stop=False)
                                            last = pe.matmul(to, ident[:, :], gbuf[:, k, j, :], start=False, stop=True)
                                            if j % 4 == 3:
                                                last.then_inc(hidden, 1)
                                        lhs = [bufA]
                                    else:
                                        pe.wait_ge(gathered[k], (G * 16) * (m + 1))
                                        lhs = [gbuf[:, k]]
                                    for j in range(G):
                                        if kind == "message" and j % 4 == 0:
                                            pe.wait_ge(relu_done, 2 * n + j // 4 + 1)
                                        last = pe.matmul(A, lhs[0][:, j, 0:P], onehot[:, j, :], start=j == 0, stop=j == G - 1)
                                        if halves == 2:
                                            two = (gbuf[:, k, j, P:2 * P] if kind == "wide"
                                                   else bufA[:, j, :])
                                            last = pe.matmul(B, two, onehot[:, j, :], start=j == 0, stop=j == G - 1)
                                    last.then_inc(used, 1)

                    @block.vector
                    def _(dve):
                        link = Steps(dve, steps)
                        dve.memset(acc[:, 0:halves, :], 0.0)
                        if kind == "attention":
                            dve.memset(scol, FAR)
                            dve.memset(small[:, 2:3], FAR)
                        link(dve.tensor_copy(baseF[:, :], base0[:, :]))
                        dve.sem_inc(added)
                        count = dve.value_load(sweeps[0:1, 0:1], min_val=1, max_val=NT)
                        at = dve.alloc_register(f"window_{phase.n}")
                        SPS = 4 + (3 if kind == "attention" else 0)
                        SPG = 9 if kind == "attention" else 1
                        with dve.Fori(0, count) as sw:
                            link.at(1 + sw * (SPS + NG * SPG))
                            d3, s3 = (v[:, :].rearrange("p (g j) -> p g j", j=G) for v in (dl, dstF))
                            link(dve.tensor_copy(baseI[0:1, :], baseF[0:1, :]))
                            link(dve.tensor_tensor(d3, s3, baseF[:, :].unsqueeze(2).to_broadcast([P, NG, G]), ALU.subtract))
                            if kind == "attention":
                                link(dve.tensor_scalar(pen[:, 0:ET], dl[:, :], 0.0, None, ALU.is_ge))
                                link(dve.scalar_tensor_tensor(out=pen[:, 0:ET], in0=dl[:, :], scalar=float(P - 1),
                                                              in1=pen[:, 0:ET], op0=ALU.is_le, op1=ALU.mult))
                                link(dve.tensor_scalar(pen[:, 0:ET], pen[:, 0:ET], -FAR, FAR, ALU.mult, ALU.add))
                            link(dve.tensor_tensor(baseF[:, :], baseF[:, :], step[:, :].to_broadcast([P, NG]), ALU.add))
                            link(dve.tensor_copy(small[:, 7:8], step[:, :]))
                            dve.sem_inc(base_ready)
                            with dve.Fori(0, PAIRS) as i:
                                for k in range(2):
                                    n = sw * NG + 2 * i + k
                                    link.at(1 + SPS + sw * SPS + n * SPG)
                                    gi = 2 * i + k
                                    dve.tensor_tensor(
                                        onehot[:, :, :], iota.unsqueeze(1).to_broadcast([P, G, P]),
                                        dl[:, bass.ds(gi * G, G)].unsqueeze(2).to_broadcast([P, G, P]),
                                        ALU.is_equal).then_inc(hot, 1)
                                    dve.load(at, baseI[0:1, bass.ds(gi, 1)])
                                    win = dve.snap(at, min_val=0, max_val=NW - P)
                                    if kind == "attention":
                                        L = lg[:, 0, :].rearrange("p (j h) -> p j h", h=HEADS)
                                        dve.wait_ge(gathered[k], (G * 16) * (sw * PAIRS + i + 1))
                                        dve.wait_ge(logit, n + 1)
                                        link(dve.tensor_tensor(L, gbuf[:, k, :, F:TW],
                                                               PS[1][:, 0, 0:G * HEADS].rearrange("p (j h) -> p j h", h=HEADS),
                                                               ALU.add))
                                        link(dve.scalar_tensor_tensor(out=lg[:, 2, :], in0=lg[:, 0, :], scalar=SLOPE,
                                                                      in1=lg[:, 0, :], op0=ALU.mult, op1=ALU.max))
                                        link(dve.tensor_tensor(
                                            L, lg[:, 2, :].rearrange("p (j h) -> p j h", h=HEADS),
                                            pen[:, bass.ds(gi * G, G)].unsqueeze(2).to_broadcast([P, G, HEADS]), ALU.add))
                                        link(dve.tensor_reduce(small[:, 3:4], lg[:, 0, :], AX.X, ALU.max))
                                        dve.tensor_tensor(small[:, 0:1], small[:, 3:4], small[:, 2:3], ALU.max).then_inc(colmax, 1)
                                        dve.wait_ge(topped, n + 1)
                                        dve.tensor_reduce(small[0:1, 1:2], PS[1][0:1, 1, 0:P], AX.X, ALU.max).then_inc(spread, 1)
                                        dve.wait_ge(wsteps, n + 1)
                                        link(dve.tensor_copy(small[:, 2:3], PS[1][:, 1, P:P + 1]))
                                        dve.tensor_scalar(lg[:, 0, :], lg[:, 0, :], small[:, 2:3], None, ALU.subtract)
                                        link(dve.tensor_scalar(winF, scol[:, bass.ds(win, P)], small[:, 2:3], None, ALU.subtract))
                                        dve.sem_inc(shift)
                                        link(dve.tensor_scalar(scol[:, bass.ds(win, P)], iota, 0.0, small[:, 2:3],
                                                               ALU.mult, ALU.add))
                                        dve.wait_ge(wide_w, n + 1)
                                        dve.tensor_tensor(Gw[:, :, :], gbuf[:, k, :, 0:F], bufA[:, :, :], ALU.mult
                                                          ).then_inc(summed, 1)
                                        dve.wait_ge(scaled, n + 1)
                                        dve.wait_ge(added, n + 1)
                                        link(dve.tensor_tensor(acc[:, :, bass.ds(win, P)], acc[:, :, bass.ds(win, P)],
                                                               winF.unsqueeze(1).to_broadcast([P, 2, P]), ALU.mult))
                                    dve.wait_ge(used, n + 3)
                                    dve.wait_ge(added, n + 1)
                                    link(dve.tensor_tensor(acc[:, 0:halves, bass.ds(win, P)], acc[:, 0:halves, bass.ds(win, P)],
                                                           aggA[:, 0:halves, k * P:(k + 1) * P], ALU.add))
                                    dve.sem_inc(added)
                                    assert link.k == SPG
        def moments():
            s, sem = phase()
            with s:
                steps, var, root = sem("vector_steps"), sem("var"), sem("root")
                me, mo = stats[:, :, 1], stats[:, :, 4]
                with nc.Block() as block:
                    @block.vector
                    def _(dve):
                        link = Steps(dve, steps)
                        mean, dif, r, nb, v = (ln[:, q, :] for q in range(5))
                        dve.tensor_tensor(mean, me, mo, ALU.add)
                        dve.tensor_tensor(dif, me, mo, ALU.subtract)
                        link(dve.tensor_tensor(v, stats[:, :, 2], stats[:, :, 5], ALU.add))
                        dve.tensor_scalar(mean, mean, 0.5, None, ALU.mult)
                        link(dve.tensor_tensor(dif, dif, dif, ALU.mult))
                        link(dve.tensor_scalar(dif, dif, 0.25, None, ALU.mult))
                        link(dve.scalar_tensor_tensor(out=v, in0=v, scalar=1.0 / F, in1=dif, op0=ALU.mult, op1=ALU.add))
                        dve.sem_inc(var)
                        dve.wait_ge(root, 1)
                        link(dve.reciprocal(r, r))
                        link(dve.scalar_tensor_tensor(out=nb, in0=mean, scalar=-1.0, in1=r, op0=ALU.mult, op1=ALU.mult))

                    @block.scalar
                    def _(act):
                        act.wait_ge(var, 1)
                        act.activation(ln[:, 2, :], ln[:, 4, :], ACT.Sqrt, bias=cols[:, EPSC:EPSC + 1]).then_inc(root, 1)

        def normalise(kind, table):
            moments()
            s, sem = phase()
            with s:
                normed, turned, copied, proj, evac = sem("normed"), sem("turned"), sem("copied"), sem("proj"), sem("evac")
                moved = sem("moved")
                stored = [sem(f"stored{a}") for a in range(U)]
                stored2 = [sem(f"stored_d{a}") for a in range(U)] if kind == "attention" else None
                width = {"plain": F, "message": F, "attention": TW}[kind]
                with nc.Block() as block:
                    @block.scalar
                    def _(act):
                        for i in iterations(act, NI):
                            for a in range(U):
                                t = i * U + a
                                after(act, turned, i * U)
                                if kind == "plain":
                                    after(act, stored[a], 16 * i)
                                act.activation(hn[:, a, :], X[:, bass.ds(t, 1), :].rearrange("p o f -> p (o f)"), ACT.Relu,
                                               bias=ln[:, 3, bass.ds(t, 1)], scale=ln[:, 2, bass.ds(t, 1)]
                                               ).then_inc(normed, 1)
                            for a in range(U):
                                t = i * U + a
                                act.wait_ge(turned, t + 1)
                                after(act, moved, i * U)
                                after(act, proj, i * U)
                                act.copy(hs[:, a, :], PS[a % 2][:, 0, 0:P]).then_inc(copied, 1)

                    @block.gpsimd
                    def _(pool):
                        for i in iterations(pool, NI):
                            for a in range(U):
                                t = i * U + a
                                pool.wait_ge(copied, t + 1)
                                pool.tensor_copy(Hbuf[:, 0, bass.ds(t * P, P)], hs[:, a, :]).then_inc(moved, 1)

                    @block.tensor
                    def _(pe):
                        for i in iterations(pe, NI):
                            for a in range(U):
                                t = i * U + a
                                pe.wait_ge(normed, t + 1)
                                after(pe, copied, t - 1 if a >= 2 else i * U)
                                pe.transpose(PS[a % 2][:, 0, 0:P], hn[:, a, :], ident[:, :]).then_inc(turned, 1)
                                if kind == "plain":
                                    pe.sem_inc(proj)
                                else:
                                    pe.wait_ge(copied, t + 1)
                                    after(pe, evac, t - 1 if a >= 2 else i * U)
                                    if kind == "message":
                                        to = PS[2 + a % 2][:, 0, 0:F]
                                        pe.matmul(to, hs[:, a, :], W("m1n"), start=True, stop=False)
                                        pe.matmul(to, ones[0:1, :], rows[0:1, 1, :], start=False, stop=True).then_inc(proj, 1)
                                    else:
                                        pe.matmul(PS[2 + a % 2][:, 0, 0:F + 2 * HEADS], hs[:, a, :], wext[:, :],
                                                  start=True, stop=True).then_inc(proj, 1)

                    @block.vector
                    def _(dve):
                        if kind != "plain":
                            for i in iterations(dve, NI):
                                for a in range(U):
                                    t = i * U + a
                                    dve.wait_ge(proj, t + 1)
                                    after(dve, stored[a], 16 * i)
                                    if kind == "attention":
                                        after(dve, stored2[a], 16 * i)
                                    w = F if kind == "message" else F + 2 * HEADS
                                    dve.tensor_copy(nm[:, a, 0:w], PS[2 + a % 2][:, 0, 0:w]).then_inc(evac, 1)

                    @block.sync
                    def _(sp):
                        for i in iterations(sp, NI):
                            for a in range(U):
                                t = i * U + a
                                sp.wait_ge(normed if kind == "plain" else evac, t + 1)
                                of = hn[:, a, :] if kind == "plain" else nm[:, a, 0:width]
                                sp.dma_start(table[bass.ds(t * P, P), :], of).then_inc(stored[a], 16)
                                if kind == "attention":
                                    sp.dma_start(T_DST[bass.ds(t * P, P), :], nm[:, a, TW:TW + HEADS]).then_inc(stored2[a], 16)
                        for a in range(U):
                            sp.wait_ge(stored[a], 16 * NI)
                            if kind == "attention":
                                sp.wait_ge(stored2[a], 16 * NI)

        def nodes(kind):
            s, sem = phase()
            with s:
                meaned, dense, act1, dense2, act2, turned, taken, moved, steps = (
                    sem("meaned"), sem("dense"), sem("act1"), sem("dense2"), sem("act2"), sem("turned"), sem("taken"),
                    sem("moved"), sem("vector_steps"))
                stored = [sem(f"stored{a}") for a in range(U)]
                parts = work[:, 3584:7168].rearrange("p (a q f) -> p a q f", a=U, q=NACC)
                outs = {"conv1": 2, "conv2": 2}.get(kind, 1)
                ins_ = 2 if kind == "conv2" else 1
                width = {"conv1": 2 * F, "conv2": F}.get(kind, 0)
                table = {"conv1": T_C2, "conv2": T_C3}.get(kind)
                hasdense = kind in ("l0", "conv1", "conv2", "update")
                terms = {
                    "l0": [[("l0x", (Hbuf, 0))]],
                    "conv1": [[(f"c1l0{o}", (acc, 0)), (f"c1r0{o}", (Hbuf, 0))] for o in range(2)],
                    "conv2": [[(f"c2l{q}{o}", (acc, q)) for q in range(2)] + [(f"c2r{q}{o}", (Hbuf, q)) for q in range(2)]
                              for o in range(2)],
                    "update": [[("w2u", (acc, 0)), ("u1h", (Hbuf, 0))]],
                }.get(kind)
                bias = {"l0": [B0], "conv1": [B1, B1 + 1], "conv2": [B2, B2 + 1], "update": [CU]}.get(kind)
                with nc.Block() as block:
                    @block.vector
                    def _(dve):
                        link = Steps(dve, steps)
                        if kind in ("conv1", "update"):
                            link(dve.tensor_tensor(acc[:, 0, :], acc[:, 0, :], rcnt[:, :], ALU.mult))
                            if kind == "update":
                                link(dve.tensor_scalar(acc[0:1, 1, :], rcnt[0:1, :], 0.0, None, ALU.is_gt))
                        if kind == "conv2":
                            for q in range(2):
                                link(dve.tensor_tensor(acc[:, q, :], acc[:, q, :], rcnt[:, :], ALU.mult))
                        if kind == "final":
                            link(dve.tensor_scalar(scol, scol, small[:, 2:3], None, ALU.subtract))
                            dve.sem_inc(meaned)
                            dve.wait_ge(act1, 1)
                            for q in (1, 0):
                                link(dve.tensor_tensor(acc[:, q, :], acc[:, q, :], scol, ALU.mult))
                            link(dve.tensor_scalar(acc[:, 1, :], acc[:, 1, :], ATT_EPS, None, ALU.add))
                            link(dve.reciprocal(acc[:, 1, :], acc[:, 1, :]))
                        dve.sem_inc(meaned)
                        k0 = link.k
                        per = {"l0": 1, "conv3": 1, "update": 1, "final": 0}.get(kind, 0) * U
                        for i in iterations(dve, NI):
                            link.at(k0 + i * per)
                            if kind in ("conv3", "final"):
                                for a in range(U):
                                    t = i * U + a
                                    after(dve, turned, i * U)
                                    other = rcnt if kind == "conv3" else acc[:, 1, :]
                                    dve.tensor_tensor(st[:, a, 0, :], acc[:, 0, bass.ds(t * P, P)],
                                                      other[:, bass.ds(t * P, P)], ALU.mult).then_inc(act1, 1)
                            for a in range(U):
                                t = i * U + a
                                Xt = X[:, bass.ds(t, 1), :].rearrange("p o f -> p (o f)")
                                dve.wait_ge(turned, t + 1)
                                if kind in ("l0", "final"):
                                    dve.tensor_tensor(Xt, Xt, PS[2 + a % 2][:, 0, 0:F], ALU.add).then_inc(taken, 1)
                                if kind == "l0":
                                    dve.wait_ge(taken, t + 1)
                                if kind == "conv3":
                                    R = Hbuf[:, 0, bass.ds(t * P, P)]
                                    link(dve.tensor_tensor(tmp[:, a, :], PS[2 + a % 2][:, 0, 0:F], R, ALU.add))
                                    dve.scalar_tensor_tensor(out=Xt, in0=tmp[:, a, :], scalar=0.0, in1=Xt, op0=ALU.max,
                                                             op1=ALU.add).then_inc(taken, 1)
                                    dve.wait_ge(taken, t + 1)
                                if kind in ("l0", "conv3"):
                                    dve.bn_stats(stats[:, bass.ds(t, 1), :].rearrange("p o c -> p (o c)"), Xt)
                                if kind in ("conv1", "conv2"):
                                    after(dve, stored[a], 16 * i)
                                    dve.tensor_copy(nm[:, a, 0:width], PS[2 + a % 2][:, 0, 0:width]).then_inc(taken, 1)
                                    if kind == "conv2":
                                        dve.tensor_copy(Hbuf[:, 0, bass.ds(t * P, P)], PS[2 + a % 2][:, 1, 0:F]).then_inc(moved, 1)
                                if kind == "update":
                                    Y = Hbuf[:, 1, bass.ds(t * P, P)]
                                    dve.tensor_copy(Y, PS[2 + a % 2][:, 0, 0:F]).then_inc(taken, 1)
                                    dve.wait_ge(taken, t + 1)
                                    dve.bn_stats(stats[:, bass.ds(t, 1), :].rearrange("p o c -> p (o c)"), Y)

                    @block.scalar
                    def _(act):
                        if kind == "final":
                            act.wait_ge(meaned, 1)
                            act.activation(scol, scol, ACT.Exp).then_inc(act1, 1)
                        if hasdense:
                            for i in iterations(act, NI):
                                for a in range(U):
                                    t = i * U + a
                                    if kind == "l0":
                                        act.wait_ge(dense2, t + 1)
                                        after(act, dense, i * U)
                                        act.copy(st[:, a, 1, :], PS[a % 2][:, 1, 0:P]).then_inc(act2, 1)
                                    act.wait_ge(dense, t + 1)
                                    after(act, turned, i * U)
                                    if kind == "conv1":
                                        after(act, moved, i * U)
                                    for o in range(outs):
                                        last = act.activation(st[:, a, o, :], PS[a % 2][:, o, 0:P], ACT.Relu,
                                                              bias=cols[:, bias[o]:bias[o] + 1])
                                    last.then_inc(act1, 1)
                                    if kind == "update":
                                        act.wait_ge(dense2, t + 1)
                                        act.activation(st[:, a, 1, :], PS[a % 2][:, 1, 0:P], ACT.Identity,
                                                       bias=cols[:, UB2:UB2 + 1]).then_inc(act2, 1)

                    @block.gpsimd
                    def _(pool):
                        if kind == "conv1":
                            for i in iterations(pool, NI):
                                for a in range(U):
                                    t = i * U + a
                                    pool.wait_ge(act1, t + 1)
                                    pool.tensor_copy(Hbuf[:, :, bass.ds(t * P, P)], st[:, a, :, :]).then_inc(moved, 1)

                    @block.sync
                    def _(sp):
                        if kind == "l0":
                            for i in iterations(sp, NI):
                                for a in range(U):
                                    t = i * U + a
                                    after(sp, dense2, i * U)
                                    for q in range(NACC):
                                        sp.dma_start(parts[:, a, q, :], T_PART[q][bass.ds(t * P, P), :]).then_inc(stored[a], 16)
                        if width:
                            for i in iterations(sp, NI):
                                for a in range(U):
                                    t = i * U + a
                                    sp.wait_ge(taken, t + 1)
                                    sp.dma_start(table[bass.ds(t * P, P), :], nm[:, a, 0:width]).then_inc(stored[a], 16)
                            for a in range(U):
                                sp.wait_ge(stored[a], 16 * NI)

                    @block.tensor
                    def _(pe):
                        pe.wait_ge(meaned, 2 if kind == "final" else 1)
                        for i in iterations(pe, NI):
                            def back(a):
                                t = i * U + a
                                if kind == "update":
                                    pe.wait_ge(act2, t + 1)
                                else:
                                    pe.wait_ge(act1, t + 1 + (kind == "final"))
                                after(pe, taken, t - 1 if a >= 2 else i * U)
                                if kind == "conv2":
                                    after(pe, moved, t - 1 if a >= 2 else i * U)
                                to = PS[2 + a % 2]
                                if kind == "conv2":
                                    for q in range(2):
                                        pe.matmul(to[:, 0, 0:F], st[:, a, q, :], W(f"c3l{q}0"), start=q == 0, stop=q == 1)
                                    for q in range(2):
                                        pe.matmul(to[:, 1, 0:F], st[:, a, q, :], W(f"c3r{q}0"), start=q == 0, stop=False)
                                    last = pe.matmul(to[:, 1, 0:F], ones[0:1, :], rows[0:1, 0, :], start=False, stop=True)
                                elif kind == "conv1":
                                    for q in range(2):
                                        last = pe.transpose(to[:, 0, q * P:(q + 1) * P], st[:, a, q, :], ident[:, :])
                                else:
                                    last = pe.transpose(to[:, 0, 0:P], st[:, a, int(kind == "update"), :], ident[:, :])
                                last.then_inc(turned, 1)

                            for a in range(U):
                                t = i * U + a
                                if hasdense:
                                    done = act2 if kind == "update" else act1
                                    if kind == "l0":
                                        pe.wait_ge(stored[a], (i + 1) * (16 * NACC))
                                        after(pe, act2, t - 1 if a >= 2 else i * U)
                                        for q in range(NACC):
                                            last = pe.matmul(PS[a % 2][:, 1, 0:P], parts[:, a, q, :], ident[:, :],
                                                             start=q == 0, stop=q == NACC - 1)
                                        last.then_inc(dense2, 1)
                                    after(pe, done, t - 1 if a >= 2 else i * U)
                                    for o in range(outs):
                                        for q, (w, (buf, half)) in enumerate(terms[o]):
                                            end = q == len(terms[o]) - 1 and kind not in ("update", "l0")
                                            last = pe.matmul(PS[a % 2][:, o, 0:P], W(w), buf[:, half, bass.ds(t * P, P)],
                                                             start=q == 0, stop=end)
                                    if kind == "l0":
                                        pe.wait_ge(act2, t + 1)
                                        last = pe.matmul(PS[a % 2][:, 0, 0:P], W("l0a"), st[:, a, 1, :], start=False, stop=True)
                                    if kind == "update":
                                        last = pe.matmul(PS[a % 2][:, 0, 0:P], rows[0:1, 2, :], acc[0:1, 1, bass.ds(t * P, P)],
                                                         start=False, stop=True)
                                    last.then_inc(dense, 1)
                                    if kind == "update":
                                        pe.wait_ge(act1, t + 1)
                                        pe.matmul(PS[a % 2][:, 1, 0:P], W("u2"), st[:, a, 0, :], start=True, stop=False)
                                        pe.matmul(PS[a % 2][:, 1, 0:P], ident[:, :], Hbuf[:, 0, bass.ds(t * P, P)],
                                                  start=False, stop=True).then_inc(dense2, 1)
                                if a >= 1:
                                    back(a - 1)
                            back(U - 1)

        def add_update():
            moments()
            s, sem = phase()
            with s:
                loaded, z, steps = sem("loaded"), sem("z"), sem("vector_steps")
                with nc.Block() as block:
                    @block.sync
                    def _(sp):
                        for to, v in ((gamma, L2_gnn_ln_gamma), (beta, L2_gnn_ln_beta)):
                            sp.dma_start(to, v.rearrange("(o f) -> o f", o=1).to_broadcast([P, F])).then_inc(loaded, 16)

                    @block.scalar
                    def _(act):
                        for i in iterations(act, NI):
                            for a in range(U):
                                t = i * U + a
                                after(act, steps, i * (4 * U))
                                act.activation(tmp[:, a, :], Hbuf[:, 1, bass.ds(t * P, P)], ACT.Identity,
                                               bias=ln[:, 3, bass.ds(t, 1)], scale=ln[:, 2, bass.ds(t, 1)]).then_inc(z, 1)

                    @block.vector
                    def _(dve):
                        link = Steps(dve, steps)
                        dve.wait_ge(loaded, 32)
                        for i in iterations(dve, NI):
                            link.at(i * (4 * U))
                            for a in range(U):
                                t = i * U + a
                                Xt = X[:, bass.ds(t, 1), :].rearrange("p o f -> p (o f)")
                                dve.wait_ge(z, t + 1)
                                link(dve.tensor_tensor(tmp[:, a, :], tmp[:, a, :], gamma, ALU.mult))
                                link(dve.tensor_tensor(tmp[:, a, :], tmp[:, a, :], beta, ALU.add))
                                link(dve.tensor_tensor(Xt, Xt, tmp[:, a, :], ALU.add))
                                link(dve.bn_stats(stats[:, bass.ds(t, 1), :].rearrange("p o c -> p (o c)"), Xt))

        def write_out():
            s, sem = phase()
            with s:
                stored = sem("out_stored")
                with nc.Block() as block:
                    @block.sync
                    def _(sp):
                        sp.dma_start(out[0:NFULL * P, :].rearrange("(t p) f -> p t f", p=P), X[:, 0:NFULL, :]).then_inc(stored, 16)
                        if NTAIL:
                            sp.dma_start(out[NFULL * P:N, :], X[0:NTAIL, NFULL, :]).then_inc(stored, 16)
                        sp.wait_ge(stored, 16 * (1 + (NTAIL > 0)))

        prepare()
        normalise("plain", T_L0)
        reverse_edges()
        nodes("l0")
        normalise("plain", T_C1)
        edges("sum", T_C1)
        nodes("conv1")
        edges("wide", T_C2)
        nodes("conv2")
        edges("sum", T_C3)
        nodes("conv3")
        normalise("message", T_MSG)
        edges("message", T_MSG)
        nodes("update")
        add_update()
        normalise("attention", T_ATT)
        edges("attention", T_ATT)
        nodes("final")
        write_out()


_INS = ['x', 'src', 'dst', 'edge_attr_64', 'L0_gnn_W', 'L0_gnn_b', 'L1_gnn_W1l', 'L1_gnn_b1', 'L1_gnn_W1r', 'L1_gnn_W2l',
        'L1_gnn_b2', 'L1_gnn_W2r', 'L1_gnn_W3l', 'L1_gnn_b3', 'L1_gnn_W3r', 'L2_gnn_global_state', 'L2_gnn_msg_w1',
        'L2_gnn_msg_b1', 'L2_gnn_msg_w2', 'L2_gnn_msg_b2', 'L2_gnn_upd_w1', 'L2_gnn_upd_b1', 'L2_gnn_upd_w2',
        'L2_gnn_upd_b2', 'L2_gnn_ln_gamma', 'L2_gnn_ln_beta', 'L3_gnn_W', 'L3_gnn_a']


def kernel(**inputs):
    import numpy as _np
    import concourse.bacc as _bacc
    from concourse import mybir as _mybir
    from concourse.bass_utils import run_bass_kernel_spmd as _run

    nc = _bacc.Bacc("TRN2", target_bir_lowering=False, num_devices=1)
    arrays, args = {}, []
    for name in _INS:
        a = _np.ascontiguousarray(inputs[name])
        arrays[f"in_{name}_dram"] = a
        args.append(nc.dram_tensor(f"in_{name}_dram", a.shape, _mybir.dt.from_np(a.dtype), kind="ExternalInput").ap())
    shape = tuple(inputs["x"].shape)
    args.append(nc.dram_tensor("out_dram", shape, _mybir.dt.float32, kind="ExternalOutput").ap())
    bass_gnn_preln_d4(nc, *args)
    r = _run(nc, [arrays], core_ids=[0])
    return r.results[0]["out_dram"]
```

```python
import concourse.bass as bass
from concourse import mybir
from contextlib import ExitStack


class Steps:

    def __init__(self, eng, sem):
        self.eng, self.sem, self.base, self.k = eng, sem, 0, 0

    def at(self, base):
        self.base, self.k = base, 0

    def __call__(self, ins):
        self.k += 1
        ins.then_inc(self.sem, 1)
        self.eng.wait_ge(self.sem, self.base + self.k)


def iterations(eng, n):
    yield 0
    if n > 1:
        with eng.Fori(1, n) as i:
            yield i


def after(eng, sem, value):
    if not isinstance(value, int) or value > 0:
        eng.wait_ge(sem, value)


def bass_gnn_preln_d4(nc, x, src, dst, edge_attr_64, L0_gnn_W, L0_gnn_b, L1_gnn_W1l, L1_gnn_b1, L1_gnn_W1r,
                      L1_gnn_W2l, L1_gnn_b2, L1_gnn_W2r, L1_gnn_W3l, L1_gnn_b3, L1_gnn_W3r, L2_gnn_global_state,
                      L2_gnn_msg_w1, L2_gnn_msg_b1, L2_gnn_msg_w2, L2_gnn_msg_b2, L2_gnn_upd_w1, L2_gnn_upd_b1,
                      L2_gnn_upd_w2, L2_gnn_upd_b2, L2_gnn_ln_gamma, L2_gnn_ln_beta, L3_gnn_W, L3_gnn_a, out):
    f32, i32 = mybir.dt.float32, mybir.dt.int32
    ALU, ACT, AX = mybir.AluOpType, mybir.ActivationFunctionType, mybir.AxisListType

    P = 128
    N, F = x.shape
    E, ED = edge_attr_64.shape
    GD = L2_gnn_global_state.shape[0]
    HEADS, HF = L3_gnn_a.shape[0], F // L3_gnn_a.shape[0]
    U = 7
    NT = U * -(-N // (P * U))
    NI = NT // U
    NFULL, NTAIL = N // P, N % P
    G = 8
    PAIRS = -(-E // (2 * G * P))
    NG, ET = 2 * PAIRS, 2 * PAIRS * G
    EFULL, ETAIL = E // P, E % P
    NW = NT * P + P
    QB = -(-ET // P)
    TW = F + HEADS
    LN_EPS, ATT_EPS, SLOPE, FAR = 1e-5, 1e-8, 0.2, -1e30

    T_C1, T_C3, T_MSG = [nc.dram_tensor(f"table_{n}", [NT * P, F], f32, kind="Internal").ap() for n in ("c1", "c3", "msg")]
    T_L0 = nc.dram_tensor("table_l0", [NW, F], f32, kind="Internal").ap()
    T_C2 = nc.dram_tensor("table_c2", [NT * P, 2 * F], f32, kind="Internal").ap()
    T_ATT = nc.dram_tensor("table_att", [NT * P, TW], f32, kind="Internal").ap()
    NACC = 4
    T_PART = [nc.dram_tensor(f"sum_by_source_{q}", [NT * P + P, F], f32, kind="Internal").ap() for q in range(NACC)]
    bf16 = mybir.dt.bfloat16
    DW = 3 * HEADS
    T_DST = nc.dram_tensor("table_dst_logits", [NW, DW], bf16, kind="Internal").ap()

    with ExitStack() as ctx:
        def sb(name, shape, dt=f32):
            return ctx.enter_context(nc.sbuf_tensor(name, shape, dt))

        X = sb("X", [P, NT, F])
        acc = sb("acc", [P, 2, NW])
        rcnt = sb("rcnt", [P, NW])
        Hflat = sb("Hbuf", [P, max(2 * NT * P, NT * P + 5120, NW + 1344)])
        Hbuf = Hflat[:, 0:2 * NT * P].rearrange("p (k n) -> p k n", k=2)
        scol = Hflat[:, 0:NW]
        work = sb("work", [P, 8192])
        srcI = sb("srcI", [P, ET + G], i32)
        dstF = sb("dstF", [P, ET])
        dl = sb("dl", [P, ET + G])
        base0 = sb("base0", [P, NG])
        baseF = sb("baseF", [P, NG])
        baseI = sb("baseI", [1, NG], i32)
        step = sb("step", [P, 1])
        sweeps = sb("sweeps", [1, 4], i32)
        idx = sb("idx", [P, 2, G], i32)
        wt = sb("wt", [P, 25, F])
        wext = sb("wext", [P, F + 2 * HEADS])
        cols = sb("cols", [P, 8])
        rows = sb("rows", [1, 3, F])
        ones = sb("ones", [P, P])
        ident = sb("ident", [P, P])
        small = sb("small", [P, 8])
        dwin = sb("dwin", [P, 2, DW], bf16)
        PS = [ctx.enter_context(nc.psum_tensor(f"ps{i}", [P, 2, 512], f32)) for i in range(4)]

        W_NAMES = (["l0x", "l0a"] + [f"c1{s}0{o}" for s in "lr" for o in range(2)]
                   + [f"c2{s}{i}{o}" for s in "lr" for i in range(2) for o in range(2)]
                   + [f"c3{s}{i}0" for s in "lr" for i in range(2)]
                   + ["m1n", "m1a", "m1b", "w2u", "u1h", "u2", "iota"])
        assert len(W_NAMES) <= 25

        def W(name):
            return wt[:, W_NAMES.index(name), :]

        iota = W("iota")
        B0, B1, B2, CU, UB2, EPSC = 0, 1, 3, 5, 6, 7

        g256 = work[:, 0:2 * G * 256].rearrange("p (s j f) -> p s j f", s=2, j=G)
        g128 = work[:, 0:2 * G * 128].rearrange("p (s j f) -> p s j f", s=2, j=G)
        g132 = work[:, 0:2 * G * TW].rearrange("p (s j f) -> p s j f", s=2, j=G)
        bufA = work[:, 2112:3136].rearrange("p (j f) -> p j f", j=G)
        winF = Hflat[:, NW + 1024:NW + 1024 + 2 * P].rearrange("p (k f) -> p k f", k=2)
        lg = work[:, 3264:3264 + 4 * G * HEADS].rearrange("p (k c) -> p k c", k=4)
        onehots = [work[:, o:o + 1024].rearrange("p (j f) -> p j f", j=G) for o in (4096, 6144)]
        bufB = work[:, 5120:6144].rearrange("p (j f) -> p j f", j=G)
        hotT = Hflat[:, NW:NW + 512].bitcast(bf16).rearrange("p (j f) -> p j f", j=G)
        hot16a = Hflat[:, NW + 512:NW + 1024].bitcast(bf16).rearrange("p (j f) -> p j f", j=G)
        ident16 = Hflat[:, NW + 1280:NW + 1344].bitcast(bf16)
        ea = work[:, 7168:8192].rearrange("p (s c) -> p s c", s=2)
        st = work[:, 0:2 * U * F].rearrange("p (a o f) -> p a o f", a=U, o=2)
        hn = work[:, 1792:1792 + U * F].rearrange("p (a f) -> p a f", a=U)
        hs = work[:, 2688:2688 + U * F].rearrange("p (a f) -> p a f", a=U)
        nm = work[:, 3584:3584 + U * 256].rearrange("p (a f) -> p a f", a=U)
        tmp = work[:, 5376:5376 + U * F].rearrange("p (a f) -> p a f", a=U)
        gamma = work[:, 7168:7168 + F]
        beta = work[:, 7168 + F:7168 + 2 * F]
        stats = work[:, 7424:7424 + NT * 6].rearrange("p (t c) -> p t c", c=6)
        ln = work[:, 7424 + NT * 6:7424 + NT * 11].rearrange("p (k t) -> p k t", k=5)

        def phase():
            s, mine = ExitStack(), []
            uid = phase.n
            phase.n += 1

            def sem(name):
                mine.append(nc.alloc_semaphore(f"{name}_{uid}"))
                return mine[-1]

            s.callback(nc.all_engine_barrier)
            s.callback(lambda: nc.clear_and_free_semaphores(mine))
            return s, sem
        phase.n = 0

        def prepare():
            s, sem = phase()
            with s:
                loaded, indices, filled, pads = sem("loaded"), sem("indices"), sem("filled"), sem("pads")
                steps, asfloat, turned, kept, made = (sem("vector_steps"), sem("asfloat"), sem("turned"), sem("kept"),
                                                      sem("made"))
                zeroed = sem("dst_table_zeroed")
                rawI = work[:, 0:2 * QB * P].bitcast(i32).rearrange("p (k q c) -> p k q c", k=2, q=QB)
                rawF = work[:, 1792:1792 + 2 * QB * P].rearrange("p (k q c) -> p k q c", k=2, q=QB)
                nat = work[:, 3584:3584 + 20 * F].rearrange("p (b f) -> p b f", f=F)
                w1g = work[:, 6144:6144 + F]
                u1c = work[:, 6272:6272 + F]
                u1b = work[:, 6400:6400 + F]
                w2t = work[:, 6528:6528 + F]
                ablk = work[:, 6656:6656 + 2 * HEADS]
                gcol = work[:, 6672:6673]
                mb2 = work[:, 6673:6674]
                zero4 = work[:, 6676:6676 + DW // 2].bitcast(bf16)
                ub1 = work[:, 6690:6691]
                natural = [(L0_gnn_W, 0, 0), (L0_gnn_W, 0, 1)]
                natural += [(w, o, 0) for w in (L1_gnn_W1l, L1_gnn_W1r) for o in range(2)]
                natural += [(w, o, i) for w in (L1_gnn_W2l, L1_gnn_W2r) for i in range(2) for o in range(2)]
                natural += [(w, 0, i) for w in (L1_gnn_W3l, L1_gnn_W3r) for i in range(2)]
                natural += [(L3_gnn_W, 0, 0), (L2_gnn_msg_w2, 0, 0)]
                NB, IL3, IMW2 = len(natural), len(natural) - 2, len(natural) - 1
                with nc.Block() as block:
                    @block.sync
                    def _(sp):
                        sp.wait_ge(filled, 1)
                        n = 0
                        for k, v in ((0, src), (1, dst)):
                            for q in range(QB):
                                r = min(P, EFULL - q * P)
                                if r > 0:
                                    sp.dma_start(rawI[0:r, k, q, :], v[q * P * P:(q * P + r) * P].rearrange(
                                        "(t p) -> t p", p=P)).then_inc(indices, 16)
                                    n += 1
                            if ETAIL:
                                q, r = EFULL // P, EFULL % P
                                sp.dma_start(rawI[r:r + 1, k, q, 0:ETAIL],
                                             v[EFULL * P:E].rearrange("(o c) -> o c", o=1)).then_inc(indices, 16)
                                n += 1
                        prepare.n_idx = n
                        m = 0
                        def load(o, i):
                            sp.dma_start(o, i).then_inc(loaded, 16)
                        for q in range(NACC):
                            sp.dma_start(T_PART[q].rearrange("(t p) f -> p t f", p=P),
                                         acc[:, 0, :].rearrange("p (t f) -> p t f", f=P)).then_inc(zeroed, 16)
                        for b, (w, r, c) in enumerate(natural):
                            load(nat[:, b, :], w[r * P:(r + 1) * P, c * P:(c + 1) * P])
                        load(X[:, 0:NFULL, :], x[0:NFULL * P, :].rearrange("(t p) f -> p t f", p=P))
                        if NTAIL:
                            load(X[0:NTAIL, NFULL, :], x[NFULL * P:N, :])
                        load(W("m1n"), L2_gnn_msg_w1[0:F, :])
                        load(W("m1a")[0:ED, :], L2_gnn_msg_w1[F:F + ED, :])
                        load(W("m1b")[ED:2 * ED, :], L2_gnn_msg_w1[F:F + ED, :])
                        load(w1g[0:GD, :], L2_gnn_msg_w1[F + ED:F + ED + GD, :])
                        load(W("u1h"), L2_gnn_upd_w1[0:F, :])
                        load(u1b, L2_gnn_upd_w1[F:2 * F, :])
                        load(u1c[0:GD, :], L2_gnn_upd_w1[2 * F:2 * F + GD, :])
                        load(W("u2"), L2_gnn_upd_w2)
                        for h in range(HEADS):
                            for k in range(2):
                                load(ablk[HF * h:HF * (h + 1), HEADS * k + h:HEADS * k + h + 1],
                                     L3_gnn_a[h, HF * k:HF * (k + 1)].rearrange("(f o) -> f o", o=1))
                        load(gcol[0:GD, :], L2_gnn_global_state.rearrange("(f o) -> f o", o=1))
                        load(mb2, L2_gnn_msg_b2.rearrange("(f o) -> f o", o=1))
                        load(cols[:, B0:B0 + 1], L0_gnn_b.rearrange("(f o) -> f o", o=1))
                        for o in range(2):
                            load(cols[:, B1 + o:B1 + o + 1], L1_gnn_b1[o * P:(o + 1) * P].rearrange("(f o) -> f o", o=1))
                            load(cols[:, B2 + o:B2 + o + 1], L1_gnn_b2[o * P:(o + 1) * P].rearrange("(f o) -> f o", o=1))
                        load(ub1, L2_gnn_upd_b1.rearrange("(f o) -> f o", o=1))
                        load(cols[:, UB2:UB2 + 1], L2_gnn_upd_b2.rearrange("(f o) -> f o", o=1))
                        load(rows[0:1, 0, :], L1_gnn_b3.rearrange("(o f) -> o f", o=1))
                        load(rows[0:1, 1, :], L2_gnn_msg_b1.rearrange("(o f) -> o f", o=1))
                        sp.dma_start(T_L0[NT * P:NT * P + P, :], acc[:, 0, 0:F]).then_inc(zeroed, 16)
                        for t in range(NT + 1):
                            if t >= NFULL:
                                sp.dma_start(T_DST[t * P:(t + 1) * P, :], zero4).then_inc(zeroed, 16)
                        sp.wait_ge(zeroed, 16 * (NT + 1 - NFULL + NACC + 1))

                    n_idx = 2 * sum(min(P, EFULL - q * P) > 0 for q in range(QB)) + 2 * (ETAIL > 0)
                    n_load = (NB + 1 + (NTAIL > 0) + 8 + 2 * HEADS + 2 + 1 + 4 + 2 + 2)

                    @block.gpsimd
                    def _(pool):
                        pool.iota(iota, [[1, P]], base=0, channel_multiplier=0,
                                  allow_small_or_imprecise_dtypes=True).then_inc(pads, 1)
                        pool.iota(small[:, 0:1], [[0, 1]], base=0, channel_multiplier=1,
                                  allow_small_or_imprecise_dtypes=True).then_inc(pads, 1)

                    @block.vector
                    def _(dve):
                        link = Steps(dve, steps)
                        dve.memset(rawI[:, 0, :, :], 0)
                        dve.memset(rawI[:, 1, :, :], -4096)
                        dve.memset(acc[:, 0, :], 0.0)
                        dve.memset(srcI[:, ET:ET + G], 0)
                        dve.memset(dl[:, ET:ET + G], FAR)
                        dve.memset(X[:, NFULL:NT, :], 0.0)
                        dve.memset(W("m1a"), 0.0)
                        dve.memset(W("m1b"), 0.0)
                        dve.memset(ablk, 0.0)
                        dve.memset(zero4, 0.0)
                        dve.memset(ones[:, :], 1.0)
                        dve.memset(cols[:, EPSC:EPSC + 1], LN_EPS)
                        link(dve.memset(rows[:, :, :], 0.0))
                        dve.sem_inc(filled)
                        dve.wait_ge(pads, 2)
                        link(dve.tensor_scalar(ident[:, :], iota, small[:, 0:1], None, ALU.is_equal))
                        dve.wait_ge(indices, 16 * n_idx)
                        dve.tensor_copy(rawF[:, :, :, :], rawI[:, :, :, :]).then_inc(asfloat, 1)
                        blocks = [(k, q) for k in range(2) for q in range(QB)]
                        for b, (k, q) in enumerate(blocks):
                            dve.wait_ge(turned, b + 1)
                            c = min(P, ET - q * P)
                            to = (srcI if k == 0 else dstF)[:, q * P:q * P + c]
                            dve.tensor_copy(to, PS[b % 2][:, 0, 0:c]).then_inc(kept, 1)
                        for b in range(NB):
                            dve.wait_ge(turned, len(blocks) + b + 1)
                            to = wext[:, 0:F] if b == IL3 else w2t if b == IMW2 else wt[:, b, :]
                            dve.tensor_copy(to, PS[(len(blocks) + b) % 2][:, 0, 0:P]).then_inc(kept, 1)
                        dve.wait_ge(made, 5)
                        dve.tensor_copy(wext[:, F:F + 2 * HEADS], PS[2][:, 0, 0:2 * HEADS])
                        dve.tensor_tensor(rows[0:1, 1, :], rows[0:1, 1, :], PS[2][0:1, 1, 0:F], ALU.add)
                        dve.tensor_copy(rows[0:1, 2, :], PS[3][0:1, 0, 0:F])
                        dve.tensor_tensor(cols[:, CU:CU + 1], ub1, PS[3][:, 1, 0:1], ALU.add)
                        dve.wait_ge(made, 6)
                        dve.tensor_copy(W("w2u"), PS[0][:, 1, 0:F])
                        first = dstF[:, :].rearrange("p (g j) -> p g j", j=G)[0:1, :, 0]
                        link(dve.tensor_copy(base0[0:1, :], first))
                        dve.sem_inc(filled)
                        dve.wait_ge(made, 7)
                        link(dve.tensor_copy(base0[:, :], PS[1][:, 1, 0:NG]))
                        d3, b3 = (v.rearrange("p (g j) -> p g j", j=G) for v in (dl[:, 0:ET], dstF[:, :]))
                        link(dve.tensor_tensor(d3, b3, base0[:, :].unsqueeze(2).to_broadcast([P, NG, G]), ALU.subtract))
                        inw = rawF[:, :, :, :].rearrange("p k q c -> p (k q c)")[:, 0:ET]
                        link(dve.tensor_scalar(inw, dl[:, 0:ET], 0.0, None, ALU.is_ge))
                        link(dve.scalar_tensor_tensor(out=inw, in0=dl[:, 0:ET], scalar=float(P - 1), in1=inw,
                                                      op0=ALU.is_le, op1=ALU.mult))
                        if ETAIL:
                            link(dve.tensor_scalar(small[:, 1:2], small[:, 0:1], float(ETAIL), None, ALU.is_ge))
                            link(dve.tensor_tensor(inw[:, EFULL:EFULL + 1], inw[:, EFULL:EFULL + 1], small[:, 1:2], ALU.max))
                        link(dve.tensor_reduce(small[:, 2:3], inw[:, 0:EFULL + (ETAIL > 0)], AX.X, ALU.min))
                        dve.sem_inc(filled)
                        dve.wait_ge(made, 8)
                        link(dve.tensor_reduce(small[0:1, 3:4], PS[2][0:1, 0, 0:P], AX.X, ALU.min))
                        dve.sem_inc(filled)
                        link(dve.tensor_scalar(small[0:1, 4:5], small[0:1, 3:4], float(1 - NT), float(NT), ALU.mult, ALU.add))
                        link(dve.tensor_copy(sweeps[0:1, 0:1], small[0:1, 4:5]))
                        dve.wait_ge(made, 9)
                        link(dve.tensor_copy(small[:, 5:6], PS[3][:, 0, 0:1]))
                        link(dve.tensor_scalar(step[:, :], small[:, 5:6], float(-P), float(P), ALU.mult, ALU.add))
                        link(dve.tensor_scalar(base0[:, :], base0[:, :], small[:, 5:6], None, ALU.mult))
                        for t in range(NT):
                            last = dve.bn_stats(stats[:, t, :], X[:, t, :])
                        link(last)

                    @block.tensor
                    def _(pe):
                        blocks = [(k, q) for k in range(2) for q in range(QB)]
                        pe.wait_ge(asfloat, 1)
                        pe.wait_ge(steps, 2)
                        for b, (k, q) in enumerate(blocks):
                            if b >= 2:
                                pe.wait_ge(kept, b - 1)
                            pe.transpose(PS[b % 2][:, 0, 0:P], rawF[:, k, q, :], ident[:, :]).then_inc(turned, 1)
                        pe.wait_ge(loaded, 16 * n_load)
                        for b in range(NB):
                            pe.wait_ge(kept, len(blocks) + b - 1)
                            pe.transpose(PS[(len(blocks) + b) % 2][:, 0, 0:P], nat[:, b, :], ident[:, :]).then_inc(turned, 1)
                        pe.matmul(PS[2][:, 0, 0:2 * HEADS], nat[:, IL3, :], ablk, start=True, stop=True).then_inc(made, 1)
                        pe.matmul(PS[2][0:1, 1, 0:F], gcol[0:GD, :], w1g[0:GD, :], start=True, stop=True).then_inc(made, 1)
                        pe.matmul(PS[3][0:1, 0, 0:F], mb2, u1b, start=True, stop=True).then_inc(made, 1)
                        pe.matmul(PS[3][:, 1, 0:1], u1c[0:GD, :], gcol[0:GD, :], start=True, stop=True).then_inc(made, 1)
                        pe.wait_ge(kept, len(blocks) + NB)
                        pe.sem_inc(made)
                        pe.matmul(PS[0][:, 1, 0:F], w2t, u1b, start=True, stop=True).then_inc(made, 1)
                        pe.wait_ge(filled, 2)
                        pe.matmul(PS[1][:, 1, 0:NG], ones[0:1, :], base0[0:1, :], start=True, stop=True).then_inc(made, 1)
                        pe.wait_ge(filled, 3)
                        pe.transpose(PS[2][0:1, 0, 0:P], small[:, 2:3], ident[:, :]).then_inc(made, 1)
                        pe.wait_ge(filled, 4)
                        pe.matmul(PS[3][:, 0, 0:1], ones[0:1, :], small[0:1, 3:4], start=True, stop=True).then_inc(made, 1)

        def reverse_edges():
            s, sem = phase()
            with s:
                base_ready, used, hot, gate, steps, added = (sem("base_ready"), sem("groups_used"), sem("onehot_ready"),
                                                             sem("gate"), sem("vector_steps"), sem("added"))
                window = [sem(f"window_rows{k}") for k in range(2)]
                base_read = sem("base_read")
                scattered = [sem(f"scattered{q}") for q in range(NACC)]
                spread, same_ready, mixed, copied, summed, out_ready, idx_ready, taken, start = (
                    sem("sources_spread"), sem("same_ready"), sem("mixed"), sem("mixed_copied"), sem("summed"),
                    sem("rows_ready"), sem("idx_ready"), sem("rows_scattered"), sem("degrees"))
                spare = Hflat[:, NT * P:NT * P + 5120]
                hwin = work[:, 0:2 * F].rearrange("p (k f) -> p k f", k=2)
                rows_out = spare[:, 0:2048].rearrange("p (k j f) -> p k j f", k=2, j=G)
                diag = spare[:, 2048:4096].rearrange("p (k j f) -> p k j f", k=2, j=G)
                mixT = spare[:, 4096:5120].rearrange("p (j f) -> p j f", j=G)
                hot16 = work[:, 4096:5120].bitcast(bf16).rearrange("p (k j f) -> p k j f", k=2, j=G)
                same = work[:, 2304:2816].bitcast(bf16).rearrange("p (j f) -> p j f", j=G)
                lower = work[:, 2816:3328].bitcast(bf16).rearrange("p (j f) -> p j f", j=G)
                below = work[:, 3392:3392 + P // 2].bitcast(bf16)
                lead = work[:, 3328:3328 + 2 * G].rearrange("p (k j) -> p k j", k=2)
                ones16 = work[:, 5120:5120 + P // 2].bitcast(bf16)
                trash = work[:, 3584:3585]

                def halves_of(v):
                    return v.rearrange("p (q j) f -> p q (j f)", q=2)

                with nc.Block() as block:
                    @block.gpsimd
                    def _(pool):
                        pool.iota(small[:, 0:1], [[0, 1]], base=0, channel_multiplier=1,
                                  allow_small_or_imprecise_dtypes=True).then_inc(start, 1)
                        count = pool.value_load(sweeps[0:1, 0:1], min_val=1, max_val=NT)
                        pool.wait_ge(base_ready, 1)
                        for q in range(NACC):
                            pool.indirect_dma_start(T_PART[q], bass.IndirectOffsetOnAxis(ap=idx[:, 1, q:q + 1], axis=0),
                                                    rows_out[:, 1, q, :], None, compute_op=ALU.add).then_inc(scattered[q], 16)
                        pool.sem_inc(taken)
                        with pool.Fori(0, count) as sw:
                            with pool.Fori(0, PAIRS) as i:
                                for k in range(2):
                                    n = sw * NG + 2 * i + k
                                    pool.wait_ge(idx_ready, n + 1)
                                    for j in range(G):
                                        q = j % NACC
                                        if j % 4 == 0:
                                            pool.wait_ge(out_ready, 2 * n + j // 4 + 1)
                                        pool.wait_ge(scattered[q], 32 * n + 16 * (j // NACC) + 16)
                                        pool.sem_inc(gate)
                                        pool.indirect_dma_start(
                                            T_PART[q], bass.IndirectOffsetOnAxis(ap=idx[:, k, j:j + 1], axis=0),
                                            rows_out[:, k, j, :], None, compute_op=ALU.add).then_inc(scattered[q], 16)
                                        if j == NACC - 1:
                                            pool.wait_ge(scattered[q], 32 * n + 16)
                                            pool.sem_inc(taken)
                        for q in range(NACC):
                            pool.wait_ge(scattered[q], count * (32 * NG) + 16)

                    @block.sync
                    def _(sp):
                        count = sp.value_load(sweeps[0:1, 0:1], min_val=1, max_val=NT)
                        sp.sem_inc(base_read)
                        with sp.Fori(0, count) as sw:
                            sp.wait_ge(base_ready, sw + 1)
                            sp.sem_inc(gate)
                            with sp.Fori(0, PAIRS) as i:
                                for k in range(2):
                                    n = sw * NG + 2 * i + k
                                    at = sp.value_load(baseI[0:1, bass.ds(2 * i + k, 1)], min_val=0, max_val=NW - P)
                                    sp.wait_ge(used, n + 1)
                                    sp.dma_start(hwin[:, k, :], T_L0[bass.ds(at, P), :]).then_inc(window[k], 16)
                            sp.sem_inc(base_read)

                    @block.tensor
                    def _(pe):
                        count = pe.value_load(sweeps[0:1, 0:1], min_val=1, max_val=NT)
                        pe.sem_inc(used, 2)
                        with pe.Fori(0, count) as sw:
                            with pe.Fori(0, PAIRS) as i:
                                for k in range(2):
                                    n = sw * NG + 2 * i + k
                                    pe.wait_ge(hot, n + sw + 1)
                                    for j in range(G):
                                        pe.matmul(PS[1][:, j // 4, (j % 4) * P:(j % 4 + 1) * P], ones[:, :],
                                                  diag[:, k, j, :], start=True, stop=True)
                                    for j in range(G):
                                        last = pe.matmul(PS[0][:, k, 0:P], ones16, hot16[:, k, j, :],
                                                         start=j == 0, stop=j == G - 1)
                                    last.then_inc(spread, 1)
                                    pe.wait_ge(same_ready, n + 1)
                                    for j in range(G):
                                        last = pe.matmul(PS[2][:, j // 4, (j % 4) * P:(j % 4 + 1) * P], hot16[:, k, j, :],
                                                         same[:, j, :], start=True, stop=True)
                                        if j % 4 == 3:
                                            last.then_inc(mixed, 1)
                                    pe.wait_ge(window[k], 16 * (sw * PAIRS + i + 1))
                                    for j in range(G):
                                        if j % 4 == 0:
                                            pe.wait_ge(copied, 2 * n + j // 4 + 1)
                                        last = pe.matmul(PS[3][:, j // 4, (j % 4) * P:(j % 4 + 1) * P], mixT[:, j, :],
                                                         hwin[:, k, :], start=True, stop=True)
                                        if j % 4 == 3:
                                            last.then_inc(summed, 1)
                                    pe.wait_ge(summed, 2 * n + 2)
                                    pe.sem_inc(used)

                    @block.scalar
                    def _(act):
                        count = act.value_load(sweeps[0:1, 0:1], min_val=1, max_val=NT)
                        with act.Fori(0, count) as sw:
                            with act.Fori(0, PAIRS) as i:
                                for k in range(2):
                                    n = sw * NG + 2 * i + k
                                    for q in range(2):
                                        act.wait_ge(mixed, 2 * n + q + 1)
                                        act.copy(halves_of(mixT)[:, q, :], PS[2][:, q, :]).then_inc(copied, 1)
                                    act.wait_ge(taken, n + 1)
                                    for q in range(2):
                                        act.wait_ge(summed, 2 * n + q + 1)
                                        act.copy(halves_of(rows_out[:, k])[:, q, :], PS[3][:, q, :]).then_inc(out_ready, 1)

                    @block.vector
                    def _(dve):
                        link = Steps(dve, steps)
                        dve.memset(acc[:, 1, :], 0.0)
                        dve.memset(rows_out[:, 1, :, :], 0.0)
                        dve.memset(ones16, 1.0)
                        dve.wait_ge(start, 1)
                        dve.tensor_scalar(below, iota, small[:, 0:1], None, ALU.is_lt)
                        link(dve.tensor_scalar(trash, small[:, 0:1], float(NT * P), None, ALU.add))
                        dve.tensor_copy(idx[:, 1, :], trash.to_broadcast([P, G]))
                        link(dve.tensor_copy(baseF[:, :], base0[:, :]))
                        count = dve.value_load(sweeps[0:1, 0:1], min_val=1, max_val=NT)
                        at = dve.alloc_register("degree_window")
                        SPS, SPG = 5, 8
                        full = [P, G, P]

                        def one_hot(g, k):
                            link(dve.tensor_tensor(hot16[:, k], iota.unsqueeze(1).to_broadcast(full),
                                                   dl[:, bass.ds(g * G, G)].unsqueeze(2).to_broadcast(full), ALU.is_equal))
                            link(dve.tensor_tensor(diag[:, k], ident[:, :].unsqueeze(1).to_broadcast(full),
                                                   srcI[:, bass.ds(g * G, G)].unsqueeze(2).to_broadcast(full), ALU.mult))
                            dve.sem_inc(hot)

                        with dve.Fori(0, count) as sw:
                            link.at(2 + sw * (SPS + NG * SPG))
                            dve.wait_ge(base_read, sw + 1)
                            d3, s3 = (v.rearrange("p (g j) -> p g j", j=G) for v in (dl[:, 0:ET], dstF[:, :]))
                            link(dve.tensor_copy(baseI[0:1, :], baseF[0:1, :]))
                            link(dve.tensor_tensor(d3, s3, baseF[:, :].unsqueeze(2).to_broadcast([P, NG, G]), ALU.subtract))
                            link(dve.tensor_tensor(baseF[:, :], baseF[:, :], step[:, :].to_broadcast([P, NG]), ALU.add))
                            dve.sem_inc(base_ready)
                            dve.wait_ge(used, sw * NG + 1)
                            one_hot(0, 0)
                            with dve.Fori(0, PAIRS) as i:
                                for k in range(2):
                                    gi = 2 * i + k
                                    n = sw * NG + gi
                                    link.at(2 + SPS + sw * SPS + n * SPG)
                                    source = srcI[:, bass.ds(gi * G, G)]
                                    dve.load(at, baseI[0:1, bass.ds(gi, 1)])
                                    win = dve.snap(at, min_val=0, max_val=NW - P)
                                    dve.wait_ge(spread, n + 1)
                                    link(dve.tensor_tensor(same, PS[1][:, :, :].rearrange("p q (j f) -> p (q j) f", f=P),
                                                           source.unsqueeze(2).to_broadcast(full), ALU.is_equal))
                                    dve.sem_inc(same_ready)
                                    dve.wait_ge(used, n + 2)
                                    one_hot(gi + 1, 1 - k)
                                    link(dve.tensor_tensor(lower, same, below.unsqueeze(1).to_broadcast(full), ALU.mult))
                                    link(dve.tensor_reduce(lead[:, 0, :], lower, AX.X, ALU.max))
                                    link(dve.tensor_tensor(lead[:, 1, :], trash.to_broadcast([P, G]), source, ALU.subtract))
                                    link(dve.tensor_tensor(lead[:, 1, :], lead[:, 1, :], lead[:, 0, :], ALU.mult))
                                    dve.wait_ge(taken, n + 1)
                                    dve.tensor_tensor(idx[:, k, :], lead[:, 1, :], source, ALU.add).then_inc(idx_ready, 1)
                                    link(dve.tensor_tensor(acc[:, 1, bass.ds(win, P)], acc[:, 1, bass.ds(win, P)],
                                                           PS[0][:, k, 0:P], ALU.add))
                                    dve.sem_inc(gate)
                                    assert link.k == SPG
                        dve.tensor_scalar(rcnt[:, :], acc[:, 1, :], 1.0, None, ALU.max).then_inc(start, 1)
                        dve.wait_ge(start, 2)
                        dve.reciprocal(rcnt[:, :], rcnt[:, :]).then_inc(start, 1)
                        dve.wait_ge(start, 3)
                        dve.scalar_tensor_tensor(out=rcnt[:, :], in0=acc[:, 1, :], scalar=0.5, in1=rcnt[:, :],
                                                 op0=ALU.is_ge, op1=ALU.mult)

        def edges(kind, table):
            s, sem = phase()
            halves = 1 if kind in ("sum", "message") else 2
            gbuf = {"wide": g256, "attention": g132}.get(kind, g128)
            with s:
                base_ready, idx_ready, used, hot = sem("base_ready"), sem("idx_ready"), sem("groups_used"), sem("onehot_ready")
                gathered = [sem(f"gathered{k}") for k in range(2)]
                side = [sem(f"side_loaded{k}") for k in range(2)]
                gate, steps, added, summed = sem("gate"), sem("vector_steps"), sem("added"), sem("summed")
                turned, copied, hidden, relu_done, start = (sem("turned"), sem("copied"), sem("hidden"), sem("relu_done"),
                                                            sem("start"))
                read, base_read, rows_read, summed32 = sem("dst_logits_read"), sem("base_read"), sem("rows_read"), sem("hidden_with_rows")
                logit, colmax, topped, spread, shift, weighted, scaled, wide_w, wsteps = (
                    sem("dst_logits"), sem("colmax"), sem("topped"), sem("spread"), sem("shift"), sem("weights_ready"),
                    sem("scaled"), sem("weights_spread"), sem("rescale_ready"))
                turn16 = PS[2][:, 0, :].bitcast(bf16).rearrange("p (j f) -> p j f", j=G)
                pen = rcnt
                Gw = bufB

                with nc.Block() as block:
                    @block.gpsimd
                    def _(pool):
                        count = pool.value_load(sweeps[0:1, 0:1], min_val=1, max_val=NT)
                        with pool.Fori(0, count) as sw:
                            if kind == "attention":
                                pool.wait_ge(rows_read, sw * NG + 1)
                            elif kind == "message":
                                pool.wait_ge(summed32, sw * (2 * NG) + 1)
                            else:
                                pool.wait_ge(used, sw * NG + 2)
                            pool.sem_inc(gate)
                            pool.tensor_copy(idx[:, 0, :], srcI[:, 0:G]).then_inc(idx_ready, 1)
                            with pool.Fori(0, PAIRS) as i:
                                for k in range(2):
                                    n = sw * NG + 2 * i + k
                                    pool.wait_ge(idx_ready, n + sw + 1)
                                    pool.sem_inc(gate)
                                    for j in range(G):
                                        pool.indirect_dma_start(
                                            gbuf[:, k, j, :], None, table,
                                            bass.IndirectOffsetOnAxis(ap=idx[:, k, j:j + 1], axis=0)
                                        ).then_inc(gathered[k], 16)
                                    if kind == "attention":
                                        pool.wait_ge(rows_read, n + 1)
                                    elif kind == "message":
                                        pool.wait_ge(summed32, 2 * n + 1)
                                    else:
                                        pool.wait_ge(used, n + 2)
                                    pool.sem_inc(gate)
                                    pool.tensor_copy(idx[:, 1 - k, :], srcI[:, bass.ds((2 * i + k + 1) * G, G)]
                                                     ).then_inc(idx_ready, 1)
                            pool.wait_ge(idx_ready, (sw + 1) * (NG + 1))
                            pool.sem_inc(gate)

                    @block.sync
                    def _(sp):
                        if kind == "message":
                            eat = edge_attr_64[0:EFULL * P, :].rearrange("(t p) c -> p t c", p=P)
                            count = sp.value_load(sweeps[0:1, 0:1], min_val=1, max_val=NT)
                            def load(n, t, k, tiles, tail):
                                sp.wait_ge(used, n + 1)
                                to = ea[:, k, :].rearrange("p (j c) -> p j c", c=ED)
                                if tiles:
                                    sp.dma_start(to[:, 0:tiles, :], eat[:, bass.ds(t, tiles), :]).then_inc(side[k], 16)
                                else:
                                    sp.sem_inc(side[k], 16)
                                if tail:
                                    sp.dma_start(to[0:ETAIL, tiles, :], edge_attr_64[EFULL * P:E, :]).then_inc(side[k], 16)
                                else:
                                    sp.sem_inc(side[k], 16)
                            with sp.Fori(0, count) as sw:
                                with sp.Fori(0, PAIRS - 1) as i:
                                    for k in range(2):
                                        load(sw * NG + 2 * i + k, (2 * i + k) * G, k, G, False)
                                for k in range(2):
                                    t = (NG - 2 + k) * G
                                    tiles = min(G, max(0, EFULL - t))
                                    load(sw * NG + NG - 2 + k, t, k, tiles, bool(ETAIL) and tiles < G and t + tiles == EFULL)
                                sp.wait_ge(used, sw * NG + NG + 1)
                                sp.sem_inc(side[0], 32)
                                sp.wait_ge(used, sw * NG + NG + 2)
                                sp.sem_inc(gate)
                        if kind == "attention":
                            count = sp.value_load(sweeps[0:1, 0:1], min_val=1, max_val=NT)
                            sp.sem_inc(base_read)
                            with sp.Fori(0, count) as sw:
                                sp.wait_ge(base_ready, sw + 1)
                                sp.sem_inc(gate)
                                with sp.Fori(0, PAIRS) as i:
                                    for k in range(2):
                                        n = sw * (NG + 1) + 2 * i + k
                                        at = sp.value_load(baseI[0:1, bass.ds(2 * i + k, 1)], min_val=0, max_val=NW - P)
                                        sp.wait_ge(read, n + 1)
                                        sp.dma_start(dwin[:, k, :], T_DST[bass.ds(at, P), :]).then_inc(side[k], 16)
                                sp.wait_ge(read, sw * (NG + 1) + NG + 1)
                                sp.dma_start(dwin[:, 0, :], T_DST[0:P, :]).then_inc(side[0], 16)
                                sp.sem_inc(base_read)
                                sp.wait_ge(read, (sw + 1) * (NG + 1) + 2)
                                sp.sem_inc(gate)

                    def turn_copy(act, n):
                        act.wait_ge(turned, n + 1)
                        if kind == "message":
                            act.copy(bufB[:, 0:4, :], PS[1][:, 0, :].rearrange("p (j f) -> p j f", j=4)).then_inc(copied, 1)
                        else:
                            act.copy(hotT, turn16).then_inc(copied, 1)

                    @block.scalar
                    def _(act):
                        if kind in ("message", "attention"):
                            count = act.value_load(sweeps[0:1, 0:1], min_val=1, max_val=NT)
                            with act.Fori(0, count) as sw:
                                turn_copy(act, sw * (NG + 1))
                                with act.Fori(0, PAIRS) as i:
                                    for k in range(2):
                                        n = sw * NG + 2 * i + k
                                        if kind == "message":
                                            turn_copy(act, n + sw + 1)
                                            for q in range(2):
                                                act.wait_ge(summed32, 2 * n + q + 2)
                                                act.activation(bufA[:, 4 * q:4 * q + 4, :], bufA[:, 4 * q:4 * q + 4, :],
                                                               ACT.Relu).then_inc(relu_done, 1)
                                        else:
                                            act.wait_ge(shift, n + 1)
                                            act.wait_ge(used, n + 1)
                                            act.activation(lg[:, 2 + k, :], lg[:, 0, :], ACT.Exp).then_inc(weighted, 1)
                                            act.activation(winF[:, k, :], winF[:, k, :], ACT.Exp).then_inc(scaled, 1)
                                            turn_copy(act, n + sw + 1)

                    def dst_logits(pe, n, k, m):
                        pe.wait_ge(hot, n + 1)
                        for j in range(G):
                            last = pe.transpose(turn16[:, j, :], hot16a[:, j, :], ident16)
                        last.then_inc(turned, 1)
                        pe.wait_ge(side[k], 16 * (m + 1))
                        pe.wait_ge(copied, n + 1)
                        for j in range(G):
                            last = pe.matmul(PS[1][:, 0, DW * j:DW * (j + 1)], hotT[:, j, :],
                                             dwin[:, k, :], start=True, stop=True)
                        last.then_inc(logit, 1)
                        pe.wait_ge(logit, n + 1)
                        pe.sem_inc(read)

                    def turn_features(pe, n, k, m):
                        pe.wait_ge(side[k], 32 * (m + 1))
                        pe.wait_ge(copied, n + 1)
                        for q in range(4):
                            last = pe.transpose(PS[1][:, 0, q * P:(q + 1) * P], ea[:, k, q * P:(q + 1) * P], ident[:, :])
                        last.then_inc(turned, 1)

                    def denominators(pe, n, k):
                        for j in range(G):
                            last = pe.matmul(PS[3 * k][0:HEADS, 1, 0:P], lg[:, 2 + k, HEADS * j:HEADS * (j + 1)],
                                             onehots[k][:, j, :], start=j == 0, stop=j == G - 1)
                        last.then_inc(used, 1)

                    @block.tensor
                    def _(pe):
                        count = pe.value_load(sweeps[0:1, 0:1], min_val=1, max_val=NT)
                        pe.sem_inc(read, 2)
                        pe.sem_inc(used, 1 if kind == "attention" else 2)
                        if kind == "message":
                            pe.sem_inc(copied)
                        with pe.Fori(0, count) as sw:
                            if kind == "attention":
                                dst_logits(pe, sw * (NG + 1), 0, sw * (PAIRS + 1))
                            if kind == "message":
                                turn_features(pe, sw * (NG + 1), 0, sw * (PAIRS + 1))
                            with pe.Fori(0, PAIRS) as i:
                                for k in range(2):
                                    n = sw * NG + 2 * i + k
                                    m = sw * PAIRS + i
                                    ahead = (n + sw + 1, 1 - k, sw * (PAIRS + k) + i + k)
                                    A, B = PS[3 * k][:, 0, 0:P], PS[3 * k][:, 1, 0:P]
                                    onehot = onehots[k]
                                    if kind == "attention":
                                        pe.wait_ge(colmax, n + 1)
                                        pe.transpose(PS[1][0:1, 1, 0:P], small[:, 0:1], ident[:, :]).then_inc(topped, 1)
                                        pe.wait_ge(spread, n + 1)
                                        pe.matmul(PS[1][:, 1, P:P + 1], ones[0:1, :], small[0:1, 1:2],
                                                  start=True, stop=True).then_inc(wsteps, 1)
                                        denominators(pe, n - 1, 1 - k)
                                        dst_logits(pe, *ahead)
                                        pe.wait_ge(summed, n + 1)
                                        pe.wait_ge(added, n + 1)
                                        for j in range(G):
                                            pe.matmul(A, Gw[:, j, :], onehot[:, j, :], start=j == 0, stop=j == G - 1)
                                        continue
                                    pe.wait_ge(hot, n + sw + 1)
                                    if kind != "message":
                                        pe.wait_ge(gathered[k], (G * 16) * (m + 1))
                                    lhs = gbuf[:, k]
                                    if kind == "message":
                                        pe.wait_ge(copied, n + sw + 2)
                                        for j in range(G):
                                            last = pe.matmul(PS[2][:, j // 4, (j % 4) * P:(j % 4 + 1) * P], bufB[:, j // 2, :],
                                                             W("m1b" if j % 2 else "m1a"), start=True, stop=True)
                                            if j % 4 == 3:
                                                last.then_inc(hidden, 1)
                                        pe.wait_ge(hidden, 2 * n + 2)
                                        turn_features(pe, *ahead)
                                        lhs = bufA
                                    pe.wait_ge(added, n + 1)
                                    for j in range(G):
                                        if kind == "message" and j % 4 == 0:
                                            pe.wait_ge(relu_done, 2 * n + j // 4 + 1)
                                        last = pe.matmul(A, lhs[:, j, 0:P], onehot[:, j, :], start=j == 0, stop=j == G - 1)
                                        if halves == 2:
                                            last = pe.matmul(B, gbuf[:, k, j, P:2 * P], onehot[:, j, :],
                                                             start=j == 0, stop=j == G - 1)
                                    last.then_inc(used, 1)
                        if kind == "attention":
                            pe.wait_ge(summed, count * NG)
                            denominators(pe, None, 1)

                    @block.vector
                    def _(dve):
                        link = Steps(dve, steps)
                        late = kind == "attention"
                        dve.memset(acc[:, 0:halves, :], 0.0)
                        if late:
                            dve.memset(scol, FAR)
                            dve.memset(small[:, 2:3], FAR)
                            dve.memset(PS[3][:, :, 0:P], 0.0)
                            dve.memset(PS[0][:, 1, 0:P], 0.0)
                            dve.memset(winF[:, 1, :], 1.0)
                            dve.memset(lg[:, 3, :], 0.0)
                            dve.memset(onehots[1], 0.0)
                            dve.tensor_copy(ident16, ident[:, :])
                        link(dve.tensor_copy(baseF[:, :], base0[:, :]))
                        dve.sem_inc(added, 1 if late else 2)
                        dve.sem_inc(rows_read)
                        dve.sem_inc(summed32)
                        count = dve.value_load(sweeps[0:1, 0:1], min_val=1, max_val=NT)
                        at = dve.alloc_register(f"window_{phase.n}")
                        before = dve.alloc_register(f"window_before_{phase.n}")
                        dve.reg_mov(at, 0)
                        SPS = 3 + (3 if late else 0)
                        SPG = 10 if late else 1
                        with dve.Fori(0, count) as sw:
                            link.at(1 + sw * (SPS + NG * SPG))
                            if late:
                                dve.wait_ge(base_read, sw + 1)
                            d3, s3 = (v.rearrange("p (g j) -> p g j", j=G) for v in (dl[:, 0:ET], dstF[:, :]))
                            link(dve.tensor_copy(baseI[0:1, :], baseF[0:1, :]))
                            link(dve.tensor_tensor(d3, s3, baseF[:, :].unsqueeze(2).to_broadcast([P, NG, G]), ALU.subtract))
                            if late:
                                link(dve.tensor_scalar(pen[:, 0:ET], dl[:, 0:ET], 0.0, None, ALU.is_ge))
                                link(dve.scalar_tensor_tensor(out=pen[:, 0:ET], in0=dl[:, 0:ET], scalar=float(P - 1),
                                                              in1=pen[:, 0:ET], op0=ALU.is_le, op1=ALU.mult))
                                link(dve.tensor_scalar(pen[:, 0:ET], pen[:, 0:ET], -FAR, FAR, ALU.mult, ALU.add))
                            link(dve.tensor_tensor(baseF[:, :], baseF[:, :], step[:, :].to_broadcast([P, NG]), ALU.add))
                            dve.sem_inc(base_ready)

                            def one_hot(g, to):
                                return dve.tensor_tensor(to, iota.unsqueeze(1).to_broadcast([P, G, P]),
                                                  dl[:, bass.ds(g * G, G)].unsqueeze(2).to_broadcast([P, G, P]),
                                                  ALU.is_equal)

                            if late:
                                dve.wait_ge(read, sw * (NG + 1) + 2)
                            else:
                                dve.wait_ge(used, sw * NG + 1)
                            one_hot(0, hot16a if late else onehots[0]).then_inc(hot, 1)
                            with dve.Fori(0, PAIRS) as i:
                                for k in range(2):
                                    n = sw * NG + 2 * i + k
                                    link.at(1 + SPS + sw * SPS + n * SPG)
                                    gi = 2 * i + k
                                    if late:
                                        dve.reg_mov(before, at)
                                        last_win = dve.snap(before, min_val=0, max_val=NW - P)
                                    dve.load(at, baseI[0:1, bass.ds(gi, 1)])
                                    win = dve.snap(at, min_val=0, max_val=NW - P)
                                    if late:
                                        L = lg[:, 0, :].rearrange("p (j h) -> p j h", h=HEADS)
                                        dve.wait_ge(gathered[k], (G * 16) * (sw * PAIRS + i + 1))
                                        dve.wait_ge(logit, n + sw + 1)
                                        D = PS[1][:, 0, 0:G * DW].rearrange("p (j q h) -> p j h q", q=3, h=HEADS)
                                        L2 = lg[:, 1, :].rearrange("p (j h) -> p j h", h=HEADS)
                                        link(dve.tensor_reduce(L2, D, AX.X, ALU.add))
                                        link(dve.tensor_tensor(L, gbuf[:, k, :, F:TW], L2, ALU.add))
                                        link(dve.scalar_tensor_tensor(out=lg[:, 1, :], in0=lg[:, 0, :], scalar=SLOPE,
                                                                      in1=lg[:, 0, :], op0=ALU.mult, op1=ALU.max))
                                        link(dve.tensor_tensor(
                                            L, L2, pen[:, bass.ds(gi * G, G)].unsqueeze(2).to_broadcast([P, G, HEADS]), ALU.add))
                                        link(dve.tensor_reduce(small[:, 3:4], lg[:, 0, :], AX.X, ALU.max))
                                        dve.tensor_tensor(small[:, 0:1], small[:, 3:4], small[:, 2:3], ALU.max).then_inc(colmax, 1)
                                        one_hot(gi + 1, hot16a).then_inc(hot, 1)
                                        dve.wait_ge(topped, n + 1)
                                        dve.tensor_reduce(small[0:1, 1:2], PS[1][0:1, 1, 0:P], AX.X, ALU.max).then_inc(spread, 1)
                                        dve.wait_ge(wsteps, n + 1)
                                        link(dve.tensor_copy(small[:, 2:3], PS[1][:, 1, P:P + 1]))
                                        dve.tensor_scalar(lg[:, 0, :], lg[:, 0, :], small[:, 2:3], None, ALU.subtract)
                                        dve.tensor_scalar(winF[:, k, :], scol[:, bass.ds(win, P)], small[:, 2:3], None,
                                                          ALU.subtract).then_inc(shift, 1)
                                        dve.wait_ge(shift, n + 1)
                                        link(dve.tensor_scalar(scol[:, bass.ds(win, P)], iota, 0.0, small[:, 2:3],
                                                               ALU.mult, ALU.add))
                                        dve.wait_ge(used, n + 1)
                                        one_hot(gi, onehots[k])
                                        dve.wait_ge(weighted, n + 1)
                                        link(dve.tensor_tensor(Gw.rearrange("p j (h f) -> p (j h) f", f=HF),
                                                               gbuf[:, k, :, 0:F].rearrange("p j (h f) -> p j h f", f=HF),
                                                               lg[:, 2 + k, :].unsqueeze(2).to_broadcast([P, G * HEADS, HF]),
                                                               ALU.mult))
                                        dve.sem_inc(summed)
                                        dve.sem_inc(rows_read)
                                        dve.wait_ge(used, n + 2)
                                        dve.wait_ge(scaled, n + 1)
                                        link(dve.tensor_tensor(acc[:, :, bass.ds(last_win, P)], acc[:, :, bass.ds(last_win, P)],
                                                               winF[:, 1 - k, :].unsqueeze(1).to_broadcast([P, 2, P]), ALU.mult))
                                        link(dve.tensor_tensor(acc[:, :, bass.ds(last_win, P)], acc[:, :, bass.ds(last_win, P)],
                                                               PS[3 - 3 * k][:, :, 0:P], ALU.add))
                                        dve.sem_inc(added)
                                    else:
                                        dve.wait_ge(used, n + 2)
                                        one_hot(gi + 1, onehots[1 - k]).then_inc(hot, 1)
                                        if kind == "message":
                                            for q in range(2):
                                                dve.wait_ge(gathered[k], (G * 16) * (sw * PAIRS + i + 1))
                                                dve.wait_ge(hidden, 2 * n + q + 1)
                                                dve.tensor_tensor(bufA[:, 4 * q:4 * q + 4, :], gbuf[:, k, 4 * q:4 * q + 4, :],
                                                                  PS[2][:, q, :].rearrange("p (j f) -> p j f", j=4),
                                                                  ALU.add).then_inc(summed32, 1)
                                        dve.wait_ge(used, n + 3)
                                        link(dve.tensor_tensor(acc[:, 0:halves, bass.ds(win, P)], acc[:, 0:halves, bass.ds(win, P)],
                                                               PS[3 * k][:, 0:halves, 0:P], ALU.add))
                                        dve.sem_inc(added)
                                    assert link.k == SPG
                        if late:
                            link.at(1 + count * (SPS + NG * SPG))
                            win = dve.snap(at, min_val=0, max_val=NW - P)
                            dve.wait_ge(used, count * NG + 2)
                            link(dve.tensor_tensor(acc[:, :, bass.ds(win, P)], acc[:, :, bass.ds(win, P)],
                                                   winF[:, 1, :].unsqueeze(1).to_broadcast([P, 2, P]), ALU.mult))
                            link(dve.tensor_tensor(acc[:, :, bass.ds(win, P)], acc[:, :, bass.ds(win, P)],
                                                   PS[3][:, :, 0:P], ALU.add))
                            dve.sem_inc(gate)

        def moments():
            s, sem = phase()
            with s:
                steps, var, root = sem("vector_steps"), sem("var"), sem("root")
                me, mo = stats[:, :, 1], stats[:, :, 4]
                with nc.Block() as block:
                    @block.vector
                    def _(dve):
                        link = Steps(dve, steps)
                        mean, dif, r, nb, v = (ln[:, q, :] for q in range(5))
                        dve.tensor_tensor(mean, me, mo, ALU.add)
                        dve.tensor_tensor(dif, me, mo, ALU.subtract)
                        link(dve.tensor_tensor(v, stats[:, :, 2], stats[:, :, 5], ALU.add))
                        dve.tensor_scalar(mean, mean, 0.5, None, ALU.mult)
                        link(dve.tensor_tensor(dif, dif, dif, ALU.mult))
                        link(dve.tensor_scalar(dif, dif, 0.25, None, ALU.mult))
                        link(dve.scalar_tensor_tensor(out=v, in0=v, scalar=1.0 / F, in1=dif, op0=ALU.mult, op1=ALU.add))
                        dve.sem_inc(var)
                        dve.wait_ge(root, 1)
                        link(dve.reciprocal(r, r))
                        link(dve.scalar_tensor_tensor(out=nb, in0=mean, scalar=-1.0, in1=r, op0=ALU.mult, op1=ALU.mult))

                    @block.scalar
                    def _(act):
                        act.wait_ge(var, 1)
                        act.activation(ln[:, 2, :], ln[:, 4, :], ACT.Sqrt, bias=cols[:, EPSC:EPSC + 1]).then_inc(root, 1)

        def normalise(kind, table):
            moments()
            s, sem = phase()
            with s:
                normed, turned, copied, proj, evac = sem("normed"), sem("turned"), sem("copied"), sem("proj"), sem("evac")
                moved, parted, steps, gate = sem("moved"), sem("parted"), sem("vector_steps"), sem("gate")
                split = work[:, 5376:5376 + U * DW // 2].bitcast(bf16).rearrange("p (a c) -> p a c", a=U)
                stored = [sem(f"stored{a}") for a in range(U)]
                stored2 = [sem("stored_dst_logits")]
                width = {"plain": F, "message": F, "attention": TW}[kind]
                with nc.Block() as block:
                    @block.scalar
                    def _(act):
                        for i in iterations(act, NI):
                            for a in range(U):
                                t = i * U + a
                                after(act, turned, i * U)
                                if kind == "plain":
                                    after(act, stored[a], 16 * i)
                                act.activation(hn[:, a, :], X[:, bass.ds(t, 1), :].rearrange("p o f -> p (o f)"), ACT.Relu,
                                               bias=ln[:, 3, bass.ds(t, 1)], scale=ln[:, 2, bass.ds(t, 1)]
                                               ).then_inc(normed, 1)
                            for a in range(U):
                                t = i * U + a
                                act.wait_ge(turned, t + 1)
                                after(act, moved, i * U)
                                after(act, proj, i * U)
                                act.copy(hs[:, a, :], PS[a % 2][:, 0, 0:P]).then_inc(copied, 1)

                    @block.gpsimd
                    def _(pool):
                        for i in iterations(pool, NI):
                            for a in range(U):
                                t = i * U + a
                                pool.wait_ge(copied, t + 1)
                                pool.sem_inc(gate)
                                pool.tensor_copy(Hbuf[:, 0, bass.ds(t * P, P)], hs[:, a, :]).then_inc(moved, 1)

                    @block.tensor
                    def _(pe):
                        for i in iterations(pe, NI):
                            for a in range(U):
                                t = i * U + a
                                pe.wait_ge(normed, t + 1)
                                after(pe, copied, t - 1 if a >= 2 else i * U)
                                pe.transpose(PS[a % 2][:, 0, 0:P], hn[:, a, :], ident[:, :]).then_inc(turned, 1)
                                if kind == "plain":
                                    pe.sem_inc(proj)
                                else:
                                    pe.wait_ge(copied, t + 1)
                                    after(pe, evac, t - 1 if a >= 2 else i * U)
                                    if kind == "message":
                                        to = PS[2 + a % 2][:, 0, 0:F]
                                        pe.matmul(to, hs[:, a, :], W("m1n"), start=True, stop=False)
                                        pe.matmul(to, ones[0:1, :], rows[0:1, 1, :], start=False, stop=True).then_inc(proj, 1)
                                    else:
                                        pe.matmul(PS[2 + a % 2][:, 0, 0:F + 2 * HEADS], hs[:, a, :], wext[:, :],
                                                  start=True, stop=True).then_inc(proj, 1)

                    @block.vector
                    def _(dve):
                        link = Steps(dve, steps)
                        if kind != "plain":
                            for i in iterations(dve, NI):
                                for a in range(U):
                                    t = i * U + a
                                    dve.wait_ge(proj, t + 1)
                                    after(dve, stored[a], 16 * i)
                                    if kind == "attention":
                                        after(dve, stored2[0], 16 * i)
                                    w = F if kind == "message" else F + 2 * HEADS
                                    dve.tensor_copy(nm[:, a, 0:w], PS[2 + a % 2][:, 0, 0:w]).then_inc(evac, 1)
                                if kind == "attention":
                                    link.at(i * 4)
                                    D, D16 = nm[:, :, TW:TW + HEADS], split[:, :, :]
                                    dve.wait_ge(evac, i * U + U)
                                    link(dve.tensor_copy(D16[:, :, 0:HEADS], D))
                                    link(dve.tensor_tensor(D, D, D16[:, :, 0:HEADS], ALU.subtract))
                                    link(dve.tensor_copy(D16[:, :, HEADS:2 * HEADS], D))
                                    link(dve.tensor_tensor(D, D, D16[:, :, HEADS:2 * HEADS], ALU.subtract))
                                    dve.tensor_copy(D16[:, :, 2 * HEADS:DW], D).then_inc(parted, 1)

                    @block.sync
                    def _(sp):
                        for i in iterations(sp, NI):
                            for a in range(U):
                                t = i * U + a
                                sp.wait_ge(normed if kind == "plain" else evac, t + 1)
                                of = hn[:, a, :] if kind == "plain" else nm[:, a, 0:width]
                                sp.dma_start(table[bass.ds(t * P, P), :], of).then_inc(stored[a], 16)
                            if kind == "attention":
                                sp.wait_ge(parted, i + 1)
                                sp.dma_start(T_DST[bass.ds(i * (U * P), U * P), :].rearrange("(a p) c -> p a c", p=P),
                                             split[:, :, :]).then_inc(stored2[0], 16)
                        for a in range(U):
                            sp.wait_ge(stored[a], 16 * NI)
                        if kind == "attention":
                            sp.wait_ge(stored2[0], 16 * NI)

        def nodes(kind):
            s, sem = phase()
            with s:
                gate = sem("gate")
                meaned, dense, act1, dense2, act2, turned, taken, moved, steps = (
                    sem("meaned"), sem("dense"), sem("act1"), sem("dense2"), sem("act2"), sem("turned"), sem("taken"),
                    sem("moved"), sem("vector_steps"))
                stored = [sem(f"stored{a}") for a in range(U)]
                sel = work[0:HEADS, 7168:7168 + F]
                parts = work[:, 3584:7168].rearrange("p (a q f) -> p a q f", a=U, q=NACC)
                outs = {"conv1": 2, "conv2": 2}.get(kind, 1)
                ins_ = 2 if kind == "conv2" else 1
                width = {"conv1": 2 * F, "conv2": F}.get(kind, 0)
                table = {"conv1": T_C2, "conv2": T_C3}.get(kind)
                hasdense = kind in ("l0", "conv1", "conv2", "update")
                terms = {
                    "l0": [[("l0x", (Hbuf, 0))]],
                    "conv1": [[(f"c1l0{o}", (acc, 0)), (f"c1r0{o}", (Hbuf, 0))] for o in range(2)],
                    "conv2": [[(f"c2l{q}{o}", (acc, q)) for q in range(2)] + [(f"c2r{q}{o}", (Hbuf, q)) for q in range(2)]
                              for o in range(2)],
                    "update": [[("w2u", (acc, 0)), ("u1h", (Hbuf, 0))]],
                }.get(kind)
                bias = {"l0": [B0], "conv1": [B1, B1 + 1], "conv2": [B2, B2 + 1], "update": [CU]}.get(kind)
                with nc.Block() as block:
                    @block.vector
                    def _(dve):
                        link = Steps(dve, steps)
                        if kind in ("conv1", "update"):
                            link(dve.tensor_tensor(acc[:, 0, :], acc[:, 0, :], rcnt[:, :], ALU.mult))
                            if kind == "update":
                                link(dve.tensor_scalar(acc[0:1, 1, :], rcnt[0:1, :], 0.0, None, ALU.is_gt))
                        if kind == "conv2":
                            for q in range(2):
                                link(dve.tensor_tensor(acc[:, q, :], acc[:, q, :], rcnt[:, :], ALU.mult))
                        if kind == "final":
                            dve.tensor_copy(sel.rearrange("p (h f) -> p h f", h=HEADS),
                                            ident[0:HEADS, 0:HEADS].unsqueeze(2).to_broadcast([HEADS, HEADS, HF]))
                            link(dve.tensor_scalar(scol, scol, small[:, 2:3], None, ALU.subtract))
                            dve.sem_inc(meaned)
                            dve.wait_ge(act1, 1)
                            for q, p in ((1, HEADS), (0, P)):
                                link(dve.tensor_tensor(acc[0:p, q, :], acc[0:p, q, :], scol[0:p, :], ALU.mult))
                            link(dve.tensor_scalar(acc[0:HEADS, 1, :], acc[0:HEADS, 1, :], ATT_EPS, None, ALU.add))
                            link(dve.reciprocal(acc[0:HEADS, 1, :], acc[0:HEADS, 1, :]))
                        dve.sem_inc(meaned)
                        k0 = link.k
                        per = {"l0": 1, "conv3": 1, "update": 1, "final": 0}.get(kind, 0) * U
                        for i in iterations(dve, NI):
                            link.at(k0 + i * per)
                            if kind in ("conv3", "final"):
                                for a in range(U):
                                    t = i * U + a
                                    after(dve, turned, i * U)
                                    if kind == "final":
                                        dve.wait_ge(dense, t + 1)
                                    other = rcnt[:, bass.ds(t * P, P)] if kind == "conv3" else PS[a % 2][:, 0, 0:P]
                                    dve.tensor_tensor(st[:, a, 0, :], acc[:, 0, bass.ds(t * P, P)], other,
                                                      ALU.mult).then_inc(act1, 1)
                            for a in range(U):
                                t = i * U + a
                                Xt = X[:, bass.ds(t, 1), :].rearrange("p o f -> p (o f)")
                                dve.wait_ge(turned, t + 1)
                                if kind in ("l0", "final"):
                                    dve.tensor_tensor(Xt, Xt, PS[2 + a % 2][:, 0, 0:F], ALU.add).then_inc(taken, 1)
                                if kind == "l0":
                                    dve.wait_ge(taken, t + 1)
                                if kind == "conv3":
                                    R = Hbuf[:, 0, bass.ds(t * P, P)]
                                    link(dve.tensor_tensor(tmp[:, a, :], PS[2 + a % 2][:, 0, 0:F], R, ALU.add))
                                    dve.scalar_tensor_tensor(out=Xt, in0=tmp[:, a, :], scalar=0.0, in1=Xt, op0=ALU.max,
                                                             op1=ALU.add).then_inc(taken, 1)
                                    dve.wait_ge(taken, t + 1)
                                if kind in ("l0", "conv3"):
                                    dve.bn_stats(stats[:, bass.ds(t, 1), :].rearrange("p o c -> p (o c)"), Xt)
                                if kind in ("conv1", "conv2"):
                                    after(dve, stored[a], 16 * i)
                                    dve.tensor_copy(nm[:, a, 0:width], PS[2 + a % 2][:, 0, 0:width]).then_inc(taken, 1)
                                    if kind == "conv2":
                                        dve.tensor_copy(Hbuf[:, 0, bass.ds(t * P, P)], PS[2 + a % 2][:, 1, 0:F]).then_inc(moved, 1)
                                if kind == "update":
                                    Y = Hbuf[:, 1, bass.ds(t * P, P)]
                                    dve.tensor_copy(Y, PS[2 + a % 2][:, 0, 0:F]).then_inc(taken, 1)
                                    dve.wait_ge(taken, t + 1)
                                    dve.bn_stats(stats[:, bass.ds(t, 1), :].rearrange("p o c -> p (o c)"), Y)

                    @block.scalar
                    def _(act):
                        if kind == "final":
                            act.wait_ge(meaned, 1)
                            act.activation(scol, scol, ACT.Exp).then_inc(act1, 1)
                        if hasdense:
                            for i in iterations(act, NI):
                                for a in range(U):
                                    t = i * U + a
                                    if kind == "l0":
                                        act.wait_ge(dense2, t + 1)
                                        after(act, dense, i * U)
                                        act.copy(st[:, a, 1, :], PS[a % 2][:, 1, 0:P]).then_inc(act2, 1)
                                    act.wait_ge(dense, t + 1)
                                    after(act, turned, i * U)
                                    if kind == "conv1":
                                        after(act, moved, i * U)
                                    for o in range(outs):
                                        last = act.activation(st[:, a, o, :], PS[a % 2][:, o, 0:P], ACT.Relu,
                                                              bias=cols[:, bias[o]:bias[o] + 1])
                                    last.then_inc(act1, 1)
                                    if kind == "update":
                                        act.wait_ge(dense2, t + 1)
                                        act.activation(st[:, a, 1, :], PS[a % 2][:, 1, 0:P], ACT.Identity,
                                                       bias=cols[:, UB2:UB2 + 1]).then_inc(act2, 1)

                    @block.gpsimd
                    def _(pool):
                        if kind == "conv1":
                            for i in iterations(pool, NI):
                                for a in range(U):
                                    t = i * U + a
                                    pool.wait_ge(act1, t + 1)
                                    pool.sem_inc(gate)
                                    pool.tensor_copy(Hbuf[:, :, bass.ds(t * P, P)], st[:, a, :, :]).then_inc(moved, 1)

                    @block.sync
                    def _(sp):
                        if kind == "l0":
                            for i in iterations(sp, NI):
                                for a in range(U):
                                    t = i * U + a
                                    after(sp, dense2, i * U)
                                    for q in range(NACC):
                                        sp.dma_start(parts[:, a, q, :], T_PART[q][bass.ds(t * P, P), :]).then_inc(stored[a], 16)
                        if width:
                            for i in iterations(sp, NI):
                                for a in range(U):
                                    t = i * U + a
                                    sp.wait_ge(taken, t + 1)
                                    sp.dma_start(table[bass.ds(t * P, P), :], nm[:, a, 0:width]).then_inc(stored[a], 16)
                            for a in range(U):
                                sp.wait_ge(stored[a], 16 * NI)

                    @block.tensor
                    def _(pe):
                        pe.wait_ge(meaned, 2 if kind == "final" else 1)
                        for i in iterations(pe, NI):
                            def back(a):
                                t = i * U + a
                                if kind == "update":
                                    pe.wait_ge(act2, t + 1)
                                else:
                                    pe.wait_ge(act1, t + 1 + (kind == "final"))
                                after(pe, taken, t - 1 if a >= 2 else i * U)
                                if kind == "conv2":
                                    after(pe, moved, t - 1 if a >= 2 else i * U)
                                to = PS[2 + a % 2]
                                if kind == "conv2":
                                    for q in range(2):
                                        pe.matmul(to[:, 0, 0:F], st[:, a, q, :], W(f"c3l{q}0"), start=q == 0, stop=q == 1)
                                    for q in range(2):
                                        pe.matmul(to[:, 1, 0:F], st[:, a, q, :], W(f"c3r{q}0"), start=q == 0, stop=False)
                                    last = pe.matmul(to[:, 1, 0:F], ones[0:1, :], rows[0:1, 0, :], start=False, stop=True)
                                elif kind == "conv1":
                                    for q in range(2):
                                        last = pe.transpose(to[:, 0, q * P:(q + 1) * P], st[:, a, q, :], ident[:, :])
                                else:
                                    last = pe.transpose(to[:, 0, 0:P], st[:, a, int(kind == "update"), :], ident[:, :])
                                last.then_inc(turned, 1)

                            for a in range(U):
                                t = i * U + a
                                if kind == "final":
                                    pe.wait_ge(act1, t if a >= 2 else i * U + 1)
                                    pe.matmul(PS[a % 2][:, 0, 0:P], sel, acc[0:HEADS, 1, bass.ds(t * P, P)],
                                              start=True, stop=True).then_inc(dense, 1)
                                if hasdense:
                                    done = act2 if kind == "update" else act1
                                    if kind == "l0":
                                        pe.wait_ge(stored[a], (i + 1) * (16 * NACC))
                                        after(pe, act2, t - 1 if a >= 2 else i * U)
                                        for q in range(NACC):
                                            last = pe.matmul(PS[a % 2][:, 1, 0:P], parts[:, a, q, :], ident[:, :],
                                                             start=q == 0, stop=q == NACC - 1)
                                        last.then_inc(dense2, 1)
                                    after(pe, done, t - 1 if a >= 2 else i * U)
                                    for o in range(outs):
                                        for q, (w, (buf, half)) in enumerate(terms[o]):
                                            end = q == len(terms[o]) - 1 and kind not in ("update", "l0")
                                            last = pe.matmul(PS[a % 2][:, o, 0:P], W(w), buf[:, half, bass.ds(t * P, P)],
                                                             start=q == 0, stop=end)
                                    if kind == "l0":
                                        pe.wait_ge(act2, t + 1)
                                        last = pe.matmul(PS[a % 2][:, 0, 0:P], W("l0a"), st[:, a, 1, :], start=False, stop=True)
                                    if kind == "update":
                                        last = pe.matmul(PS[a % 2][:, 0, 0:P], rows[0:1, 2, :], acc[0:1, 1, bass.ds(t * P, P)],
                                                         start=False, stop=True)
                                    last.then_inc(dense, 1)
                                    if kind == "update":
                                        pe.wait_ge(act1, t + 1)
                                        pe.matmul(PS[a % 2][:, 1, 0:P], W("u2"), st[:, a, 0, :], start=True, stop=False)
                                        pe.matmul(PS[a % 2][:, 1, 0:P], ident[:, :], Hbuf[:, 0, bass.ds(t * P, P)],
                                                  start=False, stop=True).then_inc(dense2, 1)
                                if a >= 1 and kind != "final":
                                    back(a - 1)
                            for a in range(0 if kind == "final" else U - 1, U):
                                back(a)

        def add_update():
            moments()
            s, sem = phase()
            with s:
                loaded, z, steps, gate = sem("loaded"), sem("z"), sem("vector_steps"), sem("gate")
                with nc.Block() as block:
                    @block.sync
                    def _(sp):
                        for to, v in ((gamma, L2_gnn_ln_gamma), (beta, L2_gnn_ln_beta)):
                            sp.dma_start(to, v.rearrange("(o f) -> o f", o=1).to_broadcast([P, F])).then_inc(loaded, 16)

                    @block.scalar
                    def _(act):
                        for i in iterations(act, NI):
                            for a in range(U):
                                t = i * U + a
                                after(act, steps, i * (4 * U))
                                act.activation(tmp[:, a, :], Hbuf[:, 1, bass.ds(t * P, P)], ACT.Identity,
                                               bias=ln[:, 3, bass.ds(t, 1)], scale=ln[:, 2, bass.ds(t, 1)]).then_inc(z, 1)

                    @block.vector
                    def _(dve):
                        link = Steps(dve, steps)
                        dve.wait_ge(loaded, 32)
                        for i in iterations(dve, NI):
                            link.at(i * (4 * U))
                            for a in range(U):
                                t = i * U + a
                                Xt = X[:, bass.ds(t, 1), :].rearrange("p o f -> p (o f)")
                                dve.wait_ge(z, t + 1)
                                link(dve.tensor_tensor(tmp[:, a, :], tmp[:, a, :], gamma, ALU.mult))
                                link(dve.tensor_tensor(tmp[:, a, :], tmp[:, a, :], beta, ALU.add))
                                link(dve.tensor_tensor(Xt, Xt, tmp[:, a, :], ALU.add))
                                link(dve.bn_stats(stats[:, bass.ds(t, 1), :].rearrange("p o c -> p (o c)"), Xt))
                            dve.sem_inc(gate)

        def write_out():
            s, sem = phase()
            with s:
                stored = sem("out_stored")
                with nc.Block() as block:
                    @block.sync
                    def _(sp):
                        sp.dma_start(out[0:NFULL * P, :].rearrange("(t p) f -> p t f", p=P), X[:, 0:NFULL, :]).then_inc(stored, 16)
                        if NTAIL:
                            sp.dma_start(out[NFULL * P:N, :], X[0:NTAIL, NFULL, :]).then_inc(stored, 16)
                        sp.wait_ge(stored, 16 * (1 + (NTAIL > 0)))

        prepare()
        normalise("plain", T_L0)
        reverse_edges()
        nodes("l0")
        normalise("plain", T_C1)
        edges("sum", T_C1)
        nodes("conv1")
        edges("wide", T_C2)
        nodes("conv2")
        edges("sum", T_C3)
        nodes("conv3")
        normalise("message", T_MSG)
        edges("message", T_MSG)
        nodes("update")
        add_update()
        normalise("attention", T_ATT)
        edges("attention", T_ATT)
        nodes("final")
        write_out()


_INS = ['x', 'src', 'dst', 'edge_attr_64', 'L0_gnn_W', 'L0_gnn_b', 'L1_gnn_W1l', 'L1_gnn_b1', 'L1_gnn_W1r', 'L1_gnn_W2l',
        'L1_gnn_b2', 'L1_gnn_W2r', 'L1_gnn_W3l', 'L1_gnn_b3', 'L1_gnn_W3r', 'L2_gnn_global_state', 'L2_gnn_msg_w1',
        'L2_gnn_msg_b1', 'L2_gnn_msg_w2', 'L2_gnn_msg_b2', 'L2_gnn_upd_w1', 'L2_gnn_upd_b1', 'L2_gnn_upd_w2',
        'L2_gnn_upd_b2', 'L2_gnn_ln_gamma', 'L2_gnn_ln_beta', 'L3_gnn_W', 'L3_gnn_a']


def kernel(**inputs):
    import numpy as _np
    import concourse.bacc as _bacc
    from concourse import mybir as _mybir
    from concourse.bass_utils import run_bass_kernel_spmd as _run

    nc = _bacc.Bacc("TRN2", target_bir_lowering=False, num_devices=1)
    arrays, args = {}, []
    for name in _INS:
        a = _np.ascontiguousarray(inputs[name])
        arrays[f"in_{name}_dram"] = a
        args.append(nc.dram_tensor(f"in_{name}_dram", a.shape, _mybir.dt.from_np(a.dtype), kind="ExternalInput").ap())
    shape = tuple(inputs["x"].shape)
    args.append(nc.dram_tensor("out_dram", shape, _mybir.dt.float32, kind="ExternalOutput").ap())
    bass_gnn_preln_d4(nc, *args)
    r = _run(nc, [arrays], core_ids=[0])
    return r.results[0]["out_dram"]
```

```python
import concourse.bass as bass
from concourse import mybir
from contextlib import ExitStack


class Steps:

    def __init__(self, eng, sem):
        self.eng, self.sem, self.base, self.k = eng, sem, 0, 0

    def at(self, base):
        self.base, self.k = base, 0

    def __call__(self, ins):
        self.k += 1
        ins.then_inc(self.sem, 1)
        self.eng.wait_ge(self.sem, self.base + self.k)


def iterations(eng, n):
    yield 0
    if n > 1:
        with eng.Fori(1, n) as i:
            yield i


def after(eng, sem, value):
    if not isinstance(value, int) or value > 0:
        eng.wait_ge(sem, value)


def pipelined(eng, n, u, *stages):
    for i in iterations(eng, n):
        for a in range(u):
            for lag, stage in enumerate(stages):
                if stage is not None and not (isinstance(i, int) and a < lag):
                    stage(i * u + (a - lag), (a - lag) % u)
    for r in range(len(stages) - 1):
        for lag, stage in enumerate(stages):
            if stage is not None and lag > r:
                stage(n * u + r - lag, (r - lag) % u)


def bass_gnn_preln_d4(nc, x, src, dst, edge_attr_64, L0_gnn_W, L0_gnn_b, L1_gnn_W1l, L1_gnn_b1, L1_gnn_W1r,
                      L1_gnn_W2l, L1_gnn_b2, L1_gnn_W2r, L1_gnn_W3l, L1_gnn_b3, L1_gnn_W3r, L2_gnn_global_state,
                      L2_gnn_msg_w1, L2_gnn_msg_b1, L2_gnn_msg_w2, L2_gnn_msg_b2, L2_gnn_upd_w1, L2_gnn_upd_b1,
                      L2_gnn_upd_w2, L2_gnn_upd_b2, L2_gnn_ln_gamma, L2_gnn_ln_beta, L3_gnn_W, L3_gnn_a, out):
    f32, i32 = mybir.dt.float32, mybir.dt.int32
    ALU, ACT, AX = mybir.AluOpType, mybir.ActivationFunctionType, mybir.AxisListType

    P = 128
    N, F = x.shape
    E, ED = edge_attr_64.shape
    GD = L2_gnn_global_state.shape[0]
    HEADS, HF = L3_gnn_a.shape[0], F // L3_gnn_a.shape[0]
    U = 7
    NT = U * -(-N // (P * U))
    NI = NT // U
    PORTIONS = ((0, 4), (4, U))
    NFULL, NTAIL = N // P, N % P
    G = 8
    PAIRS = 2 * -(-E // (4 * G * P))
    NG, ET = 2 * PAIRS, 2 * PAIRS * G
    EFULL, ETAIL = E // P, E % P
    NW = NT * P + P
    QB = -(-ET // P)
    TW = F + HEADS
    LN_EPS, ATT_EPS, SLOPE, FAR = 1e-5, 1e-8, 0.2, -1e30

    T_C1, T_C3, T_MSG = [nc.dram_tensor(f"table_{n}", [NT * P, F], f32, kind="Internal").ap() for n in ("c1", "c3", "msg")]
    T_L0 = nc.dram_tensor("table_l0", [NW, F], f32, kind="Internal").ap()
    T_C2 = nc.dram_tensor("table_c2", [NT * P, 2 * F], f32, kind="Internal").ap()
    T_ATT = nc.dram_tensor("table_att", [NT * P, TW], f32, kind="Internal").ap()
    NACC = 4
    T_PART = [nc.dram_tensor(f"sum_by_source_{q}", [NT * P + P, F], f32, kind="Internal").ap() for q in range(NACC)]
    bf16 = mybir.dt.bfloat16
    DW = 3 * HEADS
    T_DST = nc.dram_tensor("table_dst_logits", [NW, DW], bf16, kind="Internal").ap()

    with ExitStack() as ctx:
        def sb(name, shape, dt=f32):
            return ctx.enter_context(nc.sbuf_tensor(name, shape, dt))

        X = sb("X", [P, NT, F])
        acc = sb("acc", [P, 2, NW])
        rcnt = sb("rcnt", [P, NW])
        Hflat = sb("Hbuf", [P, max(2 * NT * P, NT * P + 5120, NW + 1344)])
        Hbuf = Hflat[:, 0:2 * NT * P].rearrange("p (k n) -> p k n", k=2)
        scol = Hflat[:, 0:NW]
        work = sb("work", [P, 8192])
        srcI = sb("srcI", [P, ET + 4 * G], i32)
        dstF = sb("dstF", [P, ET])
        dl = sb("dl", [P, ET + 2 * G])
        base0 = sb("base0", [P, NG])
        baseF = sb("baseF", [P, NG])
        baseI = sb("baseI", [1, NG], i32)
        step = sb("step", [P, 1])
        sweeps = sb("sweeps", [1, 4], i32)
        idx = sb("idx", [P, 4, G], i32)
        wt = sb("wt", [P, 25, F])
        wext = sb("wext", [P, F + 2 * HEADS])
        cols = sb("cols", [P, 8])
        rows = sb("rows", [1, 2, F])
        ones = sb("ones", [P, P])
        ident = sb("ident", [P, P])
        small = sb("small", [P, 8])
        dwin = sb("dwin", [P, 2, DW], bf16)
        PS = [ctx.enter_context(nc.psum_tensor(f"ps{i}", [P, 2, 512], f32)) for i in range(4)]

        W_NAMES = (["l0x", "l0a"] + [f"c1{s}0{o}" for s in "lr" for o in range(2)]
                   + [f"c2{s}{i}{o}" for s in "lr" for i in range(2) for o in range(2)]
                   + [f"c3{s}{i}0" for s in "lr" for i in range(2)]
                   + ["m1n", "m1a", "m1b", "w2u", "u1h", "u2", "iota"])
        assert len(W_NAMES) <= 25

        def W(name):
            return wt[:, W_NAMES.index(name), :]

        iota = W("iota")
        B0, B1, B2, CU, UB2, EPSC = 0, 1, 3, 5, 6, 7

        def tile_of(v, t):
            return v[:, bass.ds(t, 1), :].rearrange("p o f -> p (o f)")

        g256 = work[:, 0:2 * G * 256].rearrange("p (s j f) -> p s j f", s=2, j=G)
        g128 = work[:, 0:2 * G * 128].rearrange("p (s j f) -> p s j f", s=2, j=G)
        g132 = work[:, 0:4 * G * TW].rearrange("p (s j f) -> p s j f", s=4, j=G)
        bufA = work[:, 2112:3136].rearrange("p (j f) -> p j f", j=G)
        winF = Hflat[:, NW + 1024:NW + 1024 + 2 * P].rearrange("p (k f) -> p k f", k=2)
        lg = work[:, 7424:7424 + 4 * G * HEADS].rearrange("p (k c) -> p k c", k=4)
        def edge_buffers(o):
            return ([work[:, o + q:o + q + 1024].rearrange("p (j f) -> p j f", j=G) for q in (4096, 6144)],
                    work[:, o + 5120:o + 6144].rearrange("p (j f) -> p j f", j=G))
        hotT = Hflat[:, NW:NW + 512].bitcast(bf16).rearrange("p (j f) -> p j f", j=G)
        hot16a = Hflat[:, NW + 512:NW + 1024].bitcast(bf16).rearrange("p (j f) -> p j f", j=G)
        ident16 = Hflat[:, NW + 1280:NW + 1344].bitcast(bf16)
        ea = work[:, 7168:8192].rearrange("p (s c) -> p s c", s=2)
        st = work[:, 0:2 * U * F].rearrange("p (a o f) -> p a o f", a=U, o=2)
        hn = work[:, 1792:1792 + U * F].rearrange("p (a f) -> p a f", a=U)
        hs = work[:, 2688:2688 + U * F].rearrange("p (a f) -> p a f", a=U)
        nm = work[:, 3584:3584 + U * 256].rearrange("p (a f) -> p a f", a=U)
        tmp = work[:, 5376:5376 + U * F].rearrange("p (a f) -> p a f", a=U)
        gamma = work[:, 7168:7168 + F]
        beta = work[:, 7168 + F:7168 + 2 * F]
        stats = work[:, 7424:7424 + NT * 6].rearrange("p (t c) -> p t c", c=6)
        ln = work[:, 7424 + NT * 6:7424 + NT * 11].rearrange("p (k t) -> p k t", k=5)

        def phase():
            s, mine = ExitStack(), []
            uid = phase.n
            phase.n += 1

            def sem(name):
                mine.append(nc.alloc_semaphore(f"{name}_{uid}"))
                return mine[-1]

            s.callback(nc.all_engine_barrier)
            s.callback(lambda: nc.clear_and_free_semaphores(mine))
            return s, sem
        phase.n = 0

        def prepare():
            s, sem = phase()
            with s:
                loaded, indices, filled, pads = sem("loaded"), sem("indices"), sem("filled"), sem("pads")
                steps, asfloat, turned, kept, made = (sem("vector_steps"), sem("asfloat"), sem("turned"), sem("kept"),
                                                      sem("made"))
                zeroed = sem("dst_table_zeroed")
                rawI = work[:, 0:2 * QB * P].bitcast(i32).rearrange("p (k q c) -> p k q c", k=2, q=QB)
                rawF = work[:, 1792:1792 + 2 * QB * P].rearrange("p (k q c) -> p k q c", k=2, q=QB)
                nat = work[:, 3584:3584 + 20 * F].rearrange("p (b f) -> p b f", f=F)
                w1g = work[:, 6144:6144 + F]
                u1c = work[:, 6272:6272 + F]
                u1b = work[:, 6400:6400 + F]
                w2t = work[:, 6528:6528 + F]
                ablk = work[:, 6656:6656 + 2 * HEADS]
                gcol = work[:, 6672:6673]
                mb2 = work[:, 6673:6674]
                zero4 = work[:, 6676:6676 + DW // 2].bitcast(bf16)
                ub1 = work[:, 6690:6691]
                natural = [(L0_gnn_W, 0, 0), (L0_gnn_W, 0, 1)]
                natural += [(w, o, 0) for w in (L1_gnn_W1l, L1_gnn_W1r) for o in range(2)]
                natural += [(w, o, i) for w in (L1_gnn_W2l, L1_gnn_W2r) for i in range(2) for o in range(2)]
                natural += [(w, 0, i) for w in (L1_gnn_W3l, L1_gnn_W3r) for i in range(2)]
                natural += [(L3_gnn_W, 0, 0), (L2_gnn_msg_w2, 0, 0)]
                NB, IL3, IMW2 = len(natural), len(natural) - 2, len(natural) - 1
                with nc.Block() as block:
                    @block.sync
                    def _(sp):
                        sp.wait_ge(filled, 1)
                        for k, v in ((0, src), (1, dst)):
                            for q in range(QB):
                                r = min(P, EFULL - q * P)
                                if r > 0:
                                    sp.dma_start(rawI[0:r, k, q, :], v[q * P * P:(q * P + r) * P].rearrange(
                                        "(t p) -> t p", p=P)).then_inc(indices, 16)
                            if ETAIL:
                                q, r = EFULL // P, EFULL % P
                                sp.dma_start(rawI[r:r + 1, k, q, 0:ETAIL],
                                             v[EFULL * P:E].rearrange("(o c) -> o c", o=1)).then_inc(indices, 16)
                        def load(o, i):
                            sp.dma_start(o, i).then_inc(loaded, 16)
                        for b, (w, r, c) in enumerate(natural):
                            load(nat[:, b, :], w[r * P:(r + 1) * P, c * P:(c + 1) * P])
                        load(X[:, 0:NFULL, :], x[0:NFULL * P, :].rearrange("(t p) f -> p t f", p=P))
                        if NTAIL:
                            load(X[0:NTAIL, NFULL, :], x[NFULL * P:N, :])
                        load(W("m1n"), L2_gnn_msg_w1[0:F, :])
                        load(W("m1a")[0:ED, :], L2_gnn_msg_w1[F:F + ED, :])
                        load(W("m1b")[ED:2 * ED, :], L2_gnn_msg_w1[F:F + ED, :])
                        load(w1g[0:GD, :], L2_gnn_msg_w1[F + ED:F + ED + GD, :])
                        load(W("u1h"), L2_gnn_upd_w1[0:F, :])
                        load(u1b, L2_gnn_upd_w1[F:2 * F, :])
                        load(u1c[0:GD, :], L2_gnn_upd_w1[2 * F:2 * F + GD, :])
                        load(W("u2"), L2_gnn_upd_w2)
                        for h in range(HEADS):
                            for k in range(2):
                                load(ablk[HF * h:HF * (h + 1), HEADS * k + h:HEADS * k + h + 1],
                                     L3_gnn_a[h, HF * k:HF * (k + 1)].rearrange("(f o) -> f o", o=1))
                        load(gcol[0:GD, :], L2_gnn_global_state.rearrange("(f o) -> f o", o=1))
                        load(mb2, L2_gnn_msg_b2.rearrange("(f o) -> f o", o=1))
                        load(cols[:, B0:B0 + 1], L0_gnn_b.rearrange("(f o) -> f o", o=1))
                        for o in range(2):
                            load(cols[:, B1 + o:B1 + o + 1], L1_gnn_b1[o * P:(o + 1) * P].rearrange("(f o) -> f o", o=1))
                            load(cols[:, B2 + o:B2 + o + 1], L1_gnn_b2[o * P:(o + 1) * P].rearrange("(f o) -> f o", o=1))
                        load(ub1, L2_gnn_upd_b1.rearrange("(f o) -> f o", o=1))
                        load(cols[:, UB2:UB2 + 1], L2_gnn_upd_b2.rearrange("(f o) -> f o", o=1))
                        load(rows[0:1, 0, :], L2_gnn_msg_b1.rearrange("(o f) -> o f", o=1))
                        for q in range(NACC):
                            sp.dma_start(T_PART[q].rearrange("(t p) f -> p t f", p=P),
                                         acc[:, 0, :].rearrange("p (t f) -> p t f", f=P)).then_inc(zeroed, 16)
                        sp.dma_start(T_L0[NT * P:NT * P + P, :], acc[:, 0, 0:F]).then_inc(zeroed, 16)
                        for t in range(NT + 1):
                            if t >= NFULL:
                                sp.dma_start(T_DST[t * P:(t + 1) * P, :], zero4).then_inc(zeroed, 16)
                        sp.wait_ge(zeroed, 16 * (NT + 1 - NFULL + NACC + 1))

                    n_idx = 2 * sum(min(P, EFULL - q * P) > 0 for q in range(QB)) + 2 * (ETAIL > 0)
                    n_load = NB + 1 + (NTAIL > 0) + 8 + 2 * HEADS + 2 + 1 + 4 + 2 + 1

                    @block.gpsimd
                    def _(pool):
                        pool.iota(iota, [[1, P]], base=0, channel_multiplier=0,
                                  allow_small_or_imprecise_dtypes=True).then_inc(pads, 1)
                        pool.iota(small[:, 0:1], [[0, 1]], base=0, channel_multiplier=1,
                                  allow_small_or_imprecise_dtypes=True).then_inc(pads, 1)

                    @block.vector
                    def _(dve):
                        link = Steps(dve, steps)
                        dve.memset(rawI[:, 0, :, :], 0)
                        dve.memset(rawI[:, 1, :, :], -4096)
                        dve.memset(acc[:, 0, :], 0.0)
                        dve.memset(srcI[:, ET:ET + 4 * G], 0)
                        dve.memset(dl[:, ET:ET + 2 * G], FAR)
                        dve.memset(X[:, NFULL:NT, :], 0.0)
                        dve.memset(W("m1a"), 0.0)
                        dve.memset(W("m1b"), 0.0)
                        dve.memset(ablk, 0.0)
                        dve.memset(zero4, 0.0)
                        dve.memset(ones[:, :], 1.0)
                        dve.memset(cols[:, EPSC:EPSC + 1], LN_EPS)
                        link(dve.memset(rows[:, :, :], 0.0))
                        dve.sem_inc(filled)
                        dve.wait_ge(pads, 2)
                        link(dve.tensor_scalar(ident[:, :], iota, small[:, 0:1], None, ALU.is_equal))
                        dve.wait_ge(indices, 16 * n_idx)
                        dve.tensor_copy(rawF[:, :, :, :], rawI[:, :, :, :]).then_inc(asfloat, 1)
                        blocks = [(k, q) for k in range(2) for q in range(QB)]
                        for b, (k, q) in enumerate(blocks):
                            dve.wait_ge(turned, b + 1)
                            c = min(P, ET - q * P)
                            to = (srcI if k == 0 else dstF)[:, q * P:q * P + c]
                            dve.tensor_copy(to, PS[b % 2][:, 0, 0:c]).then_inc(kept, 1)
                        for b in range(NB):
                            dve.wait_ge(turned, len(blocks) + b + 1)
                            to = wext[:, 0:F] if b == IL3 else w2t if b == IMW2 else wt[:, b, :]
                            dve.tensor_copy(to, PS[(len(blocks) + b) % 2][:, 0, 0:P]).then_inc(kept, 1)
                        dve.wait_ge(made, 5)
                        dve.tensor_copy(wext[:, F:F + 2 * HEADS], PS[2][:, 0, 0:2 * HEADS])
                        dve.tensor_tensor(rows[0:1, 0, :], rows[0:1, 0, :], PS[2][0:1, 1, 0:F], ALU.add)
                        dve.tensor_copy(rows[0:1, 1, :], PS[3][0:1, 0, 0:F])
                        dve.tensor_tensor(cols[:, CU:CU + 1], ub1, PS[3][:, 1, 0:1], ALU.add)
                        dve.wait_ge(made, 6)
                        dve.tensor_copy(W("w2u"), PS[0][:, 1, 0:F])
                        first = dstF[:, :].rearrange("p (g j) -> p g j", j=G)[0:1, :, 0]
                        link(dve.tensor_copy(base0[0:1, :], first))
                        dve.sem_inc(filled)
                        dve.wait_ge(made, 7)
                        link(dve.tensor_copy(base0[:, :], PS[1][:, 1, 0:NG]))
                        d3, b3 = (v.rearrange("p (g j) -> p g j", j=G) for v in (dl[:, 0:ET], dstF[:, :]))
                        link(dve.tensor_tensor(d3, b3, base0[:, :].unsqueeze(2).to_broadcast([P, NG, G]), ALU.subtract))
                        inw = rawF[:, :, :, :].rearrange("p k q c -> p (k q c)")[:, 0:ET]
                        link(dve.tensor_scalar(inw, dl[:, 0:ET], 0.0, None, ALU.is_ge))
                        link(dve.scalar_tensor_tensor(out=inw, in0=dl[:, 0:ET], scalar=float(P - 1), in1=inw,
                                                      op0=ALU.is_le, op1=ALU.mult))
                        if ETAIL:
                            link(dve.tensor_scalar(small[:, 1:2], small[:, 0:1], float(ETAIL), None, ALU.is_ge))
                            link(dve.tensor_tensor(inw[:, EFULL:EFULL + 1], inw[:, EFULL:EFULL + 1], small[:, 1:2], ALU.max))
                        link(dve.tensor_reduce(small[:, 2:3], inw[:, 0:EFULL + (ETAIL > 0)], AX.X, ALU.min))
                        dve.sem_inc(filled)
                        dve.wait_ge(made, 8)
                        link(dve.tensor_reduce(small[0:1, 3:4], PS[2][0:1, 0, 0:P], AX.X, ALU.min))
                        dve.sem_inc(filled)
                        link(dve.tensor_scalar(small[0:1, 4:5], small[0:1, 3:4], float(1 - NT), float(NT), ALU.mult, ALU.add))
                        link(dve.tensor_copy(sweeps[0:1, 0:1], small[0:1, 4:5]))
                        dve.wait_ge(made, 9)
                        link(dve.tensor_copy(small[:, 5:6], PS[3][:, 0, 0:1]))
                        link(dve.tensor_scalar(step[:, :], small[:, 5:6], float(-P), float(P), ALU.mult, ALU.add))
                        link(dve.tensor_scalar(base0[:, :], base0[:, :], small[:, 5:6], None, ALU.mult))
                        for t in range(NT):
                            last = dve.bn_stats(stats[:, t, :], X[:, t, :])
                        link(last)

                    @block.tensor
                    def _(pe):
                        blocks = [(k, q) for k in range(2) for q in range(QB)]
                        pe.wait_ge(asfloat, 1)
                        pe.wait_ge(steps, 2)
                        for b, (k, q) in enumerate(blocks):
                            if b >= 2:
                                pe.wait_ge(kept, b - 1)
                            pe.transpose(PS[b % 2][:, 0, 0:P], rawF[:, k, q, :], ident[:, :]).then_inc(turned, 1)
                        pe.wait_ge(loaded, 16 * n_load)
                        for b in range(NB):
                            pe.wait_ge(kept, len(blocks) + b - 1)
                            pe.transpose(PS[(len(blocks) + b) % 2][:, 0, 0:P], nat[:, b, :], ident[:, :]).then_inc(turned, 1)
                        pe.matmul(PS[2][:, 0, 0:2 * HEADS], nat[:, IL3, :], ablk, start=True, stop=True).then_inc(made, 1)
                        pe.matmul(PS[2][0:1, 1, 0:F], gcol[0:GD, :], w1g[0:GD, :], start=True, stop=True).then_inc(made, 1)
                        pe.matmul(PS[3][0:1, 0, 0:F], mb2, u1b, start=True, stop=True).then_inc(made, 1)
                        pe.matmul(PS[3][:, 1, 0:1], u1c[0:GD, :], gcol[0:GD, :], start=True, stop=True).then_inc(made, 1)
                        pe.wait_ge(kept, len(blocks) + NB)
                        pe.sem_inc(made)
                        pe.matmul(PS[0][:, 1, 0:F], w2t, u1b, start=True, stop=True).then_inc(made, 1)
                        pe.wait_ge(filled, 2)
                        pe.matmul(PS[1][:, 1, 0:NG], ones[0:1, :], base0[0:1, :], start=True, stop=True).then_inc(made, 1)
                        pe.wait_ge(filled, 3)
                        pe.transpose(PS[2][0:1, 0, 0:P], small[:, 2:3], ident[:, :]).then_inc(made, 1)
                        pe.wait_ge(filled, 4)
                        pe.matmul(PS[3][:, 0, 0:1], ones[0:1, :], small[0:1, 3:4], start=True, stop=True).then_inc(made, 1)

        def reverse_edges():
            s, sem = phase()
            with s:
                base_ready, used, hot, gate, steps, added = (sem("base_ready"), sem("groups_used"), sem("onehot_ready"),
                                                             sem("gate"), sem("vector_steps"), sem("added"))
                window = [sem(f"window_rows{k}") for k in range(2)]
                base_read = sem("base_read")
                scattered = [sem(f"scattered{q}") for q in range(NACC)]
                spread, same_ready, mixed, copied, summed, out_ready, idx_ready, taken, start = (
                    sem("sources_spread"), sem("same_ready"), sem("mixed"), sem("mixed_copied"), sem("summed"),
                    sem("rows_ready"), sem("idx_ready"), sem("rows_scattered"), sem("degrees"))
                spare = Hflat[:, NT * P:NT * P + 5120]
                hwin = work[:, 0:2 * F].rearrange("p (k f) -> p k f", k=2)
                rows_out = spare[:, 0:2048].rearrange("p (k j f) -> p k j f", k=2, j=G)
                diag = spare[:, 2048:4096].rearrange("p (k j f) -> p k j f", k=2, j=G)
                mixT = spare[:, 4096:5120].rearrange("p (j f) -> p j f", j=G)
                hot16 = work[:, 4096:5120].bitcast(bf16).rearrange("p (k j f) -> p k j f", k=2, j=G)
                same = work[:, 2304:2816].bitcast(bf16).rearrange("p (j f) -> p j f", j=G)
                lower = work[:, 2816:3328].bitcast(bf16).rearrange("p (j f) -> p j f", j=G)
                below = work[:, 3392:3392 + P // 2].bitcast(bf16)
                lead = work[:, 3328:3328 + 2 * G].rearrange("p (k j) -> p k j", k=2)
                ones16 = work[:, 5120:5120 + P // 2].bitcast(bf16)
                trash = work[:, 3584:3585]

                def halves_of(v):
                    return v.rearrange("p (q j) f -> p q (j f)", q=2)

                with nc.Block() as block:
                    @block.gpsimd
                    def _(pool):
                        pool.iota(small[:, 0:1], [[0, 1]], base=0, channel_multiplier=1,
                                  allow_small_or_imprecise_dtypes=True).then_inc(start, 1)
                        count = pool.value_load(sweeps[0:1, 0:1], min_val=1, max_val=NT)
                        pool.wait_ge(base_ready, 1)
                        for q in range(NACC):
                            pool.indirect_dma_start(T_PART[q], bass.IndirectOffsetOnAxis(ap=idx[:, 1, q:q + 1], axis=0),
                                                    rows_out[:, 1, q, :], None, compute_op=ALU.add).then_inc(scattered[q], 16)
                        pool.sem_inc(taken)
                        with pool.Fori(0, count) as sw:
                            with pool.Fori(0, PAIRS) as i:
                                for k in range(2):
                                    n = sw * NG + 2 * i + k
                                    pool.wait_ge(idx_ready, n + 1)
                                    for j in range(G):
                                        q = j % NACC
                                        if j % 4 == 0:
                                            pool.wait_ge(out_ready, 2 * n + j // 4 + 1)
                                        pool.wait_ge(scattered[q], 32 * n + 16 * (j // NACC) + 16)
                                        pool.sem_inc(gate)
                                        pool.indirect_dma_start(
                                            T_PART[q], bass.IndirectOffsetOnAxis(ap=idx[:, k, j:j + 1], axis=0),
                                            rows_out[:, k, j, :], None, compute_op=ALU.add).then_inc(scattered[q], 16)
                                        if j == NACC - 1:
                                            pool.wait_ge(scattered[q], 32 * n + 16)
                                            pool.sem_inc(taken)
                        for q in range(NACC):
                            pool.wait_ge(scattered[q], count * (32 * NG) + 16)

                    @block.sync
                    def _(sp):
                        count = sp.value_load(sweeps[0:1, 0:1], min_val=1, max_val=NT)
                        sp.sem_inc(base_read)
                        with sp.Fori(0, count) as sw:
                            sp.wait_ge(base_ready, sw + 1)
                            sp.sem_inc(gate)
                            with sp.Fori(0, PAIRS) as i:
                                for k in range(2):
                                    n = sw * NG + 2 * i + k
                                    at = sp.value_load(baseI[0:1, bass.ds(2 * i + k, 1)], min_val=0, max_val=NW - P)
                                    sp.wait_ge(used, n + 1)
                                    sp.dma_start(hwin[:, k, :], T_L0[bass.ds(at, P), :]).then_inc(window[k], 16)
                            sp.sem_inc(base_read)

                    @block.tensor
                    def _(pe):
                        count = pe.value_load(sweeps[0:1, 0:1], min_val=1, max_val=NT)
                        pe.sem_inc(used, 2)
                        with pe.Fori(0, count) as sw:
                            with pe.Fori(0, PAIRS) as i:
                                for k in range(2):
                                    n = sw * NG + 2 * i + k
                                    pe.wait_ge(hot, n + sw + 1)
                                    for j in range(G):
                                        pe.matmul(PS[1][:, j // 4, (j % 4) * P:(j % 4 + 1) * P], ones[:, :],
                                                  diag[:, k, j, :], start=True, stop=True)
                                    for j in range(G):
                                        last = pe.matmul(PS[0][:, k, 0:P], ones16, hot16[:, k, j, :],
                                                         start=j == 0, stop=j == G - 1)
                                    last.then_inc(spread, 1)
                                    pe.wait_ge(same_ready, n + 1)
                                    for j in range(G):
                                        last = pe.matmul(PS[2][:, j // 4, (j % 4) * P:(j % 4 + 1) * P], hot16[:, k, j, :],
                                                         same[:, j, :], start=True, stop=True)
                                        if j % 4 == 3:
                                            last.then_inc(mixed, 1)
                                    pe.wait_ge(window[k], 16 * (sw * PAIRS + i + 1))
                                    for j in range(G):
                                        if j % 4 == 0:
                                            pe.wait_ge(copied, 2 * n + j // 4 + 1)
                                        last = pe.matmul(PS[3][:, j // 4, (j % 4) * P:(j % 4 + 1) * P], mixT[:, j, :],
                                                         hwin[:, k, :], start=True, stop=True)
                                        if j % 4 == 3:
                                            last.then_inc(summed, 1)
                                    pe.wait_ge(summed, 2 * n + 2)
                                    pe.sem_inc(used)

                    @block.scalar
                    def _(act):
                        count = act.value_load(sweeps[0:1, 0:1], min_val=1, max_val=NT)
                        with act.Fori(0, count) as sw:
                            with act.Fori(0, PAIRS) as i:
                                for k in range(2):
                                    n = sw * NG + 2 * i + k
                                    for q in range(2):
                                        act.wait_ge(mixed, 2 * n + q + 1)
                                        act.copy(halves_of(mixT)[:, q, :], PS[2][:, q, :]).then_inc(copied, 1)
                                    act.wait_ge(taken, n + 1)
                                    for q in range(2):
                                        act.wait_ge(summed, 2 * n + q + 1)
                                        act.copy(halves_of(rows_out[:, k])[:, q, :], PS[3][:, q, :]).then_inc(out_ready, 1)

                    @block.vector
                    def _(dve):
                        link = Steps(dve, steps)
                        dve.memset(acc[:, 1, :], 0.0)
                        dve.memset(rows_out[:, 1, :, :], 0.0)
                        dve.memset(ones16, 1.0)
                        dve.wait_ge(start, 1)
                        dve.tensor_scalar(below, iota, small[:, 0:1], None, ALU.is_lt)
                        link(dve.tensor_scalar(trash, small[:, 0:1], float(NT * P), None, ALU.add))
                        dve.tensor_copy(idx[:, 1, :], trash.to_broadcast([P, G]))
                        link(dve.tensor_copy(baseF[:, :], base0[:, :]))
                        count = dve.value_load(sweeps[0:1, 0:1], min_val=1, max_val=NT)
                        at = dve.alloc_register("degree_window")
                        SPS, SPG = 5, 8
                        full = [P, G, P]

                        def one_hot(g, k):
                            link(dve.tensor_tensor(hot16[:, k], iota.unsqueeze(1).to_broadcast(full),
                                                   dl[:, bass.ds(g * G, G)].unsqueeze(2).to_broadcast(full), ALU.is_equal))
                            link(dve.tensor_tensor(diag[:, k], ident[:, :].unsqueeze(1).to_broadcast(full),
                                                   srcI[:, bass.ds(g * G, G)].unsqueeze(2).to_broadcast(full), ALU.mult))
                            dve.sem_inc(hot)

                        with dve.Fori(0, count) as sw:
                            link.at(2 + sw * (SPS + NG * SPG))
                            dve.wait_ge(base_read, sw + 1)
                            d3, s3 = (v.rearrange("p (g j) -> p g j", j=G) for v in (dl[:, 0:ET], dstF[:, :]))
                            link(dve.tensor_copy(baseI[0:1, :], baseF[0:1, :]))
                            link(dve.tensor_tensor(d3, s3, baseF[:, :].unsqueeze(2).to_broadcast([P, NG, G]), ALU.subtract))
                            link(dve.tensor_tensor(baseF[:, :], baseF[:, :], step[:, :].to_broadcast([P, NG]), ALU.add))
                            dve.sem_inc(base_ready)
                            dve.wait_ge(used, sw * NG + 1)
                            one_hot(0, 0)
                            with dve.Fori(0, PAIRS) as i:
                                for k in range(2):
                                    gi = 2 * i + k
                                    n = sw * NG + gi
                                    link.at(2 + SPS + sw * SPS + n * SPG)
                                    source = srcI[:, bass.ds(gi * G, G)]
                                    dve.load(at, baseI[0:1, bass.ds(gi, 1)])
                                    win = dve.snap(at, min_val=0, max_val=NW - P)
                                    dve.wait_ge(spread, n + 1)
                                    link(dve.tensor_tensor(same, PS[1][:, :, :].rearrange("p q (j f) -> p (q j) f", f=P),
                                                           source.unsqueeze(2).to_broadcast(full), ALU.is_equal))
                                    dve.sem_inc(same_ready)
                                    dve.wait_ge(used, n + 2)
                                    one_hot(gi + 1, 1 - k)
                                    link(dve.tensor_tensor(lower, same, below.unsqueeze(1).to_broadcast(full), ALU.mult))
                                    link(dve.tensor_reduce(lead[:, 0, :], lower, AX.X, ALU.max))
                                    link(dve.tensor_tensor(lead[:, 1, :], trash.to_broadcast([P, G]), source, ALU.subtract))
                                    link(dve.tensor_tensor(lead[:, 1, :], lead[:, 1, :], lead[:, 0, :], ALU.mult))
                                    dve.wait_ge(taken, n + 1)
                                    dve.tensor_tensor(idx[:, k, :], lead[:, 1, :], source, ALU.add).then_inc(idx_ready, 1)
                                    link(dve.tensor_tensor(acc[:, 1, bass.ds(win, P)], acc[:, 1, bass.ds(win, P)],
                                                           PS[0][:, k, 0:P], ALU.add))
                                    dve.sem_inc(gate)
                                    assert link.k == SPG

        def edges(kind, table):
            s, sem = phase()
            halves = 1 if kind in ("sum", "message") else 2
            BUFS = 4 if kind == "attention" else 2
            onehots, bufB = edge_buffers(128 if kind == "attention" else 0)
            gbuf = {"wide": g256, "attention": g132}.get(kind, g128)
            with s:
                base_ready, idx_ready, used, hot = sem("base_ready"), sem("idx_ready"), sem("groups_used"), sem("onehot_ready")
                gathered = [sem(f"gathered{k}") for k in range(BUFS)]
                side = [sem(f"side_loaded{k}") for k in range(2)]
                gate, steps, added, summed = sem("gate"), sem("vector_steps"), sem("added"), sem("summed")
                turned, copied, hidden, relu_done = sem("turned"), sem("copied"), sem("hidden"), sem("relu_done")
                read, base_read, summed32 = sem("dst_logits_read"), sem("base_read"), sem("hidden_with_rows")
                colmax, topped, largest, everywhere = (sem("lanes_largest"), sem("largest_on_one_lane"), sem("largest"),
                                                       sem("largest_on_every_lane"))
                logit, shift, weighted, scaled = sem("dst_logits"), sem("shifted"), sem("weights_ready"), sem("rescale_ready")
                turn16 = PS[2][:, 0, :].bitcast(bf16).rearrange("p (j f) -> p j f", j=G)
                pen = rcnt
                Gw = bufB

                with nc.Block() as block:
                    @block.gpsimd
                    def _(pool):
                        count = pool.value_load(sweeps[0:1, 0:1], min_val=1, max_val=NT)
                        with pool.Fori(0, count) as sw:
                            with pool.Fori(0, NG // BUFS) as i:
                                for k in range(BUFS):
                                    n = sw * NG + BUFS * i + k
                                    pool.wait_ge(idx_ready, n + BUFS * sw + 2 if kind == "attention" else n + sw + 1)
                                    pool.sem_inc(gate)
                                    for j in range(G):
                                        pool.indirect_dma_start(
                                            gbuf[:, k, j, :], None, table,
                                            bass.IndirectOffsetOnAxis(ap=idx[:, k, j:j + 1], axis=0)
                                        ).then_inc(gathered[k], 16)

                    @block.sync
                    def _(sp):
                        if kind == "message":
                            eat = edge_attr_64[0:EFULL * P, :].rearrange("(t p) c -> p t c", p=P)
                            count = sp.value_load(sweeps[0:1, 0:1], min_val=1, max_val=NT)
                            def load(n, t, k, tiles, tail):
                                sp.wait_ge(used, n + 1)
                                to = ea[:, k, :].rearrange("p (j c) -> p j c", c=ED)
                                if tiles:
                                    sp.dma_start(to[:, 0:tiles, :], eat[:, bass.ds(t, tiles), :]).then_inc(side[k], 16)
                                else:
                                    sp.sem_inc(side[k], 16)
                                if tail:
                                    sp.dma_start(to[0:ETAIL, tiles, :], edge_attr_64[EFULL * P:E, :]).then_inc(side[k], 16)
                                else:
                                    sp.sem_inc(side[k], 16)
                            with sp.Fori(0, count) as sw:
                                whole = EFULL // (2 * G)
                                with sp.Fori(0, whole) as i:
                                    for k in range(2):
                                        load(sw * NG + 2 * i + k, (2 * i + k) * G, k, G, False)
                                for g in range(2 * whole, NG):
                                    t = g * G
                                    tiles = min(G, max(0, EFULL - t))
                                    load(sw * NG + g, t, g % 2, tiles, bool(ETAIL) and tiles < G and t + tiles == EFULL)
                                sp.wait_ge(used, sw * NG + NG + 1)
                                sp.sem_inc(side[0], 32)
                                sp.wait_ge(used, sw * NG + NG + 2)
                                sp.sem_inc(gate)
                        if kind == "attention":
                            count = sp.value_load(sweeps[0:1, 0:1], min_val=1, max_val=NT)
                            sp.sem_inc(base_read)
                            with sp.Fori(0, count) as sw:
                                sp.wait_ge(base_ready, sw + 1)
                                sp.sem_inc(gate)
                                with sp.Fori(0, NG // BUFS) as i:
                                    for k in range(BUFS):
                                        n = sw * (NG + 1) + BUFS * i + k
                                        at = sp.value_load(baseI[0:1, bass.ds(BUFS * i + k, 1)], min_val=0, max_val=NW - P)
                                        sp.wait_ge(read, n + 1)
                                        sp.dma_start(dwin[:, k % 2, :], T_DST[bass.ds(at, P), :]).then_inc(side[k % 2], 16)
                                sp.wait_ge(read, sw * (NG + 1) + NG + 1)
                                sp.dma_start(dwin[:, 0, :], T_DST[0:P, :]).then_inc(side[0], 16)
                                sp.sem_inc(base_read)
                                sp.wait_ge(read, (sw + 1) * (NG + 1) + 2)
                                sp.sem_inc(gate)

                    def turn_copy(act, n):
                        act.wait_ge(turned, n + 1)
                        if kind == "message":
                            act.copy(bufB[:, 0:4, :], PS[1][:, 0, :].rearrange("p (j f) -> p j f", j=4)).then_inc(copied, 1)
                        else:
                            act.copy(hotT, turn16).then_inc(copied, 1)

                    @block.scalar
                    def _(act):
                        count = act.value_load(sweeps[0:1, 0:1], min_val=1, max_val=NT)
                        with act.Fori(0, count) as sw:
                            if kind != "attention":
                                if kind == "message":
                                    act.wait_ge(summed32, sw * (2 * NG) + 1)
                                else:
                                    act.wait_ge(used, sw * NG + 2)
                                act.copy(idx[:, 0, :], srcI[:, 0:G]).then_inc(idx_ready, 1)
                            if kind in ("message", "attention"):
                                turn_copy(act, sw * (NG + 1))
                            with act.Fori(0, NG // BUFS) as i:
                                for k in range(BUFS):
                                    n = sw * NG + BUFS * i + k
                                    if kind != "attention":
                                        if kind == "message":
                                            act.wait_ge(summed32, 2 * n + 1)
                                        else:
                                            act.wait_ge(used, n + 2)
                                        act.copy(idx[:, 1 - k, :], srcI[:, bass.ds((BUFS * i + k + 1) * G, G)]
                                                 ).then_inc(idx_ready, 1)
                                    if kind in ("sum", "wide"):
                                        continue
                                    if kind == "message":
                                        turn_copy(act, n + sw + 1)
                                        for q in range(2):
                                            act.wait_ge(summed32, 2 * n + q + 2)
                                            act.activation(bufA[:, 4 * q:4 * q + 4, :], bufA[:, 4 * q:4 * q + 4, :],
                                                           ACT.Relu).then_inc(relu_done, 1)
                                    else:
                                        turn_copy(act, n + sw + 1)
                                        act.wait_ge(shift, n + 1)
                                        act.wait_ge(used, n + 1)
                                        act.activation(lg[:, 2 + k % 2, :], lg[:, 0, :], ACT.Exp).then_inc(weighted, 1)
                                        act.activation(winF[:, k % 2, :], winF[:, k % 2, :], ACT.Exp).then_inc(scaled, 1)
                            if kind != "attention":
                                act.wait_ge(idx_ready, (sw + 1) * (NG + 1))
                                act.sem_inc(gate)

                    def turn_one_hot(pe, n, sw):
                        pe.wait_ge(hot, n + sw + 1)
                        for j in range(G):
                            last = pe.transpose(turn16[:, j, :], hot16a[:, j, :], ident16)
                        last.then_inc(turned, 1)

                    def dst_logits(pe, n, k, m):
                        pe.wait_ge(side[k], 16 * (m + 1))
                        pe.wait_ge(copied, n + 1)
                        for j in range(G):
                            last = pe.matmul(PS[1][:, 0, DW * j:DW * (j + 1)], hotT[:, j, :],
                                             dwin[:, k, :], start=True, stop=True)
                        last.then_inc(logit, 1)
                        pe.wait_ge(logit, n + 1)
                        pe.sem_inc(read)

                    def turn_features(pe, n, k, m):
                        pe.wait_ge(side[k], 32 * (m + 1))
                        pe.wait_ge(copied, n + 1)
                        for q in range(4):
                            last = pe.transpose(PS[1][:, 0, q * P:(q + 1) * P], ea[:, k, q * P:(q + 1) * P], ident[:, :])
                        last.then_inc(turned, 1)

                    @block.tensor
                    def _(pe):
                        count = pe.value_load(sweeps[0:1, 0:1], min_val=1, max_val=NT)
                        pe.sem_inc(read, 2)
                        pe.sem_inc(used, 1 if kind == "attention" else 2)
                        if kind == "message":
                            pe.sem_inc(copied)
                        with pe.Fori(0, count) as sw:
                            if kind == "attention":
                                turn_one_hot(pe, sw * (NG + 1), sw)
                                dst_logits(pe, sw * (NG + 1), 0, sw * (PAIRS + 1))
                            if kind == "message":
                                turn_features(pe, sw * (NG + 1), 0, sw * (PAIRS + 1))
                            with pe.Fori(0, NG // BUFS) as i:
                                for k in range(BUFS):
                                    n = sw * NG + BUFS * i + k
                                    ahead = (n + sw + 1, (k + 1) % 2, sw * (PAIRS + k % 2) + BUFS // 2 * i + (k + 1) // 2)
                                    k2 = k % 2
                                    A, B = PS[3 * k2][:, 0, 0:P], PS[3 * k2][:, 1, 0:P]
                                    onehot = onehots[k2]
                                    if kind == "attention":
                                        turn_one_hot(pe, ahead[0], sw)
                                        pe.wait_ge(colmax, n + 1)
                                        pe.transpose(PS[1][0:1, 1, 0:P], small[:, 0:1], ident[:, :]).then_inc(topped, 1)
                                        pe.wait_ge(largest, n + 1)
                                        pe.matmul(PS[1][:, 1, P:P + 1], ones[0:1, :], small[0:1, 1:2],
                                                  start=True, stop=True).then_inc(everywhere, 1)
                                        dst_logits(pe, *ahead)
                                        pe.wait_ge(added, n + 1)
                                        pe.wait_ge(weighted, n + 1)
                                        for j in range(G):
                                            pe.matmul(B[0:HEADS], lg[:, 2 + k2, HEADS * j:HEADS * (j + 1)], onehot[:, j, :],
                                                      start=j == 0, stop=j == G - 1)
                                        pe.wait_ge(summed, n + 1)
                                        for j in range(G):
                                            last = pe.matmul(A, Gw[:, j, :], onehot[:, j, :], start=j == 0, stop=j == G - 1)
                                        last.then_inc(used, 1)
                                        continue
                                    pe.wait_ge(hot, n + sw + 1)
                                    if kind != "message":
                                        pe.wait_ge(gathered[k], (G * 16) * (sw * (NG // BUFS) + i + 1))
                                    lhs = gbuf[:, k]
                                    if kind == "message":
                                        pe.wait_ge(copied, n + sw + 2)
                                        for j in range(G):
                                            last = pe.matmul(PS[2][:, j // 4, (j % 4) * P:(j % 4 + 1) * P], bufB[:, j // 2, :],
                                                             W("m1b" if j % 2 else "m1a"), start=True, stop=True)
                                            if j % 4 == 3:
                                                last.then_inc(hidden, 1)
                                        pe.wait_ge(hidden, 2 * n + 2)
                                        turn_features(pe, *ahead)
                                        lhs = bufA
                                    pe.wait_ge(added, n + 1)
                                    for j in range(G):
                                        if kind == "message" and j % 4 == 0:
                                            pe.wait_ge(relu_done, 2 * n + j // 4 + 1)
                                        last = pe.matmul(A, lhs[:, j, 0:P], onehot[:, j, :], start=j == 0, stop=j == G - 1)
                                        if halves == 2:
                                            last = pe.matmul(B, gbuf[:, k, j, P:2 * P], onehot[:, j, :],
                                                             start=j == 0, stop=j == G - 1)
                                    last.then_inc(used, 1)

                    @block.vector
                    def _(dve):
                        link = Steps(dve, steps)
                        late = kind == "attention"
                        dve.memset(acc[:, 0:halves, :], 0.0)
                        if late:
                            dve.memset(scol, FAR)
                            dve.memset(small[:, 2:3], FAR)
                            dve.memset(PS[3][:, :, 0:P], 0.0)
                            dve.memset(PS[0][:, 1, 0:P], 0.0)
                            dve.memset(winF[:, 1, :], 1.0)
                            dve.memset(lg[:, 3, :], 0.0)
                            dve.memset(onehots[1], 0.0)
                            dve.tensor_copy(ident16, ident[:, :])
                        link(dve.tensor_copy(baseF[:, :], base0[:, :]))
                        dve.sem_inc(added, 1 if late else 2)
                        if late:
                            dve.sem_inc(idx_ready)
                        dve.sem_inc(summed32)
                        count = dve.value_load(sweeps[0:1, 0:1], min_val=1, max_val=NT)
                        at = dve.alloc_register(f"window_{phase.n}")
                        before = dve.alloc_register(f"window_before_{phase.n}")
                        dve.reg_mov(at, 0)
                        SPS = 3 + (6 if late else 0)
                        SPG = 10 if late else 1
                        with dve.Fori(0, count) as sw:
                            link.at(1 + sw * (SPS + NG * SPG))
                            if late:
                                dve.wait_ge(base_read, sw + 1)
                            d3, s3 = (v.rearrange("p (g j) -> p g j", j=G) for v in (dl[:, 0:ET], dstF[:, :]))
                            link(dve.tensor_copy(baseI[0:1, :], baseF[0:1, :]))
                            link(dve.tensor_tensor(d3, s3, baseF[:, :].unsqueeze(2).to_broadcast([P, NG, G]), ALU.subtract))
                            if late:
                                link(dve.tensor_scalar(pen[:, 0:ET], dl[:, 0:ET], 0.0, None, ALU.is_ge))
                                link(dve.scalar_tensor_tensor(out=pen[:, 0:ET], in0=dl[:, 0:ET], scalar=float(P - 1),
                                                              in1=pen[:, 0:ET], op0=ALU.is_le, op1=ALU.mult))
                                link(dve.tensor_scalar(pen[:, 0:ET], pen[:, 0:ET], -FAR, FAR, ALU.mult, ALU.add))
                            link(dve.tensor_tensor(baseF[:, :], baseF[:, :], step[:, :].to_broadcast([P, NG]), ALU.add))
                            dve.sem_inc(base_ready)

                            def one_hot(g, to, half=None):
                                m, at = (G, 0) if half is None else (G // 2, half * (G // 2))
                                return dve.tensor_tensor(to[:, at:at + m, :], iota.unsqueeze(1).to_broadcast([P, m, P]),
                                                         dl[:, bass.ds(g * G + at, m)].unsqueeze(2).to_broadcast([P, m, P]),
                                                         ALU.is_equal)

                            if late:
                                dve.wait_ge(read, sw * (NG + 1) + 2)
                            else:
                                dve.wait_ge(used, sw * NG + 1)
                            if late:
                                dve.wait_ge(idx_ready, sw * (NG + BUFS) + 1)
                                for k in range(BUFS):
                                    dve.tensor_copy(idx[:, k, :], srcI[:, k * G:(k + 1) * G]).then_inc(idx_ready, 1)
                                link(one_hot(0, onehots[0]))
                                link(one_hot(0, hot16a))
                                dve.sem_inc(hot)
                                dve.wait_ge(turned, sw * (NG + 1) + 1)
                                link(one_hot(1, hot16a))
                                dve.sem_inc(hot)
                            else:
                                one_hot(0, onehots[0]).then_inc(hot, 1)
                            with dve.Fori(0, NG // BUFS) as i:
                                for k in range(BUFS):
                                    n = sw * NG + BUFS * i + k
                                    link.at(1 + SPS + sw * SPS + n * SPG)
                                    gi = BUFS * i + k
                                    if late:
                                        dve.reg_mov(before, at)
                                        last_win = dve.snap(before, min_val=0, max_val=NW - P)
                                    dve.load(at, baseI[0:1, bass.ds(gi, 1)])
                                    win = dve.snap(at, min_val=0, max_val=NW - P)
                                    if late:
                                        L = lg[:, 0, :].rearrange("p (j h) -> p j h", h=HEADS)
                                        dve.wait_ge(gathered[k], (G * 16) * (sw * (NG // BUFS) + i + 1))
                                        dve.wait_ge(logit, n + sw + 1)
                                        D = PS[1][:, 0, 0:G * DW].rearrange("p (j q h) -> p j h q", q=3, h=HEADS)
                                        L2 = lg[:, 1, :].rearrange("p (j h) -> p j h", h=HEADS)
                                        link(dve.tensor_reduce(L2, D, AX.X, ALU.add))
                                        link(dve.tensor_tensor(L, gbuf[:, k, :, F:TW], L2, ALU.add))
                                        link(dve.scalar_tensor_tensor(out=lg[:, 1, :], in0=lg[:, 0, :], scalar=SLOPE,
                                                                      in1=lg[:, 0, :], op0=ALU.mult, op1=ALU.max))
                                        link(dve.tensor_tensor(
                                            L, L2, pen[:, bass.ds(gi * G, G)].unsqueeze(2).to_broadcast([P, G, HEADS]), ALU.add))
                                        link(dve.tensor_reduce(small[:, 3:4], lg[:, 0, :], AX.X, ALU.max))
                                        dve.tensor_tensor(small[:, 0:1], small[:, 3:4], small[:, 2:3], ALU.max).then_inc(colmax, 1)
                                        dve.wait_ge(used, n + 1)
                                        one_hot(gi + 1, onehots[1 - k % 2], 0)
                                        dve.wait_ge(topped, n + 1)
                                        dve.tensor_reduce(small[0:1, 1:2], PS[1][0:1, 1, 0:P], AX.X, ALU.max).then_inc(largest, 1)
                                        one_hot(gi + 1, onehots[1 - k % 2], 1)
                                        dve.wait_ge(everywhere, n + 1)
                                        link(dve.tensor_copy(small[:, 2:3], PS[1][:, 1, P:P + 1]))
                                        dve.tensor_scalar(lg[:, 0, :], lg[:, 0, :], small[:, 2:3], None, ALU.subtract)
                                        dve.tensor_scalar(winF[:, k % 2, :], scol[:, bass.ds(win, P)], small[:, 2:3], None,
                                                          ALU.subtract).then_inc(shift, 1)
                                        dve.wait_ge(turned, n + sw + 2)
                                        one_hot(gi + 2, hot16a, 0)
                                        dve.wait_ge(shift, n + 1)
                                        dve.tensor_scalar(scol[:, bass.ds(win, P)], iota, 0.0, small[:, 2:3],
                                                          ALU.mult, ALU.add)
                                        dve.wait_ge(weighted, n + 1)
                                        link(dve.tensor_tensor(Gw.rearrange("p j (h f) -> p (j h) f", f=HF),
                                                               gbuf[:, k, :, 0:F].rearrange("p j (h f) -> p j h f", f=HF),
                                                               lg[:, 2 + k % 2, :].unsqueeze(2).to_broadcast([P, G * HEADS, HF]),
                                                               ALU.mult))
                                        dve.sem_inc(summed)
                                        dve.tensor_copy(idx[:, k, :], srcI[:, bass.ds((gi + BUFS) * G, G)]).then_inc(idx_ready, 1)
                                        link(one_hot(gi + 2, hot16a, 1))
                                        dve.sem_inc(hot)
                                        dve.wait_ge(scaled, n + 1)
                                        link(dve.tensor_tensor(acc[:, :, bass.ds(last_win, P)], acc[:, :, bass.ds(last_win, P)],
                                                               winF[:, 1 - k % 2, :].unsqueeze(1).to_broadcast([P, 2, P]), ALU.mult))
                                        link(dve.tensor_tensor(acc[:, :, bass.ds(last_win, P)], acc[:, :, bass.ds(last_win, P)],
                                                               PS[3 - 3 * (k % 2)][:, :, 0:P], ALU.add))
                                        dve.sem_inc(added)
                                    else:
                                        dve.wait_ge(used, n + 2)
                                        one_hot(gi + 1, onehots[1 - k % 2]).then_inc(hot, 1)
                                        if kind == "message":
                                            for q in range(2):
                                                dve.wait_ge(gathered[k], (G * 16) * (sw * (NG // BUFS) + i + 1))
                                                dve.wait_ge(hidden, 2 * n + q + 1)
                                                dve.tensor_tensor(bufA[:, 4 * q:4 * q + 4, :], gbuf[:, k, 4 * q:4 * q + 4, :],
                                                                  PS[2][:, q, :].rearrange("p (j f) -> p j f", j=4),
                                                                  ALU.add).then_inc(summed32, 1)
                                        dve.wait_ge(used, n + 3)
                                        link(dve.tensor_tensor(acc[:, 0:halves, bass.ds(win, P)], acc[:, 0:halves, bass.ds(win, P)],
                                                               PS[3 * (k % 2)][:, 0:halves, 0:P], ALU.add))
                                        dve.sem_inc(added)
                                    assert link.k == SPG
                        if late:
                            link.at(1 + count * (SPS + NG * SPG))
                            win = dve.snap(at, min_val=0, max_val=NW - P)
                            dve.wait_ge(used, count * NG + 1)
                            link(dve.tensor_tensor(acc[:, :, bass.ds(win, P)], acc[:, :, bass.ds(win, P)],
                                                   winF[:, 1, :].unsqueeze(1).to_broadcast([P, 2, P]), ALU.mult))
                            link(dve.tensor_tensor(acc[:, :, bass.ds(win, P)], acc[:, :, bass.ds(win, P)],
                                                   PS[3][:, :, 0:P], ALU.add))
                            dve.sem_inc(gate)

        def moments():
            s, sem = phase()
            with s:
                steps, var, root = sem("vector_steps"), sem("var"), sem("root")
                me, mo = stats[:, :, 1], stats[:, :, 4]
                with nc.Block() as block:
                    @block.vector
                    def _(dve):
                        link = Steps(dve, steps)
                        mean, dif, r, nb, v = (ln[:, q, :] for q in range(5))
                        dve.tensor_tensor(mean, me, mo, ALU.add)
                        dve.tensor_tensor(dif, me, mo, ALU.subtract)
                        link(dve.tensor_tensor(v, stats[:, :, 2], stats[:, :, 5], ALU.add))
                        dve.tensor_scalar(mean, mean, 0.5, None, ALU.mult)
                        link(dve.tensor_tensor(dif, dif, dif, ALU.mult))
                        link(dve.tensor_scalar(dif, dif, 0.25, None, ALU.mult))
                        link(dve.scalar_tensor_tensor(out=v, in0=v, scalar=1.0 / F, in1=dif, op0=ALU.mult, op1=ALU.add))
                        dve.sem_inc(var)
                        dve.wait_ge(root, 1)
                        link(dve.reciprocal(r, r))
                        link(dve.scalar_tensor_tensor(out=nb, in0=mean, scalar=-1.0, in1=r, op0=ALU.mult, op1=ALU.mult))

                    @block.scalar
                    def _(act):
                        act.wait_ge(var, 1)
                        act.activation(ln[:, 2, :], ln[:, 4, :], ACT.Sqrt, bias=cols[:, EPSC:EPSC + 1]).then_inc(root, 1)

        def normalise(kind, table):
            moments()
            s, sem = phase()
            with s:
                normed, turned, copied, proj, evac = sem("normed"), sem("turned"), sem("copied"), sem("proj"), sem("evac")
                moved, parted, steps, gate = sem("moved"), sem("parted"), sem("vector_steps"), sem("gate")
                split = work[:, 5376:5376 + U * DW // 2].bitcast(bf16).rearrange("p (a c) -> p a c", a=U)
                stored = [sem(f"stored{h}") for h in range(2)]
                stored2 = [sem("stored_dst_logits")]
                width = {"plain": F, "message": F, "attention": TW}[kind]
                tall = kind != "plain"
                with nc.Block() as block:
                    @block.scalar
                    def _(act):
                        def norm(t, a):
                            after(act, turned, t + 1 - U)
                            if kind == "plain" and not (isinstance(t, int) and t < U):
                                act.wait_ge(stored[a // 4], (t - a) // U * 16)
                            act.activation(hn[:, a, :], X[:, bass.ds(t, 1), :].rearrange("p o f -> p (o f)"), ACT.Relu,
                                           bias=ln[:, 3, bass.ds(t, 1)], scale=ln[:, 2, bass.ds(t, 1)]
                                           ).then_inc(normed, 1)
                        pipelined(act, NI, U, norm)

                    @block.gpsimd
                    def _(pool):
                        def keep(t, a):
                            pool.wait_ge(copied, t + 1)
                            pool.sem_inc(gate)
                            pool.tensor_copy(Hbuf[:, 0, bass.ds(t * P, P)], hs[:, a, :]).then_inc(moved, 1)
                        if kind == "message":
                            pipelined(pool, NI, U, keep)

                    def bank_free(eng, sem, t, a):
                        after(eng, sem, t - 2 if a < 3 else t - 3)

                    @block.tensor
                    def _(pe):
                        def turn(t, a):
                            pe.wait_ge(normed, t + 1)
                            bank_free(pe, copied, t, a)
                            pe.transpose(PS[a % 4][:, 0, 0:P], hn[:, a, :], ident[:, :]).then_inc(turned, 1)
                        def project(t, a):
                            pe.wait_ge(copied, t + 1)
                            bank_free(pe, evac, t, a)
                            if kind == "message":
                                to = PS[a % 4][:, 1, 0:F]
                                pe.matmul(to, hs[:, a, :], W("m1n"), start=True, stop=False)
                                pe.matmul(to, ones[0:1, :], rows[0:1, 0, :], start=False, stop=True).then_inc(proj, 1)
                            else:
                                pe.matmul(PS[a % 4][:, 1, 0:F + 2 * HEADS], hs[:, a, :], wext[:, :],
                                          start=True, stop=True).then_inc(proj, 1)
                        pipelined(pe, NI, U, turn, None, *([project] if tall else []))

                    @block.vector
                    def _(dve):
                        link = Steps(dve, steps)
                        def take(t, a):
                            dve.wait_ge(turned, t + 1)
                            if tall:
                                after(dve, proj, t + 1 - U)
                                if kind == "message":
                                    after(dve, moved, t + 1 - U)
                                dve.tensor_copy(hs[:, a, :], PS[a % 4][:, 0, 0:P]).then_inc(copied, 1)
                            else:
                                dve.tensor_copy(Hbuf[:, 0, bass.ds(t * P, P)], PS[a % 4][:, 0, 0:P]).then_inc(copied, 1)

                        def out(i, a):
                            t = i * U + a
                            dve.wait_ge(proj, t + 1)
                            after(dve, stored[a // 4], i * 16)
                            if kind == "attention":
                                after(dve, stored2[0], i * 16)
                            w = F if kind == "message" else F + 2 * HEADS
                            dve.tensor_copy(nm[:, a, 0:w], PS[a % 4][:, 1, 0:w]).then_inc(evac, 1)

                        for i in iterations(dve, NI):
                            for a in range(U):
                                take(i * U + a, a)
                                if tall and a >= 2:
                                    out(i, a - 2)
                            if tall:
                                out(i, U - 2)
                                out(i, U - 1)
                            if kind == "attention":
                                link.at(i * 4)
                                D, D16 = nm[:, :, TW:TW + HEADS], split[:, :, :]
                                dve.wait_ge(evac, i * U + U)
                                link(dve.tensor_copy(D16[:, :, 0:HEADS], D))
                                link(dve.tensor_tensor(D, D, D16[:, :, 0:HEADS], ALU.subtract))
                                link(dve.tensor_copy(D16[:, :, HEADS:2 * HEADS], D))
                                link(dve.tensor_tensor(D, D, D16[:, :, HEADS:2 * HEADS], ALU.subtract))
                                dve.tensor_copy(D16[:, :, 2 * HEADS:DW], D).then_inc(parted, 1)

                    @block.sync
                    def _(sp):
                        for i in iterations(sp, NI):
                            for h, (lo, hi) in enumerate(PORTIONS):
                                sp.wait_ge(normed if kind == "plain" else evac, i * U + hi)
                                of = hn[:, lo:hi, :] if kind == "plain" else nm[:, lo:hi, 0:width]
                                sp.dma_start(table[bass.ds((i * U + lo) * P, (hi - lo) * P), :].rearrange(
                                    "(a p) c -> p a c", p=P), of).then_inc(stored[h], 16)
                            if kind == "attention":
                                sp.wait_ge(parted, i + 1)
                                sp.dma_start(T_DST[bass.ds(i * (U * P), U * P), :].rearrange("(a p) c -> p a c", p=P),
                                             split[:, :, :]).then_inc(stored2[0], 16)
                        for h in range(2):
                            sp.wait_ge(stored[h], 16 * NI)
                        if kind == "attention":
                            sp.wait_ge(stored2[0], 16 * NI)

        def nodes(kind):
            s, sem = phase()
            with s:
                bias_loaded = sem("bias_loaded")
                gate, count_r = sem("gate"), [sem("degrees_at_least_one"), sem("degrees_inverted")]
                meaned, dense, act1, dense2, act2, turned, taken, moved, steps = (
                    sem("meaned"), sem("dense"), sem("act1"), sem("dense2"), sem("act2"), sem("turned"), sem("taken"),
                    sem("moved"), sem("vector_steps"))
                stored = [sem(f"stored{a}") for a in range(U)]
                sel = work[0:HEADS, 7168:7168 + F]
                parts = work[:, 3584:7168].rearrange("p (a q f) -> p a q f", a=U, q=NACC)
                outs = {"conv1": 2, "conv2": 2}.get(kind, 1)
                width = {"conv1": 2 * F, "conv2": F}.get(kind, 0)
                table = {"conv1": T_C2, "conv2": T_C3}.get(kind)
                hasdense = kind in ("l0", "conv1", "conv2", "update")
                terms = {
                    "l0": [[("l0x", (Hbuf, 0))]],
                    "conv1": [[(f"c1l0{o}", (acc, 0)), (f"c1r0{o}", (Hbuf, 0))] for o in range(2)],
                    "conv2": [[(f"c2l{q}{o}", (acc, q)) for q in range(2)] + [(f"c2r{q}{o}", (Hbuf, q)) for q in range(2)]
                              for o in range(2)],
                    "update": [[("w2u", (acc, 0)), ("u1h", (Hbuf, 0))]],
                }.get(kind)
                bias = {"l0": [B0], "conv1": [B1, B1 + 1], "conv2": [B2, B2 + 1], "update": [CU]}.get(kind)
                with nc.Block() as block:
                    @block.vector
                    def _(dve):
                        link = Steps(dve, steps)
                        if kind in ("conv1", "update"):
                            link(dve.tensor_tensor(acc[:, 0, :], acc[:, 0, :], rcnt[:, :], ALU.mult))
                            if kind == "update":
                                link(dve.tensor_scalar(acc[0:1, 1, :], rcnt[0:1, :], 0.0, None, ALU.is_gt))
                        if kind == "conv2":
                            for q in range(2):
                                link(dve.tensor_tensor(acc[:, q, :], acc[:, q, :], rcnt[:, :], ALU.mult))
                        if kind == "final":
                            dve.tensor_copy(sel.rearrange("p (h f) -> p h f", h=HEADS),
                                            ident[0:HEADS, 0:HEADS].unsqueeze(2).to_broadcast([HEADS, HEADS, HF]))
                            link(dve.tensor_scalar(scol, scol, small[:, 2:3], None, ALU.subtract))
                            dve.sem_inc(meaned)
                            dve.wait_ge(act1, 1)
                            for q, p in ((1, HEADS), (0, P)):
                                link(dve.tensor_tensor(acc[0:p, q, :], acc[0:p, q, :], scol[0:p, :], ALU.mult))
                            link(dve.tensor_scalar(acc[0:HEADS, 1, :], acc[0:HEADS, 1, :], ATT_EPS, None, ALU.add))
                            link(dve.reciprocal(acc[0:HEADS, 1, :], acc[0:HEADS, 1, :]))
                        dve.sem_inc(meaned)

                        def mult(t, a):
                            after(dve, turned, t + 3 - U)
                            if kind == "final":
                                dve.wait_ge(dense, t + 1)
                            other = rcnt[:, bass.ds(t * P, P)] if kind == "conv3" else PS[a % 2][:, a // 2 % 2, 0:P]
                            dve.tensor_tensor(st[:, a, 0, :], acc[:, 0, bass.ds(t * P, P)], other, ALU.mult).then_inc(act1, 1)

                        def take(t, a):
                            bank = PS[2 + a % 2]
                            dve.wait_ge(turned, t + 1)
                            if kind in ("l0", "final"):
                                Xt = tile_of(X, t)
                                dve.tensor_tensor(Xt, Xt, bank[:, 0, 0:F], ALU.add).then_inc(taken, 1)
                            elif kind == "conv3":
                                after(dve, moved, t + 3 - U)
                                dve.tensor_tensor(tmp[:, a, :], bank[:, 0, 0:F], Hbuf[:, 0, bass.ds(t * P, P)],
                                                  ALU.add).then_inc(taken, 1)
                            elif kind == "update":
                                dve.tensor_copy(Hbuf[:, 1, bass.ds(t * P, P)], bank[:, 0, 0:F]).then_inc(taken, 1)
                            else:
                                if not (isinstance(t, int) and t < U):
                                    dve.wait_ge(stored[a], (t - a) // U * 16)
                                dve.tensor_copy(nm[:, a, 0:width], bank[:, 0, 0:width]).then_inc(taken, 1)
                                if kind == "conv2":
                                    dve.tensor_tensor(Hbuf[:, 0, bass.ds(t * P, P)], bank[:, 1, 0:F], gamma,
                                                      ALU.add).then_inc(moved, 1)

                        def into_x(t, a):
                            dve.wait_ge(taken, t + 1)
                            Xt = tile_of(X, t)
                            dve.scalar_tensor_tensor(out=Xt, in0=tmp[:, a, :], scalar=0.0, in1=Xt, op0=ALU.max,
                                                     op1=ALU.add).then_inc(moved, 1)

                        def measure(t, a):
                            dve.wait_ge(moved if kind == "conv3" else taken, t + 1)
                            of = Hbuf[:, 1, bass.ds(t * P, P)] if kind == "update" else tile_of(X, t)
                            dve.bn_stats(tile_of(stats, t), of)

                        def at_least_one(t, a):
                            dve.tensor_scalar(rcnt[:, bass.ds(t * P, P)], acc[:, 1, bass.ds(t * P, P)], 1.0, None,
                                              ALU.max).then_inc(count_r[0], 1)

                        def inverse(t, a):
                            dve.wait_ge(count_r[0], t + 1)
                            dve.sem_inc(gate)
                            dve.reciprocal(rcnt[:, bass.ds(t * P, P)], rcnt[:, bass.ds(t * P, P)]).then_inc(count_r[1], 1)

                        def or_none(t, a):
                            dve.wait_ge(count_r[1], t + 1)
                            dve.scalar_tensor_tensor(out=rcnt[:, bass.ds(t * P, P)], in0=acc[:, 1, bass.ds(t * P, P)],
                                                     scalar=0.5, in1=rcnt[:, bass.ds(t * P, P)], op0=ALU.is_ge, op1=ALU.mult)

                        def take_and_count(t, a):
                            take(t, a)
                            at_least_one(t, a)

                        def measure_and_invert(t, a):
                            measure(t, a)
                            inverse(t, a)

                        if kind == "conv2":
                            dve.wait_ge(bias_loaded, 16)
                        if kind == "l0":
                            dve.memset(rcnt[:, NT * P:NW], 0.0)
                        pipelined(dve, NI, U, *{"l0": (take_and_count, measure_and_invert, or_none), "update": (take, measure), "final": (mult, None, take),
                                                "conv3": (mult, None, take, into_x, measure)}.get(kind, (take,)))

                    @block.scalar
                    def _(act):
                        if kind == "final":
                            act.wait_ge(meaned, 1)
                            act.activation(scol, scol, ACT.Exp).then_inc(act1, 1)

                        def parts_kept(t, a):
                            act.wait_ge(dense2, t + 1)
                            after(act, dense, t + 2 - U)
                            act.copy(st[:, a, 1, :], PS[a % 2][:, 1, 0:P]).then_inc(act2, 1)

                        def relu(t, a):
                            act.wait_ge(dense, t + 1)
                            after(act, turned, t + 4 - U)
                            if kind == "conv1":
                                after(act, moved, t + 2 - U)
                            for o in range(outs):
                                last = act.activation(st[:, a, o, :], PS[a % 2][:, o, 0:P], ACT.Relu,
                                                      bias=cols[:, bias[o]:bias[o] + 1])
                            last.then_inc(act1, 1)

                        def updated(t, a):
                            act.wait_ge(dense2, t + 1)
                            after(act, turned, t + 4 - U)
                            act.activation(st[:, a, 1, :], PS[a % 2][:, 1, 0:P], ACT.Identity,
                                           bias=cols[:, UB2:UB2 + 1]).then_inc(act2, 1)

                        if hasdense:
                            pipelined(act, NI, U, *{"l0": (parts_kept, relu), "update": (relu, updated)}.get(kind, (relu,)))

                    @block.gpsimd
                    def _(pool):
                        def replace(t, a):
                            pool.wait_ge(act1, t + 1)
                            pool.sem_inc(gate)
                            pool.tensor_copy(Hbuf[:, :, bass.ds(t * P, P)], st[:, a, :, :]).then_inc(moved, 1)
                        if kind == "conv1":
                            pipelined(pool, NI, U, replace)

                    @block.sync
                    def _(sp):
                        def load_parts(i, h):
                            lo, hi = PORTIONS[h]
                            after(sp, dense2, i * U + hi - U)
                            for q in range(NACC):
                                sp.dma_start(parts[:, lo:hi, q, :], T_PART[q][bass.ds((i * U + lo) * P, (hi - lo) * P), :]
                                             .rearrange("(a p) f -> p a f", p=P)).then_inc(stored[h], 16)

                        def store(t, a):
                            sp.wait_ge(taken, t + 1)
                            sp.dma_start(table[bass.ds(t * P, P), :], nm[:, a, 0:width]).then_inc(stored[a], 16)

                        if kind == "l0":
                            for i in iterations(sp, NI):
                                for h in range(2):
                                    load_parts(i, h)
                        if kind == "conv2":
                            sp.dma_start(gamma, L1_gnn_b3.rearrange("(o f) -> o f", o=1).to_broadcast([P, F])
                                         ).then_inc(bias_loaded, 16)
                        if width:
                            pipelined(sp, NI, U, store)
                            for a in range(U):
                                sp.wait_ge(stored[a], 16 * NI)

                    def bank_free(eng, sem, t, a):
                        after(eng, sem, t if a == 0 else t - 1)

                    @block.tensor
                    def _(pe):
                        def sum_parts(t, a):
                            pe.wait_ge(stored[a // 4], ((t - a) // U + 1) * (16 * NACC))
                            bank_free(pe, act2, t, a)
                            for q in range(NACC):
                                last = pe.matmul(PS[a % 2][:, 1, 0:P], parts[:, a, q, :], ident[:, :],
                                                 start=q == 0, stop=q == NACC - 1)
                            last.then_inc(dense2, 1)

                        def layer(t, a):
                            bank_free(pe, act1, t, a)
                            for o in range(outs):
                                for q, (w, (buf, half)) in enumerate(terms[o]):
                                    end = q == len(terms[o]) - 1 and kind not in ("update", "l0")
                                    last = pe.matmul(PS[a % 2][:, o, 0:P], W(w), buf[:, half, bass.ds(t * P, P)],
                                                     start=q == 0, stop=end)
                            if kind == "l0":
                                pe.wait_ge(act2, t + 1)
                                last = pe.matmul(PS[a % 2][:, 0, 0:P], W("l0a"), st[:, a, 1, :], start=False, stop=True)
                            if kind == "update":
                                last = pe.matmul(PS[a % 2][:, 0, 0:P], rows[0:1, 1, :], acc[0:1, 1, bass.ds(t * P, P)],
                                                 start=False, stop=True)
                            last.then_inc(dense, 1)

                        def second_layer(t, a):
                            pe.wait_ge(act1, t + 1)
                            bank_free(pe, act2, t, a)
                            pe.matmul(PS[a % 2][:, 1, 0:P], W("u2"), st[:, a, 0, :], start=True, stop=False)
                            pe.matmul(PS[a % 2][:, 1, 0:P], ident[:, :], Hbuf[:, 0, bass.ds(t * P, P)],
                                      start=False, stop=True).then_inc(dense2, 1)

                        def denominators(t, a):
                            after(pe, act1, t - 1 if a < 3 else t - 2)
                            pe.matmul(PS[a % 2][:, a // 2 % 2, 0:P], sel, acc[0:HEADS, 1, bass.ds(t * P, P)],
                                      start=True, stop=True).then_inc(dense, 1)

                        def back(t, a):
                            pe.wait_ge(act2 if kind == "update" else act1, t + 1 + (kind == "final"))
                            bank_free(pe, taken, t, a)
                            if kind == "conv2":
                                bank_free(pe, moved, t, a)
                            to = PS[2 + a % 2]
                            if kind == "conv2":
                                for q in range(2):
                                    pe.matmul(to[:, 0, 0:F], st[:, a, q, :], W(f"c3l{q}0"), start=q == 0, stop=q == 1)
                                for q in range(2):
                                    last = pe.matmul(to[:, 1, 0:F], st[:, a, q, :], W(f"c3r{q}0"), start=q == 0, stop=q == 1)
                            elif kind == "conv1":
                                for q in range(2):
                                    last = pe.transpose(to[:, 0, q * P:(q + 1) * P], st[:, a, q, :], ident[:, :])
                            else:
                                last = pe.transpose(to[:, 0, 0:P], st[:, a, int(kind == "update"), :], ident[:, :])
                            last.then_inc(turned, 1)

                        pe.wait_ge(meaned, 2 if kind == "final" else 1)
                        pipelined(pe, NI, U, *{"l0": (sum_parts, layer, back), "update": (layer, second_layer, back),
                                               "conv3": (back,), "final": (denominators, back)}.get(kind, (layer, back)))

        def add_update():
            moments()
            s, sem = phase()
            with s:
                loaded, z, steps = sem("loaded"), sem("z"), sem("vector_steps")
                with nc.Block() as block:
                    @block.sync
                    def _(sp):
                        for to, v in ((gamma, L2_gnn_ln_gamma), (beta, L2_gnn_ln_beta)):
                            sp.dma_start(to, v.rearrange("(o f) -> o f", o=1).to_broadcast([P, F])).then_inc(loaded, 16)

                    @block.scalar
                    def _(act):
                        def standardise(t, a):
                            Yt = Hbuf[:, 1, bass.ds(t * P, P)]
                            act.activation(Yt, Yt, ACT.Identity, bias=ln[:, 3, bass.ds(t, 1)],
                                           scale=ln[:, 2, bass.ds(t, 1)]).then_inc(z, 1)
                        pipelined(act, NI, U, standardise)

                    @block.vector
                    def _(dve):
                        link = Steps(dve, steps)
                        dve.wait_ge(loaded, 32)
                        for i in iterations(dve, NI):
                            link.at(i * 3)
                            Y = Hbuf[:, 1, bass.ds(i * (U * P), U * P)].rearrange("p (a f) -> p a f", a=U)
                            Xi = X[:, bass.ds(i * U, U), :]
                            dve.wait_ge(z, i * U + U)
                            link(dve.tensor_tensor(Y, Y, gamma.unsqueeze(1).to_broadcast([P, U, F]), ALU.mult))
                            link(dve.tensor_tensor(Y, Y, beta.unsqueeze(1).to_broadcast([P, U, F]), ALU.add))
                            link(dve.tensor_tensor(Xi, Xi, Y, ALU.add))
                            for a in range(U):
                                dve.bn_stats(tile_of(stats, i * U + a), tile_of(X, i * U + a))

        def write_out():
            s, sem = phase()
            with s:
                stored = sem("out_stored")
                with nc.Block() as block:
                    @block.sync
                    def _(sp):
                        sp.dma_start(out[0:NFULL * P, :].rearrange("(t p) f -> p t f", p=P), X[:, 0:NFULL, :]).then_inc(stored, 16)
                        if NTAIL:
                            sp.dma_start(out[NFULL * P:N, :], X[0:NTAIL, NFULL, :]).then_inc(stored, 16)
                        sp.wait_ge(stored, 16 * (1 + (NTAIL > 0)))

        prepare()
        normalise("plain", T_L0)
        reverse_edges()
        nodes("l0")
        normalise("plain", T_C1)
        edges("sum", T_C1)
        nodes("conv1")
        edges("wide", T_C2)
        nodes("conv2")
        edges("sum", T_C3)
        nodes("conv3")
        normalise("message", T_MSG)
        edges("message", T_MSG)
        nodes("update")
        add_update()
        normalise("attention", T_ATT)
        edges("attention", T_ATT)
        nodes("final")
        write_out()


_INS = ['x', 'src', 'dst', 'edge_attr_64', 'L0_gnn_W', 'L0_gnn_b', 'L1_gnn_W1l', 'L1_gnn_b1', 'L1_gnn_W1r', 'L1_gnn_W2l',
        'L1_gnn_b2', 'L1_gnn_W2r', 'L1_gnn_W3l', 'L1_gnn_b3', 'L1_gnn_W3r', 'L2_gnn_global_state', 'L2_gnn_msg_w1',
        'L2_gnn_msg_b1', 'L2_gnn_msg_w2', 'L2_gnn_msg_b2', 'L2_gnn_upd_w1', 'L2_gnn_upd_b1', 'L2_gnn_upd_w2',
        'L2_gnn_upd_b2', 'L2_gnn_ln_gamma', 'L2_gnn_ln_beta', 'L3_gnn_W', 'L3_gnn_a']


def kernel(**inputs):
    import numpy as _np
    import concourse.bacc as _bacc
    from concourse import mybir as _mybir
    from concourse.bass_utils import run_bass_kernel_spmd as _run

    nc = _bacc.Bacc("TRN2", target_bir_lowering=False, num_devices=1)
    arrays, args = {}, []
    for name in _INS:
        a = _np.ascontiguousarray(inputs[name])
        arrays[f"in_{name}_dram"] = a
        args.append(nc.dram_tensor(f"in_{name}_dram", a.shape, _mybir.dt.from_np(a.dtype), kind="ExternalInput").ap())
    shape = tuple(inputs["x"].shape)
    args.append(nc.dram_tensor("out_dram", shape, _mybir.dt.float32, kind="ExternalOutput").ap())
    bass_gnn_preln_d4(nc, *args)
    r = _run(nc, [arrays], core_ids=[0])
    return r.results[0]["out_dram"]
```
